# Optimizing a Trainium2 kernel written in Bass

```python
import numpy as np
import jax
import jax.numpy as jnp

def _softmax(x, axis=-1):
    return jax.nn.softmax(x, axis=axis)

def _gelu(x):
    return jax.nn.gelu(x, approximate=True)

def _silu(x):
    return jax.nn.silu(x)

def _sigmoid(x):
    return jax.nn.sigmoid(x)

def _layernorm(x, axis=-1, eps=1e-05):
    m = jnp.mean(x, axis=axis, keepdims=True)
    v = jnp.var(x, axis=axis, keepdims=True)
    return (x - m) / jnp.sqrt(v + eps)

def _scatter_add(tgt, idx, src, axis=0):
    return tgt.at[idx].add(src)

def _segment_sum(src, seg, n):
    return jax.ops.segment_sum(src, seg, n)
kernel_name = 'mk_seq_postln_d2_jaxref_r8_20cb5b'

def setup_inputs(seed: int=0):
    np.random.seed(seed)
    _w = jnp.asarray

    def _L0_attn_setup():
        import jax, jax.numpy as jnp
        import numpy as np
        B, L, DIM, HID, DSSH, DSSN = (2, 512, 128, 512, 64, 64)

        def _ln(x, w, b):
            m = x.mean(-1, keepdims=True)
            v = ((x - m) ** 2).mean(-1, keepdims=True)
            return (x - m) * jax.lax.rsqrt(v + 1e-05) * w + b

        def _dss(x, n2_w, n2_b, LR, LI, CR, CI, D):
            Lseq = x.shape[-2]
            xn = _ln(x, n2_w, n2_b)
            Lam = (-jnp.exp(LR) + 1j * jnp.exp(LI)).astype(jnp.complex64)
            t = jnp.arange(Lseq, dtype=jnp.float32)
            S = jnp.exp(Lam[:, None] * t[None, :])
            Cc = (CR + 1j * CI) * ((jnp.exp(Lam) - 1.0) / Lam)
            K = jnp.einsum('hn,nl->lh', Cc, S).real
            n2 = 2 * Lseq
            Kf = jnp.fft.rfft(K, n=n2, axis=-2)
            uf = jnp.fft.rfft(xn, n=n2, axis=-2)
            y = jnp.fft.irfft(uf * Kf, n=n2, axis=-2)[..., :Lseq, :]
            return y + D * xn
        key = jax.random.key(seed)
        ks = jax.random.split(key, 12)
        s = lambda k, sh, sc=1.0: jax.random.normal(k, sh, jnp.float32) * sc
        return dict(idx=s(ks[0], (B, L, DIM)), n1_w=jnp.ones((DIM,), jnp.float32), n1_b=jnp.zeros((DIM,), jnp.float32), Wxg=s(ks[1], (DIM, HID), 0.02), Wdin=s(ks[2], (DIM, DSSH), 0.02), n2_w=jnp.ones((DSSH,), jnp.float32), n2_b=jnp.zeros((DSSH,), jnp.float32), LR=s(ks[3], (DSSN,)), LI=s(ks[4], (DSSN,)), CR=s(ks[5], (DSSH, DSSN), 0.1), CI=s(ks[6], (DSSH, DSSN), 0.1), D=s(ks[7], (DSSH,)), Wgate=s(ks[8], (DSSH, HID), 0.02), Wout=s(ks[9], (HID, DIM), 0.02), bout=jnp.zeros((DIM,), jnp.float32))
    _L0_attn_in = _L0_attn_setup()

    def _L0_ffn_setup():
        import jax, jax.numpy as jnp
        import numpy as np
        H = 128
        NH = 16
        HD = H // NH
        HH = HD // 2
        L = H // 4
        I = int(H * 1.0)
        ER = 7
        TOPK = 2
        BASE = 10000.0
        EPS = 1e-05

        def rmsnorm(x, w):
            norm = jnp.sqrt(jnp.mean(x * x, axis=-1, keepdims=True)) + EPS
            return x / norm * w

        def rope_tables(seq_len):
            inv_freq = 1.0 / BASE ** (jnp.arange(0, HH, 2, dtype=jnp.float32) / HH)
            t = jnp.arange(seq_len, dtype=jnp.float32)
            freqs = jnp.einsum('i,j->ij', t, inv_freq)
            emb = jnp.concatenate([freqs, freqs], axis=-1)
            cos = jnp.cos(emb)[None, :, None, :]
            sin = jnp.sin(emb)[None, :, None, :]
            return (cos, sin)

        def rotate_half(x):
            x1, x2 = jnp.split(x, 2, axis=-1)
            return jnp.concatenate([-x2, x1], axis=-1)

        def silu(x):
            return x * jax.nn.sigmoid(x)

        def mla(xn, W_kvd, W_qd, W_ku, W_qu, W_vu, W_ropeq, W_ropek, W_o):
            B, S, _ = xn.shape
            kv_lat = xn @ W_kvd
            q_lat = xn @ W_qd
            k = (kv_lat @ W_ku).reshape(B, S, NH, HH)
            q = (q_lat @ W_qu).reshape(B, S, NH, HH)
            v = (kv_lat @ W_vu).reshape(B, S, NH, HD)
            q_rope = (q_lat @ W_ropeq).reshape(B, S, NH, HH)
            k_rope = (xn @ W_ropek).reshape(B, S, NH, HH)
            cos, sin = rope_tables(S)
            k_rope = k_rope * cos + rotate_half(k_rope) * sin
            q_rope = q_rope * cos + rotate_half(q_rope) * sin
            kk = jnp.concatenate([k, k_rope], axis=-1)
            qq = jnp.concatenate([q, q_rope], axis=-1)
            scale = 1.0 / jnp.sqrt(jnp.float32(HD))
            scores = jnp.einsum('bqhd,bkhd->bhqk', qq, kk) * scale
            causal = jnp.tril(jnp.ones((S, S), dtype=bool))
            scores = jnp.where(causal[None, None], scores, jnp.finfo(scores.dtype).min)
            probs = jax.nn.softmax(scores, axis=-1)
            y = jnp.einsum('bhqk,bkhd->bqhd', probs, v).reshape(B, S, H)
            return y @ W_o

        def moe(xn, Wg_s, Wu_s, Wd_s, Wg_r, Wu_r, Wd_r, W_router, routing_bias):
            B, S, _ = xn.shape
            xt = xn.reshape(B * S, H)
            shared = silu(xt @ Wg_s) * (xt @ Wu_s) @ Wd_s
            logits = xt @ W_router + routing_bias
            probs = jax.nn.sigmoid(logits)
            scores, idx = jax.lax.top_k(probs, TOPK)
            scores = scores / jnp.sum(scores, axis=-1, keepdims=True)
            wts = jnp.sum(jax.nn.one_hot(idx, ER, dtype=xt.dtype) * scores[..., None], axis=1)
            g = jnp.einsum('th,ehi->tei', xt, Wg_r)
            u = jnp.einsum('th,ehi->tei', xt, Wu_r)
            hmid = silu(g) * u
            combined = jnp.einsum('tei,eih,te->th', hmid, Wd_r, wts)
            return (shared + combined).reshape(B, S, H)
        key = jax.random.key(seed)
        ks = jax.random.split(key, 20)
        s = 0.02
        r = lambda k, shp: jax.random.normal(k, shp, dtype=jnp.float32) * s
        return {'x': jax.random.normal(ks[0], (4, 128, H), dtype=jnp.float32), 'w_ln1': jnp.ones((H,), jnp.float32), 'w_ln2': jnp.ones((H,), jnp.float32), 'W_kvd': r(ks[1], (H, L)), 'W_qd': r(ks[2], (H, L)), 'W_ku': r(ks[3], (L, NH * HH)), 'W_qu': r(ks[4], (L, NH * HH)), 'W_vu': r(ks[5], (L, H)), 'W_ropeq': r(ks[6], (L, H // 2)), 'W_ropek': r(ks[7], (H, H // 2)), 'W_o': r(ks[8], (H, H)), 'Wg_s': r(ks[9], (H, I)), 'Wu_s': r(ks[10], (H, I)), 'Wd_s': r(ks[11], (I, H)), 'Wg_r': r(ks[12], (ER, H, I)), 'Wu_r': r(ks[13], (ER, H, I)), 'Wd_r': r(ks[14], (ER, I, H)), 'W_router': r(ks[15], (H, ER)), 'routing_bias': jnp.zeros((ER,), jnp.float32)}
    _L0_ffn_in = _L0_ffn_setup()

    def _L1_attn_setup():
        import jax, jax.numpy as jnp
        import numpy as np
        HIDDEN = 128
        NUM_HEADS = 16
        HEAD_DIM = HIDDEN // NUM_HEADS
        MASK_BIAS = -10000.0

        def _split_heads(t):
            B, S, _ = t.shape
            return t.reshape(B, S, NUM_HEADS, HEAD_DIM).transpose(0, 2, 1, 3)
        key = jax.random.key(seed)
        ks = jax.random.split(key, 5)
        B, S = (4, 256)
        hidden_states = jax.random.normal(ks[0], (B, S, HIDDEN), dtype=jnp.float32)
        w_qkv = jax.random.normal(ks[1], (HIDDEN, 3 * HIDDEN), dtype=jnp.float32) * HIDDEN ** (-0.5)
        b_qkv = jax.random.normal(ks[2], (3 * HIDDEN,), dtype=jnp.float32) * 0.02
        w_dense = jax.random.normal(ks[3], (HIDDEN, HIDDEN), dtype=jnp.float32) * HIDDEN ** (-0.5)
        b_dense = jax.random.normal(ks[4], (HIDDEN,), dtype=jnp.float32) * 0.02
        return {'hidden_states': hidden_states, 'w_qkv': w_qkv, 'b_qkv': b_qkv, 'w_dense': w_dense, 'b_dense': b_dense}
    _L1_attn_in = _L1_attn_setup()

    def _L1_ffn_setup():
        import jax, jax.numpy as jnp
        import numpy as np
        B, S, F, E, K = (4, 128, 128, 8, 2)
        H = 4 * F
        key = jax.random.key(seed)
        ks = jax.random.split(key, 7)

        def xavier(k, shape):
            fan_in, fan_out = (shape[-2], shape[-1])
            scale = jnp.sqrt(6.0 / (fan_in + fan_out))
            return jax.random.uniform(k, shape, jnp.float32, -scale, scale)
        return {'x': jax.random.normal(ks[0], (B, S, F), jnp.float32), 'Wg': xavier(ks[1], (F, E)), 'bg': jnp.zeros((E,), jnp.float32), 'W1': xavier(ks[2], (E, F, H)), 'b1': jnp.zeros((E, H), jnp.float32), 'W2': xavier(ks[3], (E, H, F)), 'b2': jnp.zeros((E, F), jnp.float32)}
    _L1_ffn_in = _L1_ffn_setup()
    _d = {'L0_attn_idx': _L0_attn_in['idx'], 'L0_attn_n1_w': _L0_attn_in['n1_w'], 'L0_attn_n1_b': _L0_attn_in['n1_b'], 'L0_attn_Wxg': _L0_attn_in['Wxg'], 'L0_attn_Wdin': _L0_attn_in['Wdin'], 'L0_attn_n2_w': _L0_attn_in['n2_w'], 'L0_attn_n2_b': _L0_attn_in['n2_b'], 'L0_attn_LR': _L0_attn_in['LR'], 'L0_attn_LI': _L0_attn_in['LI'], 'L0_attn_CR': _L0_attn_in['CR'], 'L0_attn_CI': _L0_attn_in['CI'], 'L0_attn_D': _L0_attn_in['D'], 'L0_attn_Wgate': _L0_attn_in['Wgate'], 'L0_attn_Wout': _L0_attn_in['Wout'], 'L0_attn_bout': _L0_attn_in['bout'], 'L0_ffn_w_ln1': _L0_ffn_in['w_ln1'], 'L0_ffn_w_ln2': _L0_ffn_in['w_ln2'], 'L0_ffn_W_kvd': _L0_ffn_in['W_kvd'], 'L0_ffn_W_qd': _L0_ffn_in['W_qd'], 'L0_ffn_W_ku': _L0_ffn_in['W_ku'], 'L0_ffn_W_qu': _L0_ffn_in['W_qu'], 'L0_ffn_W_vu': _L0_ffn_in['W_vu'], 'L0_ffn_W_ropeq': _L0_ffn_in['W_ropeq'], 'L0_ffn_W_ropek': _L0_ffn_in['W_ropek'], 'L0_ffn_W_o': _L0_ffn_in['W_o'], 'L0_ffn_Wg_s': _L0_ffn_in['Wg_s'], 'L0_ffn_Wu_s': _L0_ffn_in['Wu_s'], 'L0_ffn_Wd_s': _L0_ffn_in['Wd_s'], 'L0_ffn_Wg_r': _L0_ffn_in['Wg_r'], 'L0_ffn_Wu_r': _L0_ffn_in['Wu_r'], 'L0_ffn_Wd_r': _L0_ffn_in['Wd_r'], 'L0_ffn_W_router': _L0_ffn_in['W_router'], 'L0_ffn_routing_bias': _L0_ffn_in['routing_bias'], 'L1_attn_w_qkv': _L1_attn_in['w_qkv'], 'L1_attn_b_qkv': _L1_attn_in['b_qkv'], 'L1_attn_w_dense': _L1_attn_in['w_dense'], 'L1_attn_b_dense': _L1_attn_in['b_dense'], 'L1_ffn_Wg': _L1_ffn_in['Wg'], 'L1_ffn_bg': _L1_ffn_in['bg'], 'L1_ffn_W1': _L1_ffn_in['W1'], 'L1_ffn_b1': _L1_ffn_in['b1'], 'L1_ffn_W2': _L1_ffn_in['W2'], 'L1_ffn_b2': _L1_ffn_in['b2']}
    _x0 = _d['L0_attn_idx']
    _d['L0_attn_idx'] = jax.random.normal(jax.random.fold_in(jax.random.key(seed), 1), (16, 512, 128), dtype=_x0.dtype)
    del _x0
    return _d

def reference(L0_attn_idx, L0_attn_n1_w, L0_attn_n1_b, L0_attn_Wxg, L0_attn_Wdin, L0_attn_n2_w, L0_attn_n2_b, L0_attn_LR, L0_attn_LI, L0_attn_CR, L0_attn_CI, L0_attn_D, L0_attn_Wgate, L0_attn_Wout, L0_attn_bout, L0_ffn_w_ln1, L0_ffn_w_ln2, L0_ffn_W_kvd, L0_ffn_W_qd, L0_ffn_W_ku, L0_ffn_W_qu, L0_ffn_W_vu, L0_ffn_W_ropeq, L0_ffn_W_ropek, L0_ffn_W_o, L0_ffn_Wg_s, L0_ffn_Wu_s, L0_ffn_Wd_s, L0_ffn_Wg_r, L0_ffn_Wu_r, L0_ffn_Wd_r, L0_ffn_W_router, L0_ffn_routing_bias, L1_attn_w_qkv, L1_attn_b_qkv, L1_attn_w_dense, L1_attn_b_dense, L1_ffn_Wg, L1_ffn_bg, L1_ffn_W1, L1_ffn_b1, L1_ffn_W2, L1_ffn_b2):

    def _L0_attn_ref(idx, n1_w, n1_b, Wxg, Wdin, n2_w, n2_b, LR, LI, CR, CI, D, Wgate, Wout, bout):
        import jax, jax.numpy as jnp
        import numpy as np
        B, L, DIM, HID, DSSH, DSSN = (2, 512, 128, 512, 64, 64)

        def _ln(x, w, b):
            m = x.mean(-1, keepdims=True)
            v = ((x - m) ** 2).mean(-1, keepdims=True)
            return (x - m) * jax.lax.rsqrt(v + 1e-05) * w + b

        def _dss(x, n2_w, n2_b, LR, LI, CR, CI, D):
            Lseq = x.shape[-2]
            xn = _ln(x, n2_w, n2_b)
            Lam = (-jnp.exp(LR) + 1j * jnp.exp(LI)).astype(jnp.complex64)
            t = jnp.arange(Lseq, dtype=jnp.float32)
            S = jnp.exp(Lam[:, None] * t[None, :])
            Cc = (CR + 1j * CI) * ((jnp.exp(Lam) - 1.0) / Lam)
            K = jnp.einsum('hn,nl->lh', Cc, S).real
            n2 = 2 * Lseq
            Kf = jnp.fft.rfft(K, n=n2, axis=-2)
            uf = jnp.fft.rfft(xn, n=n2, axis=-2)
            y = jnp.fft.irfft(uf * Kf, n=n2, axis=-2)[..., :Lseq, :]
            return y + D * xn
        x = _ln(idx, n1_w, n1_b)
        xg = x @ Wxg
        d = _dss(x @ Wdin, n2_w, n2_b, LR, LI, CR, CI, D)
        g = d @ Wgate
        out = g * xg @ Wout + bout
        return out + idx

    def _L0_ffn_ref(x, w_ln1, w_ln2, W_kvd, W_qd, W_ku, W_qu, W_vu, W_ropeq, W_ropek, W_o, Wg_s, Wu_s, Wd_s, Wg_r, Wu_r, Wd_r, W_router, routing_bias):
        import jax, jax.numpy as jnp
        import numpy as np
        H = 128
        NH = 16
        HD = H // NH
        HH = HD // 2
        L = H // 4
        I = int(H * 1.0)
        ER = 7
        TOPK = 2
        BASE = 10000.0
        EPS = 1e-05

        def rmsnorm(x, w):
            norm = jnp.sqrt(jnp.mean(x * x, axis=-1, keepdims=True)) + EPS
            return x / norm * w

        def rope_tables(seq_len):
            inv_freq = 1.0 / BASE ** (jnp.arange(0, HH, 2, dtype=jnp.float32) / HH)
            t = jnp.arange(seq_len, dtype=jnp.float32)
            freqs = jnp.einsum('i,j->ij', t, inv_freq)
            emb = jnp.concatenate([freqs, freqs], axis=-1)
            cos = jnp.cos(emb)[None, :, None, :]
            sin = jnp.sin(emb)[None, :, None, :]
            return (cos, sin)

        def rotate_half(x):
            x1, x2 = jnp.split(x, 2, axis=-1)
            return jnp.concatenate([-x2, x1], axis=-1)

        def silu(x):
            return x * jax.nn.sigmoid(x)

        def mla(xn, W_kvd, W_qd, W_ku, W_qu, W_vu, W_ropeq, W_ropek, W_o):
            B, S, _ = xn.shape
            kv_lat = xn @ W_kvd
            q_lat = xn @ W_qd
            k = (kv_lat @ W_ku).reshape(B, S, NH, HH)
            q = (q_lat @ W_qu).reshape(B, S, NH, HH)
            v = (kv_lat @ W_vu).reshape(B, S, NH, HD)
            q_rope = (q_lat @ W_ropeq).reshape(B, S, NH, HH)
            k_rope = (xn @ W_ropek).reshape(B, S, NH, HH)
            cos, sin = rope_tables(S)
            k_rope = k_rope * cos + rotate_half(k_rope) * sin
            q_rope = q_rope * cos + rotate_half(q_rope) * sin
            kk = jnp.concatenate([k, k_rope], axis=-1)
            qq = jnp.concatenate([q, q_rope], axis=-1)
            scale = 1.0 / jnp.sqrt(jnp.float32(HD))
            scores = jnp.einsum('bqhd,bkhd->bhqk', qq, kk) * scale
            causal = jnp.tril(jnp.ones((S, S), dtype=bool))
            scores = jnp.where(causal[None, None], scores, jnp.finfo(scores.dtype).min)
            probs = jax.nn.softmax(scores, axis=-1)
            y = jnp.einsum('bhqk,bkhd->bqhd', probs, v).reshape(B, S, H)
            return y @ W_o

        def moe(xn, Wg_s, Wu_s, Wd_s, Wg_r, Wu_r, Wd_r, W_router, routing_bias):
            B, S, _ = xn.shape
            xt = xn.reshape(B * S, H)
            shared = silu(xt @ Wg_s) * (xt @ Wu_s) @ Wd_s
            logits = xt @ W_router + routing_bias
            probs = jax.nn.sigmoid(logits)
            scores, idx = jax.lax.top_k(probs, TOPK)
            scores = scores / jnp.sum(scores, axis=-1, keepdims=True)
            wts = jnp.sum(jax.nn.one_hot(idx, ER, dtype=xt.dtype) * scores[..., None], axis=1)
            g = jnp.einsum('th,ehi->tei', xt, Wg_r)
            u = jnp.einsum('th,ehi->tei', xt, Wu_r)
            hmid = silu(g) * u
            combined = jnp.einsum('tei,eih,te->th', hmid, Wd_r, wts)
            return (shared + combined).reshape(B, S, H)
        x = x + mla(rmsnorm(x, w_ln1), W_kvd, W_qd, W_ku, W_qu, W_vu, W_ropeq, W_ropek, W_o)
        x = x + moe(rmsnorm(x, w_ln2), Wg_s, Wu_s, Wd_s, Wg_r, Wu_r, Wd_r, W_router, routing_bias)
        return x

    def _L1_attn_ref(hidden_states, w_qkv, b_qkv, w_dense, b_dense):
        import jax, jax.numpy as jnp
        import numpy as np
        HIDDEN = 128
        NUM_HEADS = 16
        HEAD_DIM = HIDDEN // NUM_HEADS
        MASK_BIAS = -10000.0

        def _split_heads(t):
            B, S, _ = t.shape
            return t.reshape(B, S, NUM_HEADS, HEAD_DIM).transpose(0, 2, 1, 3)
        B, S, _ = hidden_states.shape
        kvq = hidden_states @ w_qkv + b_qkv
        k, v, q = jnp.split(kvq, 3, axis=-1)
        q = _split_heads(q) * HEAD_DIM ** (-0.5)
        k = _split_heads(k)
        v = _split_heads(v)
        scores = jnp.einsum('bhqd,bhkd->bhqk', q, k)
        causal = jnp.tril(jnp.ones((S, S), dtype=bool))
        scores = jnp.where(causal[None, None], scores, jnp.asarray(MASK_BIAS, scores.dtype))
        dt = scores.dtype
        attn = jax.nn.softmax(scores.astype(jnp.float32), axis=-1).astype(dt)
        ctx = jnp.einsum('bhqk,bhkd->bhqd', attn, v)
        ctx = ctx.transpose(0, 2, 1, 3).reshape(B, S, HIDDEN)
        return ctx @ w_dense + b_dense

    def _L1_ffn_ref(x, Wg, bg, W1, b1, W2, b2):
        import jax, jax.numpy as jnp
        import numpy as np
        B, S, F, E, K = (4, 128, 128, 8, 2)
        H = 4 * F
        gate_probs = jax.nn.softmax(x @ Wg + bg, axis=-1)
        k = K
        _, top_idx = jax.lax.top_k(gate_probs, k)
        expert_mask = jax.nn.one_hot(top_idx, gate_probs.shape[-1], dtype=gate_probs.dtype).sum(-2)
        selected = gate_probs * expert_mask
        selected = selected / (selected.sum(-1, keepdims=True) + 1e-08)
        h = jax.nn.gelu(jnp.einsum('bsf,efh->bseh', x, W1) + b1)
        expert_out = jnp.einsum('bseh,ehf->bsef', h, W2) + b2[None, None]
        return jnp.einsum('bsef,bse->bsf', expert_out, selected)
    x = L0_attn_idx
    x = _layernorm(x + _L0_attn_ref(x, L0_attn_n1_w, L0_attn_n1_b, L0_attn_Wxg, L0_attn_Wdin, L0_attn_n2_w, L0_attn_n2_b, L0_attn_LR, L0_attn_LI, L0_attn_CR, L0_attn_CI, L0_attn_D, L0_attn_Wgate, L0_attn_Wout, L0_attn_bout), axis=-1)
    x = _layernorm(x + _L0_ffn_ref(x, L0_ffn_w_ln1, L0_ffn_w_ln2, L0_ffn_W_kvd, L0_ffn_W_qd, L0_ffn_W_ku, L0_ffn_W_qu, L0_ffn_W_vu, L0_ffn_W_ropeq, L0_ffn_W_ropek, L0_ffn_W_o, L0_ffn_Wg_s, L0_ffn_Wu_s, L0_ffn_Wd_s, L0_ffn_Wg_r, L0_ffn_Wu_r, L0_ffn_Wd_r, L0_ffn_W_router, L0_ffn_routing_bias), axis=-1)
    x = _layernorm(x + _L1_attn_ref(x, L1_attn_w_qkv, L1_attn_b_qkv, L1_attn_w_dense, L1_attn_b_dense), axis=-1)
    x = _layernorm(x + _L1_ffn_ref(x, L1_ffn_Wg, L1_ffn_bg, L1_ffn_W1, L1_ffn_b1, L1_ffn_W2, L1_ffn_b2), axis=-1)
    return x

_drawn_inputs = setup_inputs


def setup_inputs(seed=0):
    import zlib

    import numpy as np

    out = dict(_drawn_inputs(seed))
    spreads = {'L0_attn_n1_w': (1.0, 0.6),
     'L0_attn_n1_b': (0.0, 0.685),
     'L0_attn_n2_w': (1.0, 0.6),
     'L0_attn_n2_b': (0.0, 0.8),
     'L0_attn_bout': (0.0, 0.1),
     'L0_ffn_w_ln1': (1.0, 0.6),
     'L0_ffn_w_ln2': (1.0, 0.6),
     'L0_ffn_routing_bias': (0.0, 0.8),
     'L1_ffn_bg': (0.0, 0.1),
     'L1_ffn_b1': (0.0, 0.1),
     'L1_ffn_b2': (0.0, 0.1)}
    factors = {'L0_attn_LR': 3.766,
     'L0_attn_LI': 3.129,
     'L0_attn_CR': 3.341,
     'L0_attn_CI': 4.194,
     'L0_ffn_W_kvd': 8.0,
     'L0_ffn_W_qd': 8.0,
     'L0_ffn_W_ku': 8.0,
     'L0_ffn_W_qu': 8.0,
     'L0_ffn_W_vu': 8.0,
     'L0_ffn_W_ropeq': 8.0,
     'L0_ffn_W_ropek': 8.0,
     'L0_ffn_W_o': 8.0,
     'L0_ffn_Wg_s': 4.525,
     'L0_ffn_Wu_s': 4.506,
     'L0_ffn_Wd_s': 4.093,
     'L0_ffn_Wg_r': 5.344,
     'L0_ffn_Wu_r': 5.008,
     'L0_ffn_Wd_r': 5.601,
     'L0_ffn_W_router': 5.769}
    for name, (base, spread) in spreads.items():
        noise = np.random.default_rng([zlib.crc32(name.encode()), seed]).standard_normal(out[name].shape)
        drawn = base * np.exp(spread * noise) if base else spread * noise
        out[name] = jnp.asarray(drawn.astype(out[name].dtype))
    for name, factor in factors.items():
        out[name] = (out[name] * factor).astype(out[name].dtype)
    return out
```

```python
from contextlib import ExitStack
import math

import numpy as np
import concourse.bass as bass
from concourse import mybir
from concourse.alu_op_type import AluOpType as ALU

F32 = mybir.dt.float32
F32R = mybir.dt.float32r
BF16 = mybir.dt.bfloat16
I32 = mybir.dt.int32
ACT = mybir.ActivationFunctionType
AX = mybir.AxisListType

P = 128
NB, L, C = 16, 512, 128
BLK = L // P
HID = 512
NS, NC = 64, 64
NH, HD = 16, 8
NG, HG = 4, 4
LAT = 32
E0, E1, H1 = 8, 8, 512
H1B = H1 // P
EPS = 1e-5
NEG = -1e30
KPAD = P - 1
KROW = KPAD + L + 1
MROW = 3 * 8 * HG


class Counts:

    def __init__(self, eng):
        self.eng, self.taken = eng, {}

    def next(self, sem, n=1):
        self.taken[sem] = self.taken.get(sem, 0) + n
        return self.taken[sem]

    def settle(self):
        for sem, n in self.taken.items():
            self.eng.sem_inc(sem, -n)
        self.taken = {}


class Names:

    used = set()

    def __init__(self, nc, ctx, stage):
        self.nc, self.ctx, self.stage = nc, ctx, stage

    def sems(self, text):
        made = [self.ctx.enter_context(self.nc.semaphore(f"{self.stage}_{n}")) for n in text.split()]
        Names.used.update(s.num for s in made)
        return made

    def sb(self, name, shape, dt=F32):
        return self.ctx.enter_context(self.nc.sbuf_tensor(f"{self.stage}_{name}", shape, dt))


def clear(nc):
    with nc.Block() as block:

        @block.sync
        def _(sp):
            while Names.used:
                lo = hi = min(Names.used)
                while hi in Names.used:
                    Names.used.discard(hi)
                    hi += 1
                sp.sem_clear(range(lo, hi))


def f32(ap):
    return ap.bitcast(F32)


def chain(eng, c, done, ins):
    ins.then_inc(done, 1)
    eng.wait_ge(done, c.next(done))


def rows(ap, n=P):
    return bass.AP(tensor=ap.tensor, offset=ap.offset, ap=[[0, n]] + [list(x) for x in ap.ap])


def column(ap):
    return ap.rearrange("(p a) -> p a", a=1)


def block_stats(dve, c, done, src, st, mv):
    for b in range(BLK):
        last = dve.bn_stats(st[:, b, :], src[:, b, :])
    chain(dve, c, done, last)
    for b in range(BLK):
        last = dve.bn_aggr(mv[:, b, :], st[:, b, :])
    return last


def pool_rstd(pool, c, done, mv, var, mhalf, out):
    chain(pool, c, done, pool.tensor_scalar(var[:, :], mv[:, :, 1], EPS, 1.0, ALU.add, ALU.mult))
    return pool.tensor_tensor(out[:, :], var[:, :], mhalf[:, :], ALU.pow)


def split(dve, c, done, x, hi, lo):
    chain(dve, c, done, dve.tensor_copy(hi, x))
    return dve.tensor_tensor(lo, x, f32(hi), ALU.subtract)



LOG2E = math.log2(math.e)
LN2_HI, LN2_LO = 0.693145751953125, math.log(2) - 0.693145751953125
MAGIC = 1.5 * 2.0 ** 23


def parts(x, bits, n):
    out = []
    for _ in range(n - 1):
        e = math.floor(math.log2(abs(x))) + 1 - bits
        p = math.trunc(x / 2.0 ** e) * 2.0 ** e
        out.append(p)
        x -= p
    return out + [x]


def exact_exp(dve, link, z, k, r, q, ki, out):
    link(dve.tensor_scalar(z, z, -87.0, 87.0, ALU.max, ALU.min))
    link(dve.tensor_scalar(k, z, LOG2E, MAGIC, ALU.mult, ALU.add))
    link(dve.tensor_scalar(k, k, -MAGIC, None, ALU.add))
    link(dve.scalar_tensor_tensor(r, k, -LN2_HI, z, ALU.mult, ALU.add))
    link(dve.scalar_tensor_tensor(r, k, -LN2_LO, r, ALU.mult, ALU.add))
    link(dve.tensor_scalar(q, r, 1.0 / math.factorial(8), None, ALU.mult))
    for d in range(7, 0, -1):
        link(dve.scalar_tensor_tensor(q, q, 1.0 / math.factorial(d), r, ALU.add, ALU.mult))
    link(dve.tensor_scalar(q, q, 1.0, None, ALU.add))
    link(dve.tensor_scalar(ki, k, 127.0, None, ALU.add))
    link(dve.tensor_scalar(ki, ki, 23, None, ALU.logical_shift_left))
    link(dve.tensor_tensor(out, q, ki.bitcast(F32), ALU.mult))


def kernel_stage(nc, io, ps, kd):
    with ExitStack() as ctx:
        N = Names(nc, ctx, "kern")
        z, k, r, q, ex = (N.sb(n, [P, 2]) for n in ("z", "k", "r", "q", "ex"))
        ki = N.sb("ki", [P, 2], I32)
        crt, cit, coef = (N.sb(n, [P, NC]) for n in ("crt", "cit", "coef"))
        t = N.sb("t", [P, L])
        half = N.sb("half", [P, 5])
        turn, ph, ph2, arg, decay = (N.sb(n, [P, L]) for n in ("turn", "ph", "ph2", "arg", "decay"))
        arg1, cs, w = N.sb("arg1", [P, 2]), N.sb("cs", [P, 2]), N.sb("w", [P, 16])
        kpad, dcol = N.sb("kpad", [NC, KROW]), N.sb("dcol", [NC, 1])
        loaded, done, args_ready, waves_ready, table_ready, k_ready, kpad_ready, stored = N.sems(
            "loaded done args_ready waves_ready table_ready k_ready kpad_ready stored")
        a_ready, decay_ready = N.sems("a_ready decay_ready")
        with nc.Block() as block:

            @block.sync
            def _(sp):
                for lo in (0, NS):
                    sp.dma_start(z[lo:lo + NS, 0:1], column(io["LR"])).then_inc(loaded, 16)
                    sp.dma_start(z[lo:lo + NS, 1:2], column(io["LI"])).then_inc(loaded, 16)
                    sp.dma_start(crt[lo:lo + NS, :], io["CR"].rearrange("h n -> n h"),
                                 allow_slow_non_contiguous=True).then_inc(loaded, 16)
                    sp.dma_start(cit[lo:lo + NS, :], io["CI"].rearrange("h n -> n h"),
                                 allow_slow_non_contiguous=True).then_inc(loaded, 16)
                sp.dma_start(t[:, :], io["c_t"]).then_inc(loaded, 16)
                sp.dma_start(half[:, :], io["c_half"]).then_inc(loaded, 16)
                sp.dma_start(dcol[:, :], column(io["D"])).then_inc(loaded, 16)
                sp.wait_ge(kpad_ready, 1)
                sp.dma_start(kd, kpad[:, :]).then_inc(stored, 16)
                sp.wait_ge(stored, 16)

            @block.vector
            def _(dve):
                c = Counts(dve)
                link = lambda ins: chain(dve, c, done, ins)
                link(dve.memset(kpad[:, :], 0.0))
                dve.wait_ge(loaded, 11 * 16)
                exact_exp(dve, link, z[:, :], k[:, :], r[:, :], q[:, :], ki[:, :], ex[:, :])
                a, b = w[:, 0:1], ex[:, 1:2]
                dve.tensor_scalar(a, ex[:, 0:1], -1.0, None, ALU.mult).then_inc(a_ready, 1)
                link(dve.tensor_scalar(ph[:, :], t[:, :], b, None, ALU.mult))
                for unit, bits, n in ((2048 * 2 * math.pi, 8, 5), (2 * math.pi, 12, 3)):
                    link(dve.tensor_scalar(turn[:, :], ph[:, :], 1.0 / unit, MAGIC, ALU.mult, ALU.add))
                    link(dve.tensor_scalar(turn[:, :], turn[:, :], -MAGIC, None, ALU.add))
                    for p in parts(unit, bits, n):
                        link(dve.scalar_tensor_tensor(ph[:, :], turn[:, :], -p, ph[:, :], ALU.mult, ALU.add))
                link(dve.tensor_scalar(ph[:, :], ph[:, :], 3.1415925, -3.1415925, ALU.min, ALU.max))
                link(dve.tensor_scalar(ph2[:, :], ph[:, :], -1.0, None, ALU.mult))
                link(dve.tensor_tensor(ph2[:, :], ph2[:, :], ph[:, :], ALU.max))
                link(dve.tensor_scalar(arg1[:, 0:1], ph2[:, 1:2], -1.0, math.pi / 2, ALU.mult, ALU.add))
                link(dve.tensor_copy(arg1[:, 1:2], ph[:, 1:2]))
                link(dve.tensor_scalar(ph2[:, :], ph2[:, :], half[:, 1:2], half[:, 3:4], ALU.mult, ALU.add))
                dve.scalar_tensor_tensor(arg[:, :], ph[:, :], half[:, 2:3], ph2[:, :], ALU.mult,
                                         ALU.add).then_inc(args_ready, 1)
                dve.wait_ge(a_ready, 1)
                link(dve.tensor_copy(z[:, 0:1], a))
                exact_exp(dve, link, z[:, 0:1], k[:, 0:1], r[:, 0:1], q[:, 0:1], ki[:, 0:1], ex[:, 0:1])
                ea = ex[:, 0:1]
                er, ei, dd, u, wr, wi, p1, p2 = (w[:, n:n + 1] for n in range(1, 9))
                dve.wait_ge(waves_ready, 1)
                link(dve.tensor_tensor(er, ea, cs[:, 0:1], ALU.mult))
                link(dve.tensor_scalar(er, er, -1.0, None, ALU.add))
                link(dve.tensor_tensor(ei, ea, cs[:, 1:2], ALU.mult))
                link(dve.tensor_tensor(dd, a, a, ALU.mult))
                link(dve.scalar_tensor_tensor(dd, b, b, dd, ALU.mult, ALU.add))
                link(dve.reciprocal(dd, dd))
                link(dve.tensor_tensor(u, er, a, ALU.mult))
                link(dve.scalar_tensor_tensor(wr, ei, b, u, ALU.mult, ALU.add))
                link(dve.tensor_tensor(wr, wr, dd, ALU.mult))
                link(dve.tensor_tensor(u, er, b, ALU.mult))
                link(dve.scalar_tensor_tensor(wi, ei, a, u, ALU.mult, ALU.subtract))
                link(dve.tensor_tensor(wi, wi, dd, ALU.mult))
                link(dve.tensor_tensor(u, wi, half[:, 2:3], ALU.mult))
                link(dve.scalar_tensor_tensor(p1, wr, half[:, 0:1], u, ALU.mult, ALU.subtract))
                link(dve.tensor_tensor(u, wr, half[:, 2:3], ALU.mult))
                link(dve.scalar_tensor_tensor(p2, wi, half[:, 1:2], u, ALU.mult, ALU.subtract))
                link(dve.tensor_scalar(crt[:, :], crt[:, :], p1, None, ALU.mult))
                link(dve.scalar_tensor_tensor(coef[:, :], cit[:, :], p2, crt[:, :], ALU.mult, ALU.add))
                dve.wait_ge(decay_ready, 1)
                dve.tensor_tensor(arg[:, :], arg[:, :], decay[:, :], ALU.mult).then_inc(table_ready, 1)
                dve.wait_ge(k_ready, 1)
                link(dve.tensor_copy(kpad[:, KPAD:KPAD + L], ps[0:NC, 0, :]))
                dve.tensor_tensor(kpad[:, KPAD:KPAD + 1], kpad[:, KPAD:KPAD + 1], dcol[:, :],
                                  ALU.add).then_inc(kpad_ready, 1)

            @block.scalar
            def _(act):
                act.wait_ge(a_ready, 1)
                act.activation(decay[:, :], t[:, :], ACT.Exp, scale=w[:, 0:1]).then_inc(decay_ready, 1)
                act.wait_ge(args_ready, 1)
                act.activation(cs[:, :], arg1[:, :], ACT.Sin)
                act.activation(arg[:, :], arg[:, :], ACT.Sin).then_inc(waves_ready, 1)

            @block.tensor
            def _(pe):
                pe.wait_ge(table_ready, 1)
                pe.matmul(ps[0:NC, 0, :], coef[:, :], arg[:, :], start=True, stop=True).then_inc(k_ready, 1)



def input_stage(nc, io, ps, X, stats, ident, flip, mhalf, U):
    with ExitStack() as ctx:
        N = Names(nc, ctx, "inp")
        w1, b1, wd, bcast = N.sb("w1", [P, 1]), N.sb("b1", [P, 1]), N.sb("wd", [P, NC]), N.sb("bcast", [P, P])
        wdh, wdl = N.sb("wdh", [P, NC], F32R), N.sb("wdl", [P, NC], F32R)
        bd, w2, b2 = N.sb("bd", [P, NC]), N.sb("w2", [P, NC]), N.sb("b2", [P, NC])
        st, mv = N.sb("st", [P, BLK, 6]), N.sb("mv", [P, BLK, 2])
        st2, mv2, rstd2 = N.sb("st2", [P, BLK, 6]), N.sb("mv2", [P, BLK, 2]), N.sb("rstd2", [P, BLK])
        var = N.sb("var", [P, BLK])
        xh = N.sb("xh", [P, 2, BLK, C])
        xth, xtl = N.sb("xth", [P, 2, L], F32R), N.sb("xtl", [P, 2, L], F32R)
        d = N.sb("d", [P, 2, BLK, NC])
        consts, done, pdone, w_ready, wb_ready, bd_ready, bd_free = N.sems(
            "consts done pdone w_ready wb_ready bd_ready bd_free")
        x_in = N.sems("x_in0 x_in1")
        x_next, mv_ready, rstd_ready, xh_ready, t_ready, th_ready, t_split, d_ready, d_free = N.sems(
            "x_next mv_ready rstd_ready xh_ready t_ready th_ready t_split d_ready d_free")
        mv2_ready, rstd2_ready, t_free = N.sems("mv2_ready rstd2_ready t_free")
        with nc.Block() as block:

            @block.sync
            def _(sp):
                sp.dma_start(ident[:, :], io["c_ident"]).then_inc(consts, 16)
                sp.dma_start(flip[:, :], io["c_flip"]).then_inc(consts, 16)
                sp.dma_start(w1[:, :], column(io["n1_w"])).then_inc(consts, 16)
                sp.dma_start(b1[:, :], column(io["n1_b"])).then_inc(consts, 16)
                sp.dma_start(wd[:, :], io["Wdin"]).then_inc(consts, 16)
                sp.dma_start(w2[:, :], rows(io["n2_w"])).then_inc(consts, 16)
                sp.dma_start(b2[:, :], rows(io["n2_b"])).then_inc(consts, 16)
                c = Counts(sp)
                with sp.Fori(0, NB // 2, 1) as i:
                    for u in range(2):
                        sp.wait_ge(x_next, c.next(x_next))
                        sp.dma_start(X[:, i * 2 + u, :, :],
                                     io["idx"][i * 2 + u].rearrange("(k p) c -> p k c", p=P)).then_inc(x_in[u], 16)
                    c.settle()

            @block.vector
            def _(dve):
                c = Counts(dve)
                dve.sem_inc(x_next, 2)
                dve.wait_ge(consts, 7 * 16)
                chain(dve, c, done, dve.memset(mhalf[:, :], -0.5))
                chain(dve, c, done, dve.tensor_copy(bcast[:, :], b1[:, :].broadcast_to([P, P])))
                dve.drain().then_inc(wb_ready, 1)
                dve.wait_ge(bd_ready, 1)
                chain(dve, c, done, dve.tensor_copy(bd[:, :], ps[:, 0, 0:NC]))
                chain(dve, c, done, dve.tensor_scalar(wd[:, :], wd[:, :], w1[:, :], None, ALU.mult))
                chain(dve, c, done, split(dve, c, done, wd[:, :], wdh[:, :], wdl[:, :]))
                dve.sem_inc(bd_free, 1)
                c.settle()
                with dve.Fori(0, NB // 2, 1) as i:
                    for u in range(2):
                        n = i * 2 + u
                        dve.wait_ge(x_in[u], c.next(x_in[u], 16))
                        dve.sem_inc(x_next, 1)
                        block_stats(dve, c, done, X[:, n, :, :], st, mv).then_inc(mv_ready, 1)
                        dve.wait_ge(rstd_ready, c.next(rstd_ready))
                        chain(dve, c, done, dve.tensor_copy(stats[:, n, :, 0], mv[:, :, 0]))
                        for b in range(BLK):
                            last = dve.tensor_scalar(xh[:, u, b, :], X[:, n, b, :], stats[:, n, b, 0:1],
                                                     stats[:, n, b, 1:2], ALU.subtract, ALU.mult)
                        last.then_inc(xh_ready, 1)
                        dve.wait_ge(th_ready, c.next(th_ready))
                        dve.tensor_tensor(xtl[:, u, :], ps[:, 1 + u, :], f32(xth[:, u, :]),
                                          ALU.subtract).then_inc(t_split, 1)
                        dve.wait_ge(d_ready, c.next(d_ready))
                        chain(dve, c, done, dve.tensor_tensor(
                            d[:, u, :, :], ps[:, 3 + u, 0:BLK * NC].rearrange("p (b h) -> p b h", b=BLK),
                            bd[:, :].unsqueeze(1).broadcast_to([P, BLK, NC]), ALU.add))
                        dve.sem_inc(d_free, 1)
                        block_stats(dve, c, done, d[:, u, :, :], st2, mv2).then_inc(mv2_ready, 1)
                        dve.wait_ge(rstd2_ready, c.next(rstd2_ready))
                        for b in range(BLK):
                            last = dve.tensor_scalar(d[:, u, b, :], d[:, u, b, :], mv2[:, b, 0:1],
                                                     rstd2[:, b:b + 1], ALU.subtract, ALU.mult)
                        chain(dve, c, done, last)
                        chain(dve, c, done, dve.tensor_tensor(
                            d[:, u, :, :], d[:, u, :, :], w2[:, :].unsqueeze(1).broadcast_to([P, BLK, NC]), ALU.mult))
                        chain(dve, c, done, dve.tensor_tensor(
                            U[:, :, :, n].rearrange("p h b -> p b h"), d[:, u, :, :],
                            b2[:, :].unsqueeze(1).broadcast_to([P, BLK, NC]), ALU.add))
                    c.settle()

            @block.gpsimd
            def _(pool):
                c = Counts(pool)
                with pool.Fori(0, NB // 2, 1) as i:
                    for u in range(2):
                        pool.wait_ge(mv_ready, c.next(mv_ready))
                        pool_rstd(pool, c, pdone, mv, var, mhalf, stats[:, i * 2 + u, :, 1]).then_inc(rstd_ready, 1)
                        pool.wait_ge(mv2_ready, c.next(mv2_ready))
                        pool_rstd(pool, c, pdone, mv2, var, mhalf, rstd2).then_inc(rstd2_ready, 1)
                    c.settle()

            @block.scalar
            def _(act):
                c = Counts(act)
                act.preload_act_table(ACT.Exp)
                with act.Fori(0, NB // 2, 1) as i:
                    for u in range(2):
                        act.wait_ge(t_ready, c.next(t_ready))
                        act.activation(xth[:, u, :], ps[:, 1 + u, :], ACT.Copy).then_inc(th_ready, 1)
                    c.settle()

            @block.tensor
            def _(pe):
                c = Counts(pe)
                pe.wait_ge(wb_ready, 1)
                pe.matmul(ps[:, 0, 0:NC], bcast[:, :], wd[:, :], start=True, stop=True).then_inc(bd_ready, 1)
                pe.wait_ge(bd_free, 1)
                pe.sem_inc(d_free, 2)
                with pe.Fori(0, NB // 2, 1) as i:
                    for u in range(2):
                        pe.wait_ge(xh_ready, c.next(xh_ready))
                        for b in range(BLK):
                            last = pe.transpose(ps[:, 1 + u, b * P:(b + 1) * P], xh[:, u, b, :], flip[:, :])
                        last.then_inc(t_ready, 1)
                        pe.wait_ge(t_split, c.next(t_split))
                        pe.wait_ge(d_free, c.next(d_free))
                        for b in range(BLK):
                            o = ps[:, 3 + u, b * NC:(b + 1) * NC]
                            tok = slice(b * P, (b + 1) * P)
                            pe.matmul(o, xth[:, u, tok], wdh[:, :], start=True, stop=False)
                            pe.matmul(o, xth[:, u, tok], wdl[:, :], start=False, stop=False)
                            last = pe.matmul(o, xtl[:, u, tok], wdh[:, :], start=False, stop=True)
                        last.then_inc(d_ready, 1)
                    c.settle()


def convolution_stage(nc, io, ps, U, kd, yd):
    with ExitStack() as ctx:
        N = Names(nc, ctx, "conv")
        CH = 4
        tz = N.sb("tz", [P, 2, CH, L])
        uw = N.sb("uw", [P, 2, CH, BLK, 32])
        y = N.sb("y", [P, 2, L])
        t_in, y_out = N.sems("t_in0 t_in1"), N.sems("y_out0 y_out1")
        t_next, u_ready, c_ready, c_free, y_ready, zeroed, u_next = N.sems(
            "t_next u_ready c_ready c_free y_ready zeroed u_next")
        with nc.Block() as block:

            @block.sync
            def _(sp):
                c = Counts(sp)
                with sp.Fori(0, NC // CH // 2, 1) as i:
                    for u in range(2):
                        sp.wait_ge(t_next, c.next(t_next))
                        g = i * 2 + u
                        src = kd.rearrange("(g a) x -> g a x", a=CH)[g]
                        src = bass.AP(tensor=kd.tensor, offset=src.offset,
                                      ap=[[1, P], [KROW, CH], [1, L]])
                        sp.dma_start(tz[:, u, :, :], src).then_inc(t_in[u], 16)
                    c.settle()

            @block.gpsimd
            def _(pool):
                c = Counts(pool)
                pool.memset(uw[:, :, :, :, :].rearrange("p a b c d -> p (a b c d)"), 0.0).then_inc(zeroed, 1)
                pool.wait_ge(zeroed, 1)
                with pool.Fori(0, NC // CH // 2, 1) as i:
                    for u in range(2):
                        pool.wait_ge(u_next, c.next(u_next))
                        pool.tensor_copy(uw[:, u, :, :, 0:NB],
                                         U[:, :, :, :].rearrange("p (g a) b n -> p g a b n", a=CH)[:, i * 2 + u]
                                         ).then_inc(u_ready, 1)
                    c.settle()

            @block.tensor
            def _(pe):
                c = Counts(pe)
                pe.sem_inc(t_next, 2)
                pe.sem_inc(u_next, 2)
                with pe.Fori(0, NC // CH // 2, 1) as i:
                    for u in range(2):
                        pe.wait_ge(t_in[u], c.next(t_in[u], 16))
                        pe.wait_ge(u_ready, c.next(u_ready))
                        pe.wait_ge(c_free, c.next(c_free))
                        for b in range(BLK):
                            for a in range(CH):
                                last = pe.matmul(ps[32 * a:32 * a + 32, u, b * P:L], uw[:, u, a, b, :],
                                                 tz[:, u, a, 0:L - b * P], start=(b == 0), stop=(b == BLK - 1),
                                                 skip_group_check=True)
                        last.then_inc(c_ready, 1)
                    c.settle()

            @block.vector
            def _(dve):
                c = Counts(dve)
                dve.sem_inc(c_free, 2)
                with dve.Fori(0, NC // CH // 2, 1) as i:
                    for u in range(2):
                        dve.wait_ge(c_ready, c.next(c_ready))
                        dve.sem_inc(t_next, 1)
                        dve.sem_inc(u_next, 1)
                        dve.wait_ge(y_out[u], c.next(y_out[u], 64))
                        dve.tensor_copy(y[:, u, :], ps[:, u, :]).then_inc(y_ready, 1)
                        dve.drain().then_inc(c_free, 1)
                    c.settle()
                dve.wait_ge(y_out[0], 64)
                dve.wait_ge(y_out[1], 64)

            @block.scalar
            def _(act):
                c = Counts(act)
                act.sem_inc(y_out[0], 64)
                act.sem_inc(y_out[1], 64)
                with act.Fori(0, NC // CH // 2, 1) as i:
                    for u in range(2):
                        act.wait_ge(y_ready, c.next(y_ready))
                        for a in range(CH):
                            dst = yd.rearrange("(g a) n l -> g a n l", a=CH)[i * 2 + u]
                            act.dma_start(dst[a], y[32 * a:32 * a + NB, u, :]).then_inc(y_out[u], 16)
                    c.settle()


def gate_stage(nc, io, ps, X, stats, ident, mhalf, yd):
    with ExitStack() as ctx:
        N = Names(nc, ctx, "gate")
        HB = HID // P
        w1, b1 = N.sb("w1", [P, 1]), N.sb("b1", [P, 1])
        wx = N.sb("wx", [P, HID])
        wxh, wxl = N.sb("wxh", [P, HID], F32R), N.sb("wxl", [P, HID], F32R)
        bx = N.sb("bx", [P, HB])
        wg = N.sb("wg", [P, HID])
        wgh, wgl = N.sb("wgh", [P, HID], F32R), N.sb("wgl", [P, HID], F32R)
        wo = N.sb("wo", [P, HB, C])
        bo = N.sb("bo", [P, C])
        sel = N.sb("sel", [P, 5])
        yt, ya, ys = N.sb("yt", [P, 2, L]), N.sb("ya", [P, L], F32R), N.sb("ys", [P, 2, L], F32R)
        xh = N.sb("xh", [P, 2, BLK, C])
        xth, xtl = N.sb("xth", [P, 2, L], F32R), N.sb("xtl", [P, 2, L], F32R)
        xg = N.sb("xg", [P, 2, L])
        gx = N.sb("gx", [P, 2, HB, L])
        r = N.sb("r", [P, 2, BLK, C])
        st, mv, var, rstd = (N.sb(n, [P, BLK, m]) for n, m in (("st", 6), ("mv", 2), ("var", 1), ("rstd", 1)))
        var, rstd = var[:, :, 0], rstd[:, :, 0]
        consts, done, pdone, bx_ready, w_done = N.sems("consts done pdone bx_ready w_done")
        y_in = N.sems("y_in0 y_in1")
        (y_next, ya_ready, ya_free, ys_ready, xh_ready, t_ready, th_ready, t_split, xg_ready, xgs_ready,
         g_ready, gx_ready, xg_free, o_ready, o_free, mv_ready, rstd_ready) = N.sems(
            "y_next ya_ready ya_free ys_ready xh_ready t_ready th_ready t_split xg_ready xgs_ready "
            "g_ready gx_ready xg_free o_ready o_free mv_ready rstd_ready")
        TB, XB, GB, OB = 0, 1, 3, 5
        with nc.Block() as block:

            @block.sync
            def _(sp):
                sp.dma_start(w1[:, :], column(io["n1_w"])).then_inc(consts, 16)
                sp.dma_start(b1[:, :], column(io["n1_b"])).then_inc(consts, 16)
                sp.dma_start(wx[:, :], io["Wxg"]).then_inc(consts, 16)
                for lo in (0, NC):
                    sp.dma_start(wg[lo:lo + NC, :], io["Wgate"]).then_inc(consts, 16)
                sp.dma_start(wo[:, :, :], io["Wout"].rearrange("(m p) c -> p m c", p=P)).then_inc(consts, 16)
                sp.dma_start(bo[:, :], rows(io["bout"])).then_inc(consts, 16)
                sp.dma_start(sel[:, :], io["c_half"]).then_inc(consts, 16)
                c = Counts(sp)
                with sp.Fori(0, NB // 2, 1) as i:
                    for u in range(2):
                        sp.wait_ge(y_next, c.next(y_next))
                        for lo in (0, NC):
                            sp.dma_start(yt[lo:lo + NC, u, :], yd[:, i * 2 + u, :]).then_inc(y_in[u], 16)
                    c.settle()

            @block.vector
            def _(dve):
                c = Counts(dve)
                dve.sem_inc(y_next, 2)
                dve.wait_ge(consts, 8 * 16)
                dve.wait_ge(bx_ready, 1)
                chain(dve, c, done, dve.tensor_copy(bx[:, :], ps[:, 0, 0:HB]))
                chain(dve, c, done, dve.tensor_scalar(wx[:, :], wx[:, :], w1[:, :], None, ALU.mult))
                chain(dve, c, done, split(dve, c, done, wx[:, :], wxh[:, :], wxl[:, :]))
                chain(dve, c, done, split(dve, c, done, wg[:, :], wgh[:, :], wgl[:, :]))
                chain(dve, c, done, dve.tensor_scalar(wgl[:, :], f32(wgl[:, :]), sel[:, 0:1], None, ALU.mult))
                dve.sem_inc(w_done, 1)
                c.settle()
                with dve.Fori(0, NB // 2, 1) as i:
                    for u in range(2):
                        n = i * 2 + u
                        for b in range(BLK):
                            last = dve.tensor_scalar(xh[:, u, b, :], X[:, n, b, :], stats[:, n, b, 0:1],
                                                     stats[:, n, b, 1:2], ALU.subtract, ALU.mult)
                        last.then_inc(xh_ready, 1)
                        dve.wait_ge(ya_ready, c.next(ya_ready))
                        chain(dve, c, done, dve.scalar_tensor_tensor(ys[:, u, :], f32(ya[:, :]), sel[:, 4:5],
                                                                     yt[:, u, :], ALU.mult, ALU.add))
                        dve.sem_inc(ys_ready, 1)
                        dve.sem_inc(ya_free, 1)
                        dve.wait_ge(th_ready, c.next(th_ready))
                        dve.tensor_tensor(xtl[:, u, :], ps[:, TB, :], f32(xth[:, u, :]),
                                          ALU.subtract).then_inc(t_split, 1)
                        for m in range(HB):
                            dve.wait_ge(g_ready, c.next(g_ready))
                            dve.wait_ge(xgs_ready, c.next(xgs_ready))
                            dve.tensor_tensor(gx[:, u, m, :], ps[:, GB + m % 2, :], xg[:, m % 2, :],
                                              ALU.mult).then_inc(gx_ready, 1)
                        dve.sem_inc(y_next, 1)
                        dve.wait_ge(o_ready, c.next(o_ready))
                        chain(dve, c, done, dve.scalar_tensor_tensor(
                            r[:, u, :, :].rearrange("p b c -> p (b c)"),
                            X[:, n, :, :].rearrange("p b c -> p (b c)"), 2.0, ps[:, OB + u, :], ALU.mult, ALU.add))
                        dve.sem_inc(o_free, 1)
                        chain(dve, c, done, dve.tensor_tensor(
                            r[:, u, :, :], r[:, u, :, :], bo[:, :].unsqueeze(1).broadcast_to([P, BLK, C]), ALU.add))
                        block_stats(dve, c, done, r[:, u, :, :], st, mv).then_inc(mv_ready, 1)
                        dve.wait_ge(rstd_ready, c.next(rstd_ready))
                        for b in range(BLK):
                            last = dve.tensor_scalar(X[:, n, b, :], r[:, u, b, :], mv[:, b, 0:1],
                                                     rstd[:, b:b + 1], ALU.subtract, ALU.mult)
                        chain(dve, c, done, last)
                    c.settle()

            @block.gpsimd
            def _(pool):
                c = Counts(pool)
                with pool.Fori(0, NB, 1):
                    pool.wait_ge(mv_ready, c.next(mv_ready))
                    pool_rstd(pool, c, pdone, mv, var, mhalf, rstd).then_inc(rstd_ready, 1)
                    c.settle()

            @block.scalar
            def _(act):
                c = Counts(act)
                act.preload_act_table(ACT.Exp)
                act.wait_ge(w_done, 1)
                act.sem_inc(ya_free, 1)
                with act.Fori(0, NB // 2, 1) as i:
                    for u in range(2):
                        act.wait_ge(y_in[u], c.next(y_in[u], 32))
                        act.wait_ge(ya_free, c.next(ya_free))
                        act.activation(ya[:, :], yt[:, u, :], ACT.Copy).then_inc(ya_ready, 1)
                        act.wait_ge(t_ready, c.next(t_ready))
                        act.activation(xth[:, u, :], ps[:, TB, :], ACT.Copy).then_inc(th_ready, 1)
                        for m in range(HB):
                            act.wait_ge(xg_ready, c.next(xg_ready))
                            act.activation(xg[:, m % 2, :], ps[:, XB + m % 2, :], ACT.Identity,
                                           bias=bx[:, m:m + 1]).then_inc(xgs_ready, 1)
                    c.settle()

            @block.tensor
            def _(pe):
                c = Counts(pe)
                pe.wait_ge(consts, 8 * 16)
                for m in range(HB):
                    last = pe.matmul(ps[:, 0, m:m + 1], wx[:, m * P:(m + 1) * P], b1[:, :], start=True, stop=True)
                last.then_inc(bx_ready, 1)
                pe.wait_ge(w_done, 1)
                pe.sem_inc(o_free, 2)
                pe.sem_inc(gx_ready, 2)
                with pe.Fori(0, NB // 2, 1) as i:
                    for u in range(2):
                        pe.wait_ge(xh_ready, c.next(xh_ready))
                        for b in range(BLK):
                            last = pe.transpose(ps[:, TB, b * P:(b + 1) * P], xh[:, u, b, :], ident[:, :])
                        last.then_inc(t_ready, 1)
                        pe.wait_ge(ys_ready, c.next(ys_ready))
                        pe.wait_ge(t_split, c.next(t_split))
                        for m in range(HB):
                            pe.wait_ge(gx_ready, c.next(gx_ready))
                            w = slice(m * P, (m + 1) * P)
                            o = ps[:, XB + m % 2, :]
                            pe.matmul(o, wxh[:, w], xth[:, u, :], start=True, stop=False)
                            pe.matmul(o, wxl[:, w], xth[:, u, :], start=False, stop=False)
                            pe.matmul(o, wxh[:, w], xtl[:, u, :], start=False, stop=True).then_inc(xg_ready, 1)
                            o = ps[:, GB + m % 2, :]
                            pe.matmul(o, wgh[:, w], ys[:, u, :], start=True, stop=False)
                            pe.matmul(o, wgl[:, w], ys[:, u, :], start=False, stop=True).then_inc(g_ready, 1)
                        pe.wait_ge(gx_ready, c.next(gx_ready, 2))
                        pe.sem_inc(gx_ready, 2)
                        pe.wait_ge(o_free, c.next(o_free))
                        for b in range(BLK):
                            for m in range(HB):
                                last = pe.matmul(ps[:, OB + u, b * P:(b + 1) * P], gx[:, u, m, b * P:(b + 1) * P],
                                                 wo[:, m, :], start=(m == 0), stop=(m == HB - 1))
                        last.then_inc(o_ready, 1)
                    c.settle()



KIND_LATENT, KIND_DIRECT = range(2)
UNITS1 = [(0, 0, 4)] + [(1, h, 2) for h in (0, 2)] + [(j, h, 1) for j in (2, 3) for h in range(HG)]
UNITS2 = [u for a in (0, 2) for u in ([(a, 0, 0, L)], [(a, 3, 0, P), (a, 1, P, L - P)],
                                      [(a + 1, 0, 0, L)], [(a + 1, 3, 0, P), (a + 1, 1, P, L - P)],
                                      [(a, 2, 0, 2 * P), (a + 1, 2, 2 * P, 2 * P)])]
WHERE = {(h, kb): (n, at, w) for n, unit in enumerate(UNITS2) for h, kb, at, w in unit}
DIAGONALS = [sorted(at for _, _, at, _ in unit) for unit in UNITS2]


def spread(ap):
    return ap.rearrange("p (g hh d) -> p hh d g", g=NG, hh=HG)


def compact(ap):
    return ap.rearrange("p (hh d g) -> p hh d g", hh=HG, d=HD)


def attention_stage(nc, io, ps, X, ident, mhalf, Qb, Kb, kind, xm_d=None):
    name = "mla" if kind == KIND_LATENT else "mha"
    latent = kind == KIND_LATENT
    with ExitStack() as ctx:
        N = Names(nc, ctx, name)
        mask, identb = N.sb("mask", [P, P], BF16), N.sb("identb", [P, P], BF16)
        xs = N.sb("xs", [P, BLK, C])
        xth, xtl = N.sb("xth", [P, L], F32R), N.sb("xtl", [P, L], F32R)
        qh, ql, kh, kl = (N.sb(n, [P, L], F32R) for n in ("qh", "ql", "kh", "kl"))
        tmp = N.sb("tmp", [P, L])
        tmp2 = xs[:, :, :].rearrange("p b c -> p (b c)")
        V = N.sb("V", [P, 2, BLK, NH, HD + 1])
        prob = N.sb("prob", [P, 2, len(UNITS2), L])
        nm = N.sb("nm", [P, 2, BLK, HG])
        mh, ml = N.sb("mh", [HG, 2, L], F32R), N.sb("ml", [HG, 2, L], F32R)
        osb = N.sb("osb", [P, L])
        rec = N.sb("rec", [P, BLK, HG])
        ctxs = N.sb("ctxs", [P, 2, BLK, C])
        ctxt = tmp
        st, mv = N.sb("st", [P, BLK, 6]), N.sb("mv", [P, BLK, 2])
        var, rstd = N.sb("var", [P, BLK]), N.sb("rstd", [P, BLK])
        xm = N.sb("xm", [P, BLK, C])
        wo = N.sb("wo", [P, C])
        raw, raw2, maskf = prob[:, 0, 0, 0:3 * P], prob[:, 0, 1, 0:3 * P], prob[:, 0, 4, 0:P]
        if latent:
            w1 = N.sb("w1", [P, 1])
            sel = N.sb("sel", [P, 2])
            phalf = N.sb("phalf", [P, BLK])
            lath, latl = N.sb("lath", [P, 2, 96], F32R), N.sb("latl", [P, 2, 96], F32R)
            up = N.sb("up", [96, 4, P], F32R)
            upa = qh[0:96, :].rearrange("p (a m) -> p a m", a=4)
            upw = prob[0:96, 0, 2, :].rearrange("p (a m) -> p a m", a=4)
            kxw = prob[:, 0, 3, 0:2 * P].rearrange("p (a m) -> p a m", a=2)
            kxh, kxl = N.sb("kxh", [P, 2, P], F32R), N.sb("kxl", [P, 2, P], F32R)
            cosr, sinr = N.sb("cosr", [P, L]), N.sb("sinr", [P, L])
            lata = (qh[0:96, :], kh[0:96, :])
            lats = N.sb("lats", [96, 2, L], F32R)
        else:
            wph, wpl = N.sb("wph", [P, 3, P], F32R), N.sb("wpl", [P, 3, P], F32R)
            bcol = N.sb("bcol", [P, 2])
            vb, bd = N.sb("vb", [P, P]), N.sb("bd", [P, P])
        consts, done, pdone, adone, weights_ready, zero_ready = N.sems(
            "consts done pdone adone weights_ready zero_ready")
        (ma_free, mb_free, xs_ready, t_ready, th_ready, lat_ready, lata_ready, k_ready, k_full, k_high, k_split,
         q_ready, q_full, q_high, q_split, v_ready, k_rows, q_rows, kb_used) = N.sems(
            "ma_free mb_free xs_ready t_ready th_ready lat_ready lata_ready k_ready k_full k_high k_split "
            "q_ready q_full q_high q_split v_ready k_rows q_rows kb_used")
        (s1_ready, s1_free, nm_ready, mt_ready, mh_ready, ml_ready, s2_ready, e_ready, p_ready, o_ready,
         osb_ready, ot_ready, ct_ready, ctxt_ready, y_ready, mv_ready, rstd_ready, xm_ready) = N.sems(
            "s1_ready s1_free nm_ready mt_ready mh_ready ml_ready s2_ready e_ready p_ready o_ready "
            "osb_ready ot_ready ct_ready ctxt_ready y_ready mv_ready rstd_ready xm_ready")
        m_rows, (xm_out,) = N.sems("m_rows0 m_rows1"), N.sems("xm_out")
        S1, S2, OB, MA, MB = 0, 2, 4, 5, 6

        def has_probs(turn, g):
            return turn == "inner" or (turn == "first" and g >= 2) or (turn == "last" and g < 2)

        def has_values(turn, g):
            return turn == "inner" or (turn == "first" and g == 3) or (turn == "last" and g < 3)

        def walk(eng, c, body):
            body(0, 0, "first", True, True)
            c.settle()
            with eng.Fori(0, (NB - 4) // 2, 1) as i:
                for v in range(2):
                    body(i * 2 + (v + 1), (v + 1) % 2, "inner", True, True)
                c.settle()
            for n in range(NB - 3, NB):
                body(n, n % 2, "inner", n + 2 < NB, n + 1 < NB)
            body(NB, NB % 2, "last", False, False)

        with nc.Block() as block:

            @block.sync
            def _(sp):
                sp.dma_start(maskf, io["c_mask"]).then_inc(consts, 16)
                if latent:
                    sp.dma_start(w1[:, :], column(io["w_ln1"])).then_inc(consts, 16)
                    sp.dma_start(sel[:, :], io["c_rows"]).then_inc(consts, 16)
                    sp.dma_start(raw[:, 0:LAT], io["W_kvd"]).then_inc(consts, 16)
                    sp.dma_start(raw[:, LAT:2 * LAT], io["W_qd"]).then_inc(consts, 16)
                    sp.dma_start(raw[:, 2 * LAT:2 * LAT + 64], io["W_ropek"]).then_inc(consts, 16)
                    for lo in range(0, 96, LAT):
                        sp.dma_start(raw2[lo:lo + LAT, 0:64], io["W_qu"]).then_inc(consts, 16)
                        sp.dma_start(raw2[lo:lo + LAT, 64:128], io["W_ropeq"]).then_inc(consts, 16)
                        sp.dma_start(raw2[lo:lo + LAT, 128:192], io["W_ku"]).then_inc(consts, 16)
                        sp.dma_start(raw2[lo:lo + LAT, 192:320], io["W_vu"]).then_inc(consts, 16)
                    sp.dma_start(cosr[:, :], io["c_cos"]).then_inc(consts, 16)
                    sp.dma_start(sinr[:, :], io["c_sin"]).then_inc(consts, 16)
                    sp.dma_start(wo[:, :], io["W_o"]).then_inc(consts, 16)
                else:
                    sp.dma_start(raw, io["w_qkv"]).then_inc(consts, 16)
                    for at, lo in ((0, 0), (1, 2 * P)):
                        for hh in range(HG):
                            src = bass.AP(tensor=io["b_qkv"].tensor, offset=io["b_qkv"].offset + lo + hh * HD,
                                          ap=[[1, HD], [HG * HD, NG], [1, 1]])
                            sp.dma_start(bcol[32 * hh:32 * hh + 32, at:at + 1], src,
                                         allow_slow_non_contiguous=True).then_inc(consts, 16)
                    sp.dma_start(vb[:, :], rows(io["b_qkv"][P:2 * P])).then_inc(consts, 16)
                    sp.dma_start(bd[:, :], rows(io["b_dense"])).then_inc(consts, 16)
                    sp.dma_start(wo[:, :], io["w_dense"]).then_inc(consts, 16)
                c = Counts(sp)

                def keys(u):
                    sp.wait_ge(k_split, c.next(k_split))
                    for at in (0, 2):
                        sp.dma_start(f32(Kb[32 * at:32 * at + 32, u, :, :]), f32(kh[:, :])).then_inc(k_rows, 16)
                    sp.dma_start(f32(Kb[32:64, u, :, :]), f32(kl[:, :])).then_inc(k_rows, 16)

                def queries(u):
                    sp.wait_ge(q_split, c.next(q_split))
                    for hh in range(HG):
                        for at in (0, 1):
                            lo = 32 * at + HD * hh
                            sp.dma_start(f32(Qb[lo:lo + HD, u, hh, :, :]), f32(qh[32 * hh:32 * hh + 32, :])).then_inc(q_rows, 16)
                    for hh in range(HG):
                        lo = 64 + HD * hh
                        sp.dma_start(f32(Qb[lo:lo + HD, u, hh, :, :]), f32(ql[32 * hh:32 * hh + 32, :])).then_inc(q_rows, 16)

                def slots(n, u, turn, prep, proj):
                    for g in range(NG):
                        if turn != "last":
                            if g == 1 and proj:
                                sp.wait_ge(kb_used, c.next(kb_used))
                                keys(1 - u)
                            if g == 2 and proj:
                                queries(1 - u)
                            sp.wait_ge(ml_ready, c.next(ml_ready))
                            sp.dma_start(f32(Qb[MROW:MROW + 1, u, :, g, :]), f32(mh[:, g % 2, :])).then_inc(m_rows[g % 2], 16)
                            sp.dma_start(f32(Qb[MROW + 1:MROW + 2, u, :, g, :]), f32(ml[:, g % 2, :])).then_inc(m_rows[g % 2], 16)
                        if g == 3 and turn != "first" and latent:
                            sp.wait_ge(xm_ready, c.next(xm_ready))
                            sp.dma_start(xm_d[n - 1].rearrange("(k p) c -> p k c", p=P),
                                         xm[:, :, :]).then_inc(xm_out, 16)

                sp.wait_ge(zero_ready, 2)
                keys(0)
                queries(0)
                walk(sp, c, slots)

            @block.vector
            def _(dve):
                c = Counts(dve)
                link = lambda ins: chain(dve, c, done, ins)
                link(dve.memset(V[:, :, :, :, HD:HD + 1], 1.0))
                link(dve.memset(ps[:, OB, :], 0.0))
                if latent:
                    dve.memset(f32(Kb[MROW:P, :, :, :].rearrange("p a g l -> p (a g l)")), 1.0).then_inc(zero_ready, 1)
                    link(dve.memset(mhalf[:, :], -0.5))
                    link(dve.memset(phalf[:, :], 0.5))
                    link(dve.memset(upw[:, :, :], 0.0))
                    link(dve.memset(kxw[:, :, :], 0.0))
                else:
                    dve.sem_inc(zero_ready, 1)
                nconst = (6 + 12 + 3) if latent else (1 + 1 + 8 + 3)
                dve.wait_ge(consts, nconst * 16)
                link(dve.tensor_copy(mask[:, :], maskf))
                link(dve.tensor_copy(identb[:, :], ident[:, :]))
                if latent:
                    link(dve.tensor_scalar(raw[:, 0:P], raw[:, 0:P], w1[:, :], None, ALU.mult))
                    for s in range(3):
                        link(dve.tensor_copy(raw[:, P + LAT * s:P + LAT * (s + 1)], raw[:, LAT:2 * LAT]))
                        link(dve.tensor_copy(raw[:, P + 96 + LAT * s:P + 96 + LAT * (s + 1)], raw[:, 0:LAT]))
                    link(split(dve, c, done, raw[:, P:P + 192].rearrange("p (a m) -> p a m", a=2),
                               lath[:, :, :], latl[:, :, :]))
                    half = HD // 2

                    def turned(dst, src):
                        link(dve.tensor_scalar(dst[:, :, half:half + 2, :], src[:, :, 2:4, :], -1.0, None, ALU.mult))
                        link(dve.tensor_copy(dst[:, :, half + 2:HD, :], src[:, :, 0:2, :]))

                    for hh in range(HG):
                        one = lambda ap: ap[:, hh:hh + 1]
                        link(dve.tensor_copy(one(compact(upw[:, 0, :]))[:, 0, 0:half, :],
                                             one(spread(raw2[0:96, 0:64]))[:, 0]))
                        link(dve.tensor_copy(one(compact(upw[:, 0, :]))[:, 0, half:HD, :],
                                             one(spread(raw2[0:96, 64:128]))[:, 0]))
                        link(dve.tensor_copy(one(compact(upw[:, 2, :]))[:, 0, 0:half, :],
                                             one(spread(raw2[0:96, 128:192]))[:, 0]))
                        link(dve.tensor_copy(one(compact(kxw[:, 0, :]))[:, 0, half:HD, :],
                                             one(spread(raw[:, 2 * LAT:2 * LAT + 64]))[:, 0]))
                        turned(one(compact(upw[:, 1, :])), one(spread(raw2[0:96, 64:128])))
                        turned(one(compact(kxw[:, 1, :])), one(spread(raw[:, 2 * LAT:2 * LAT + 64])))
                    link(dve.tensor_copy(upw[:, 3, :], raw2[0:96, 192:320]))
                    link(split(dve, c, done, kxw[:, :, :], kxh[:, :, :], kxl[:, :, :]))
                    link(dve.tensor_copy(upa[:, :, :], upw[:, :, :]))
                    link(dve.scalar_tensor_tensor(up[:, :, :].rearrange("p a m -> p (a m)"),
                                                  f32(upa[:, :, :]).rearrange("p a m -> p (a m)"), sel[0:96, 1:2],
                                                  upw[:, :, :].rearrange("p a m -> p (a m)"), ALU.mult, ALU.add))
                else:
                    for a, at in ((0, 0), (2, 2 * P)):
                        for hh in range(HG):
                            link(dve.tensor_copy(compact(raw2[:, a * P:(a + 1) * P])[:, hh],
                                                 spread(raw[:, at:at + P])[:, hh]))
                    link(dve.tensor_copy(raw2[:, P:2 * P], raw[:, P:2 * P]))
                    link(split(dve, c, done, raw2.rearrange("p (a m) -> p a m", a=3), wph[:, :, :], wpl[:, :, :]))
                dve.sem_inc(weights_ready, 1)
                dve.sem_inc(ma_free, 1)
                dve.sem_inc(mb_free, 1)
                dve.sem_inc(s1_free, 2)
                if latent:
                    dve.sem_inc(xm_out, 16)
                c.settle()

                def prepare(n):
                    if not latent:
                        link(dve.tensor_copy(xs[:, :, :], X[:, n, :, :]))
                        dve.sem_inc(xs_ready, 1)
                        return
                    link(block_stats(dve, c, done, X[:, n, :, :], st, mv))
                    link(dve.tensor_tensor(var[:, :], mv[:, :, 0], mv[:, :, 0], ALU.mult))
                    dve.tensor_tensor(var[:, :], var[:, :], mv[:, :, 1], ALU.add).then_inc(mv_ready, 1)
                    dve.wait_ge(rstd_ready, c.next(rstd_ready))
                    link(dve.tensor_scalar(var[:, :], rstd[:, :], EPS, None, ALU.add))
                    link(dve.reciprocal(var[:, :], var[:, :]))
                    for b in range(BLK):
                        last = dve.tensor_scalar(xs[:, b, :], X[:, n, b, :], var[:, b:b + 1], None, ALU.mult)
                    link(last)
                    dve.sem_inc(xs_ready, 1)

                def low_x():
                    dve.wait_ge(th_ready, c.next(th_ready))
                    dve.tensor_tensor(xtl[:, :], ps[:, MA, :], f32(xth[:, :]), ALU.subtract).then_inc(ma_free, 1)

                def low_latents():
                    for a, bank, free in ((1, MA, ma_free), (0, MB, mb_free)):
                        dve.wait_ge(lata_ready, c.next(lata_ready))
                        dve.scalar_tensor_tensor(lats[:, a, :], f32(lata[a]), sel[0:96, 0:1],
                                                 ps[0:96, bank, :], ALU.mult, ALU.add).then_inc(free, 1)

                def low_part(ready, full, high, hi, lo, split_done):
                    if latent:
                        dve.wait_ge(ready, c.next(ready))
                        link(dve.tensor_tensor(tmp2, ps[:, MB, :], sinr[:, :], ALU.mult))
                        dve.sem_inc(mb_free, 1)
                        link(dve.tensor_tensor(tmp[:, :], ps[:, MA, :], cosr[:, :], ALU.mult))
                        dve.sem_inc(ma_free, 1)
                        dve.tensor_tensor(tmp[:, :], tmp[:, :], tmp2, ALU.add).then_inc(full, 1)
                    dve.wait_ge(high, c.next(high))
                    link(dve.tensor_tensor(lo[:, :], tmp[:, :], f32(hi[:, :]), ALU.subtract))
                    dve.sem_inc(split_done, 1)
                    if not latent:
                        dve.sem_inc(ma_free, 1)

                def values(u):
                    if latent:
                        return
                    dve.wait_ge(v_ready, c.next(v_ready))
                    for b in range(BLK):
                        last = dve.tensor_tensor(
                            V[:, u, b, :, 0:HD], ps[:, MA, b * P:(b + 1) * P].rearrange("p (h d) -> p h d", h=NH),
                            vb[:, :].rearrange("p (h d) -> p h d", h=NH), ALU.add)
                    last.then_inc(ma_free, 1)

                def normalise(par, g):
                    dve.wait_ge(ot_ready, c.next(ot_ready))
                    o = ps[:, MB, :].rearrange("p (j h m) -> p j h m", j=BLK, h=HG)
                    link(dve.reciprocal(rec[:, :, :], o[:, :, :, HD]))
                    dve.tensor_tensor(
                        ctxs[:, par, :, g * 32:g * 32 + 32].rearrange("p j (h d) -> p j h d", h=HG),
                        o[:, :, :, 0:HD], rec[:, :, :].unsqueeze(3).broadcast_to([P, BLK, HG, HD]),
                        ALU.mult).then_inc(mb_free, 1)

                def finish(n):
                    x = X[:, n, :, :]
                    if latent:
                        dve.wait_ge(xm_out, c.next(xm_out, 16))
                    dve.wait_ge(y_ready, c.next(y_ready))
                    y = ps[:, MB, :].rearrange("p (b c) -> p b c", b=BLK)
                    link(dve.tensor_tensor(xm[:, :, :], x, y, ALU.add))
                    dve.sem_inc(mb_free, 1)
                    if latent:
                        dve.sem_inc(xm_ready, 1)
                        link(dve.tensor_tensor(x, x, xm[:, :, :], ALU.add))
                    else:
                        link(dve.tensor_tensor(xm[:, :, :], xm[:, :, :],
                                               bd[:, :].unsqueeze(1).broadcast_to([P, BLK, C]), ALU.add))
                        block_stats(dve, c, done, xm[:, :, :], st, mv).then_inc(mv_ready, 1)
                        dve.wait_ge(rstd_ready, c.next(rstd_ready))
                        for b in range(BLK):
                            last = dve.tensor_scalar(X[:, n, b, :], xm[:, b, :], mv[:, b, 0:1],
                                                     rstd[:, b:b + 1], ALU.subtract, ALU.mult)
                        link(last)

                def project(g, u):
                    if g == 0 and latent:
                        low_latents()
                    if g == 1:
                        low_part(k_ready, k_full, k_high, kh, kl, k_split)
                    if g == 2:
                        low_part(q_ready, q_full, q_high, qh, ql, q_split)
                        values(u)

                def slots(n, u, turn, prep, proj):
                    for g in range(NG):
                        if g == 0 and proj:
                            low_x()
                        if turn != "last":
                            for k, (j, h, heads) in enumerate(UNITS1):
                                dve.wait_ge(s1_ready, c.next(s1_ready))
                                w = P * (j + 1)
                                dve.tensor_reduce(
                                    nm[:, g % 2, j, h:h + heads],
                                    ps[:, S1 + (g * len(UNITS1) + k) % 2, 0:heads * w].rearrange(
                                        "p (h k) -> p h k", h=heads),
                                    axis=AX.X, op=ALU.max, negate=True).then_inc(s1_free, 1)
                            dve.drain().then_inc(nm_ready, 1)
                        if has_values(turn, g):
                            normalise(u if g == 3 else 1 - u, (g + 1) % NG)
                        if proj:
                            project(g, 1 - u)
                        if turn != "last":
                            dve.wait_ge(mh_ready, c.next(mh_ready))
                            link(dve.tensor_tensor(ml[:, g % 2, :], ps[0:HG, MA, :], f32(mh[:, g % 2, :]),
                                                   ALU.subtract))
                            dve.sem_inc(ml_ready, 1)
                            dve.sem_inc(ma_free, 1)
                        if g == 3 and turn != "first":
                            finish(n - 1)
                        if g == 3 and prep:
                            prepare(n + 2)

                prepare(0)
                low_x()
                for g in range(3):
                    project(g, 0)
                prepare(1)
                walk(dve, c, slots)
                if latent:
                    dve.wait_ge(xm_out, c.next(xm_out, 16))

            @block.gpsimd
            def _(pool):
                c = Counts(pool)
                if latent:
                    pool.memset(f32(Qb[:, :, :, :, :].rearrange("p a h g l -> p (a h g l)")), 0.0).then_inc(zero_ready, 1)
                else:
                    pool.sem_inc(zero_ready, 1)

                def rms_or_rstd():
                    pool.wait_ge(mv_ready, c.next(mv_ready))
                    if latent:
                        pool.tensor_tensor(rstd[:, :], var[:, :], phalf[:, :], ALU.pow).then_inc(rstd_ready, 1)
                    else:
                        pool_rstd(pool, c, pdone, mv, var, mhalf, rstd).then_inc(rstd_ready, 1)

                def slots(n, u, turn, prep, proj):
                    for g in range(NG):
                        if has_probs(turn, g):
                            for k, ats in enumerate(DIAGONALS):
                                pool.wait_ge(e_ready, c.next(e_ready))
                                if len(ats) == 1:
                                    part, pattern = prob[:, g % 2, k, 0:P], [[1, P]]
                                else:
                                    step = ats[1]
                                    part = prob[:, g % 2, k, 0:2 * step].rearrange("p (a w) -> p a w", a=2)[:, :, 0:P]
                                    pattern = [[0, 2], [1, P]]
                                pool.affine_select(out=part, in_=part, compare_op=ALU.is_ge, fill=0.0, base=0,
                                                   pattern=pattern, channel_multiplier=-1).then_inc(p_ready, 1)
                        if g == 3 and (prep if latent else turn != "first"):
                            rms_or_rstd()

                if latent:
                    rms_or_rstd()
                    rms_or_rstd()
                walk(pool, c, slots)

            @block.scalar
            def _(act):
                c = Counts(act)
                act.preload_act_table(ACT.Exp)

                def high_x():
                    act.wait_ge(t_ready, c.next(t_ready))
                    act.activation(xth[:, :], ps[:, MA, :], ACT.Copy).then_inc(th_ready, 1)

                def high_part(ready, full, high, hi, col):
                    if latent:
                        act.wait_ge(full, c.next(full))
                    else:
                        act.wait_ge(ready, c.next(ready))
                        chain(act, c, adone, act.activation(tmp[:, :], ps[:, MA, :], ACT.Identity,
                                                            bias=bcol[:, col:col + 1]))
                    act.activation(hi[:, :], tmp[:, :], ACT.Copy).then_inc(high, 1)

                def project(g, u):
                    if g == 0 and latent:
                        for a, bank in ((1, MA), (0, MB)):
                            act.wait_ge(lat_ready, c.next(lat_ready))
                            act.activation(lata[a], ps[0:96, bank, :], ACT.Copy).then_inc(lata_ready, 1)
                    if g == 1:
                        high_part(k_ready, k_full, k_high, kh, 0)
                    if g == 2:
                        high_part(q_ready, q_full, q_high, qh, 1)
                        if latent:
                            act.wait_ge(v_ready, c.next(v_ready))
                            act.activation(V[:, u, :, :, 0:HD],
                                           ps[:, MA, :].rearrange("p (b h d) -> p b h d", b=BLK, h=NH),
                                           ACT.Copy).then_inc(ma_free, 1)

                def slots(n, u, turn, prep, proj):
                    for g in range(NG):
                        if g == 0 and proj:
                            high_x()
                        if has_probs(turn, g):
                            for k in range(len(UNITS2)):
                                act.wait_ge(s2_ready, c.next(s2_ready))
                                act.activation(prob[:, g % 2, k, :], ps[:, S2 + k % 2, :], ACT.Exp,
                                               scale=HD ** -0.5).then_inc(e_ready, 1)
                        if has_values(turn, g):
                            act.wait_ge(o_ready, c.next(o_ready))
                            act.activation(osb[:, :], ps[:, OB, :], ACT.Copy).then_inc(osb_ready, 1)
                        if proj:
                            project(g, 1 - u)
                        if turn != "last":
                            act.wait_ge(mt_ready, c.next(mt_ready))
                            act.activation(mh[:, g % 2, :], ps[0:HG, MA, :], ACT.Copy).then_inc(mh_ready, 1)
                        if g == 3 and turn != "first":
                            act.wait_ge(ct_ready, c.next(ct_ready))
                            act.activation(ctxt[:, :], ps[:, MA, :], ACT.Copy).then_inc(ctxt_ready, 1)

                high_x()
                for g in range(3):
                    project(g, 0)
                walk(act, c, slots)

            @block.tensor
            def _(pe):
                c = Counts(pe)
                pe.wait_ge(weights_ready, 1)
                pe.sem_inc(p_ready, 2)

                def three(o, hi, lo, a, first=True, last=True):
                    pe.matmul(o, hi, xth[:, :], start=first, stop=False)
                    pe.matmul(o, lo, xth[:, :], start=False, stop=False)
                    return pe.matmul(o, hi, xtl[:, :], start=False, stop=last)

                def transpose_x():
                    pe.wait_ge(xs_ready, c.next(xs_ready))
                    pe.wait_ge(ma_free, c.next(ma_free))
                    for b in range(BLK):
                        last = pe.transpose(ps[:, MA, b * P:(b + 1) * P], xs[:, b, :], ident[:, :])
                    last.then_inc(t_ready, 1)

                def project(g, u):
                    if g == 0 and latent:
                        for a, bank, free in ((1, MA, ma_free), (0, MB, mb_free)):
                            pe.wait_ge(free, c.next(free))
                            three(ps[0:96, bank, :], lath[:, a, :], latl[:, a, :], a).then_inc(lat_ready, 1)
                    if g == 1:
                        pe.wait_ge(ma_free, c.next(ma_free))
                        if latent:
                            pe.wait_ge(mb_free, c.next(mb_free))
                            pe.matmul(ps[:, MA, :], up[:, 2, :], lats[:, 1, :], start=True, stop=False)
                            three(ps[:, MA, :], kxh[:, 0, :], kxl[:, 0, :], 0, first=False)
                            three(ps[:, MB, :], kxh[:, 1, :], kxl[:, 1, :], 0).then_inc(k_ready, 1)
                        else:
                            three(ps[:, MA, :], wph[:, 0, :], wpl[:, 0, :], 0).then_inc(k_ready, 1)
                    if g == 2:
                        pe.wait_ge(ma_free, c.next(ma_free))
                        if latent:
                            pe.wait_ge(mb_free, c.next(mb_free))
                            pe.matmul(ps[:, MA, :], up[:, 0, :], lats[:, 0, :], start=True, stop=True)
                            pe.matmul(ps[:, MB, :], up[:, 1, :], lats[:, 0, :], start=True,
                                      stop=True).then_inc(q_ready, 1)
                        else:
                            three(ps[:, MA, :], wph[:, 2, :], wpl[:, 2, :], 0).then_inc(q_ready, 1)
                        pe.wait_ge(ma_free, c.next(ma_free))
                        for b in range(BLK):
                            tok = slice(b * P, (b + 1) * P)
                            o = ps[:, MA, tok]
                            if latent:
                                last = pe.matmul(o, lats[:, 1, tok], up[:, 3, :], start=True, stop=True)
                            else:
                                pe.matmul(o, xth[:, tok], wph[:, 1, :], start=True, stop=False)
                                pe.matmul(o, xth[:, tok], wpl[:, 1, :], start=False, stop=False)
                                last = pe.matmul(o, xtl[:, tok], wph[:, 1, :], start=False, stop=True)
                        last.then_inc(v_ready, 1)

                def scores(g, u, k):
                    j, h, heads = UNITS1[k]
                    w = P * (j + 1)
                    bank = S1 + (g * len(UNITS1) + k) % 2
                    pe.wait_ge(s1_free, c.next(s1_free))
                    for x in range(heads):
                        pe.matmul(ps[:, bank, x * w:(x + 1) * w], Qb[0:MROW, u, h + x, g, j * P:(j + 1) * P],
                                  Kb[0:MROW, u, g, 0:w], start=True, stop=False)
                        last = pe.matmul(ps[:, bank, (x + 1) * w - P:(x + 1) * w], identb[:, :], mask[:, :],
                                         start=False, stop=True)
                    last.then_inc(s1_ready, 1)

                def scores_less_max(grp, u, k):
                    pe.wait_ge(p_ready, c.next(p_ready))
                    for h, kb, at, w in UNITS2[k]:
                        last = pe.matmul(ps[:, S2 + k % 2, at:at + w],
                                         Kb[0:MROW + 2, u, grp, kb * P:(kb + 1) * P],
                                         Qb[0:MROW + 2, u, h, grp, kb * P:L], start=True, stop=True)
                    last.then_inc(s2_ready, 1)

                def times_v(grp, u, par, kb):
                    for hh in range(HG):
                        unit, at, w = WHERE[hh, kb]
                        last = pe.matmul(ps[32 * hh:32 * hh + HD + 1, OB, kb * P:L], V[:, u, kb, grp * HG + hh, :],
                                         prob[:, par, unit, at:at + w], start=(kb == 0), stop=(kb == BLK - 1),
                                         skip_group_check=True)
                    return last

                def slots(n, u, turn, prep, proj):
                    for g in range(NG):
                        if g == 0 and proj:
                            transpose_x()
                        if g == 0 and turn != "last":
                            pe.wait_ge(k_rows, c.next(k_rows, 3 * 16))
                            pe.wait_ge(q_rows, c.next(q_rows, 12 * 16))
                        if has_probs(turn, g):
                            pe.wait_ge(m_rows[g % 2], c.next(m_rows[g % 2], 32))
                        elif has_values(turn, g):
                            pe.wait_ge(p_ready, c.next(p_ready, 2))
                        for k in range(len(UNITS1)):
                            if turn != "last":
                                scores(g, u, k)
                            if has_probs(turn, g) and k < len(UNITS2):
                                scores_less_max((g + 2) % NG, u if g >= 2 else 1 - u, k)
                            if has_values(turn, g) and k in (3, 5, 7, 9):
                                last = times_v((g + 1) % NG, u if g == 3 else 1 - u, (g + 1) % 2, (k - 3) // 2)
                        if g == 1 and turn != "last":
                            pe.drain().then_inc(kb_used, 1)
                        if has_values(turn, g):
                            last.then_inc(o_ready, 1)
                            pe.wait_ge(osb_ready, c.next(osb_ready))
                            pe.wait_ge(mb_free, c.next(mb_free))
                            for j in range(BLK):
                                last = pe.transpose(ps[:, MB, j * P:(j + 1) * P],
                                                    osb[:, j * P:(j + 1) * P], ident[:, :])
                            last.then_inc(ot_ready, 1)
                        if proj:
                            project(g, 1 - u)
                        if turn != "last":
                            pe.wait_ge(nm_ready, c.next(nm_ready))
                            pe.wait_ge(ma_free, c.next(ma_free))
                            for j in range(BLK):
                                last = pe.transpose(ps[0:HG, MA, j * P:(j + 1) * P], nm[:, g % 2, j, :], ident[:, :])
                            last.then_inc(mt_ready, 1)
                        if g == 3 and turn != "first":
                            pe.wait_ge(mb_free, c.next(mb_free))
                            pe.wait_ge(ma_free, c.next(ma_free))
                            for b in range(BLK):
                                last = pe.transpose(ps[:, MA, b * P:(b + 1) * P], ctxs[:, 1 - u, b, :], ident[:, :])
                            last.then_inc(ct_ready, 1)
                            pe.wait_ge(ctxt_ready, c.next(ctxt_ready))
                            pe.sem_inc(ma_free, 1)
                            for b in range(BLK):
                                last = pe.matmul(ps[:, MB, b * P:(b + 1) * P], ctxt[:, b * P:(b + 1) * P], wo[:, :],
                                                 start=True, stop=True)
                            last.then_inc(y_ready, 1)

                transpose_x()
                for g in range(3):
                    project(g, 0)
                walk(pe, c, slots)



KIND_SWIGLU, KIND_GELU = range(2)


def experts_stage(nc, io, ps, X, ident, mhalf, kind, xm_d=None, out=None):
    swiglu = kind == KIND_SWIGLU
    with ExitStack() as ctx:
        N = Names(nc, ctx, "glu" if swiglu else "moe")
        EXP = E0 if swiglu else E1
        R = E0 - 1 if swiglu else E1
        FIRST = EXP - R
        HB = 1 if swiglu else H1B
        UNITS = EXP * HB
        WB = 2 if swiglu else HB
        w_raw = N.sb("w_raw", [P, EXP, WB, P])
        wh, wl = N.sb("wh", [P, EXP, WB, P], F32R), N.sb("wl", [P, EXP, WB, P], F32R)
        wd = N.sb("wd", [P, EXP, HB, C])
        wr = N.sb("wr", [P, R])
        wrh, wrl = N.sb("wrh", [P, 8], F32R), N.sb("wrl", [P, 8], F32R)
        rb = N.sb("rb", [P, R])
        desc, euler, minus1 = N.sb("desc", [P, R]), N.sb("euler", [P, BLK, R]), N.sb("minus1", [P, BLK, R])
        xs = N.sb("xs", [P, BLK, C])
        xth, xtl = N.sb("xth", [P, 2, L], F32R), N.sb("xtl", [P, 2, L], F32R)
        hid = N.sb("hid", [P, 2, L])
        wts = N.sb("wts", [P, 2, BLK, R])
        acc = N.sb("acc", [P, 2, BLK, C])
        lg, pr, ex, eq, sel1, sel2 = (N.sb(n, [P, BLK, R]) for n in ("lg", "pr", "ex", "eq", "sel1", "sel2"))
        m1, m2, den = (N.sb(n, [P, BLK]) for n in ("m1", "m2", "den"))
        st, mv = N.sb("st", [P, BLK, 6]), N.sb("mv", [P, BLK, 2])
        var, rstd = N.sb("var", [P, BLK]), N.sb("rstd", [P, BLK])
        if swiglu:
            w2 = N.sb("w2", [P, 1])
            xi = N.sb("xi", [P, 2, BLK, C])
            sg = N.sb("sg", [P, 2, L])
            phalf, ms, rms = (N.sb(n, [P, BLK]) for n in ("phalf", "ms", "rms"))
            mv2 = N.sb("mv2", [P, BLK, 2])
        else:
            b1 = N.sb("b1", [P, EXP, HB])
            b2 = N.sb("b2", [EXP, C])
            wt = N.sb("wt", [EXP, L])
        consts, done, pdone, weights_ready, router_ready = N.sems("consts done pdone weights_ready router_ready")
        (xi_next, ms_ready, rms_ready, xs_ready, xs_free, t_ready, th_ready, x_ready, l_ready, lg_ready, pr_ready,
         wts_ready, wtt_ready, wt_ready, b_ready, b_free) = N.sems(
            "xi_next ms_ready rms_ready xs_ready xs_free t_ready th_ready x_ready l_ready lg_ready pr_ready "
            "wts_ready wtt_ready wt_ready b_ready b_free")
        f_ready, s_ready, hid_ready, o_ready, o_free, mv_ready, rstd_ready, y_ready, stored = N.sems(
            "f_ready s_ready hid_ready o_ready o_free mv_ready rstd_ready y_ready stored")
        xi_in = N.sems("xi_in0 xi_in1")
        TB, FB, OB, LB = 0, 1, 5, 7

        def walk(eng, c, tile):
            tile(0, 0, True, True)
            c.settle()
            with eng.Fori(0, (NB - 2) // 2, 1) as i:
                for v in range(2):
                    tile(i * 2 + (v + 1), (v + 1) % 2, False, True)
                c.settle()
            tile(NB - 1, (NB - 1) % 2, False, False)

        with nc.Block() as block:

            @block.sync
            def _(sp):
                if swiglu:
                    sp.dma_start(w2[:, :], column(io["w_ln2"])).then_inc(consts, 16)
                    sp.dma_start(wr[:, :], io["W_router"]).then_inc(consts, 16)
                    sp.dma_start(rb[:, :], rows(io["routing_bias"])).then_inc(consts, 16)
                    for a, one, many in ((0, "Wg_s", "Wg_r"), (1, "Wu_s", "Wu_r")):
                        sp.dma_start(w_raw[:, 0, a, :], io[one]).then_inc(consts, 16)
                        sp.dma_start(w_raw[:, 1:E0, a, :], io[many].rearrange("e c i -> c e i")).then_inc(consts, 16)
                    sp.dma_start(wd[:, 0, 0, :], io["Wd_s"]).then_inc(consts, 16)
                    sp.dma_start(wd[:, 1:E0, 0, :], io["Wd_r"].rearrange("e i c -> i e c")).then_inc(consts, 16)
                else:
                    sp.dma_start(wr[:, :], io["Wg"]).then_inc(consts, 16)
                    sp.dma_start(rb[:, :], rows(io["bg"])).then_inc(consts, 16)
                    sp.dma_start(b2[:, :], io["b2"]).then_inc(consts, 16)
                    sp.dma_start(b1[:, :, :], io["b1"].rearrange("e (m p) -> p e m", p=P),
                                 allow_slow_non_contiguous=True).then_inc(consts, 16)
                    sp.dma_start(w_raw[:, :, :, :].rearrange("c e m i -> c e (m i)"),
                                 io["W1"].rearrange("e c i -> c e i")).then_inc(consts, 16)
                    for e in range(E1):
                        sp.dma_start(wd[:, e, :, :], io["W2"][e].rearrange("(m p) c -> p m c", p=P)).then_inc(consts, 16)
                c = Counts(sp)

                def load(n, u):
                    sp.wait_ge(xi_next, c.next(xi_next))
                    sp.dma_start(xi[:, u, :, :], xm_d[n].rearrange("(k p) c -> p k c", p=P)).then_inc(xi_in[u], 16)

                def store(n):
                    sp.wait_ge(y_ready, c.next(y_ready))
                    sp.dma_start(out[n].rearrange("(k p) c -> p k c", p=P), X[:, n, :, :]).then_inc(stored, 16)

                if swiglu:
                    with sp.Fori(0, NB // 2, 1) as i:
                        for u in range(2):
                            load(i * 2 + u, u)
                        c.settle()
                else:
                    with sp.Fori(0, NB, 1) as i:
                        store(i)
                        c.settle()
                    sp.wait_ge(stored, NB * 16)

            @block.vector
            def _(dve):
                c = Counts(dve)
                link = lambda ins: chain(dve, c, done, ins)
                link(dve.memset(euler[:, :, :], math.e))
                link(dve.memset(minus1[:, :, :], -1.0))
                for e in range(R):
                    last = dve.memset(desc[:, e:e + 1], float(R - e))
                link(last)
                if swiglu:
                    link(dve.memset(phalf[:, :], 0.5))
                    link(dve.memset(f32(wrh[:, R:8]), 0.0))
                    link(dve.memset(f32(wrl[:, R:8]), 0.0))
                dve.wait_ge(consts, (9 if swiglu else 5 + E1) * 16)
                if swiglu:
                    link(dve.tensor_scalar(wr[:, :], wr[:, :], w2[:, :], None, ALU.mult))
                    link(dve.tensor_scalar(w_raw[:, :, :, :].rearrange("p e a i -> p (e a i)"),
                                           w_raw[:, :, :, :].rearrange("p e a i -> p (e a i)"),
                                           w2[:, :], None, ALU.mult))
                link(split(dve, c, done, wr[:, :], wrh[:, 0:R], wrl[:, 0:R]))
                link(split(dve, c, done, w_raw[:, :, :, :], wh[:, :, :, :], wl[:, :, :, :]))
                dve.sem_inc(weights_ready, 1)
                if swiglu:
                    dve.sem_inc(xi_next, 2)
                dve.sem_inc(o_free, 2)
                dve.sem_inc(b_free, 1)
                dve.sem_inc(xs_free, 1)
                c.settle()

                def mean_square(n, u):
                    dve.wait_ge(xi_in[u], c.next(xi_in[u], 16))
                    link(block_stats(dve, c, done, xi[:, u, :, :], st, mv2))
                    link(dve.tensor_tensor(ms[:, :], mv2[:, :, 0], mv2[:, :, 0], ALU.mult))
                    dve.tensor_tensor(ms[:, :], ms[:, :], mv2[:, :, 1], ALU.add).then_inc(ms_ready, 1)

                def over_rms(n, u):
                    dve.wait_ge(rms_ready, c.next(rms_ready))
                    link(dve.tensor_scalar(ms[:, :], rms[:, :], EPS, None, ALU.add))
                    link(dve.reciprocal(ms[:, :], ms[:, :]))
                    for b in range(BLK):
                        last = dve.tensor_scalar(xs[:, b, :], xi[:, u, b, :], ms[:, b:b + 1], None, ALU.mult)
                    link(last)
                    dve.sem_inc(xs_ready, 1)
                    dve.sem_inc(xi_next, 1)

                def low_x(u):
                    dve.wait_ge(th_ready, c.next(th_ready))
                    link(dve.tensor_tensor(xtl[:, u, :], ps[:, TB, :], f32(xth[:, u, :]), ALU.subtract))
                    dve.sem_inc(x_ready, 1)
                    dve.sem_inc(xs_free, 1)

                def each(ap):
                    return ap.unsqueeze(2).broadcast_to([P, BLK, R])

                def logits():
                    dve.wait_ge(l_ready, c.next(l_ready))
                    l = ps[:, LB, 0:8 * BLK].rearrange("p (b e) -> p b e", b=BLK)[:, :, 0:R]
                    rbb = rb[:, :].unsqueeze(1).broadcast_to([P, BLK, R])
                    if swiglu:
                        link(dve.tensor_tensor(lg[:, :, :], l, rbb, ALU.add))
                        dve.tensor_scalar(lg[:, :, :], lg[:, :, :], -1.0, None, ALU.mult).then_inc(lg_ready, 1)
                    else:
                        link(dve.tensor_tensor(lg[:, :, :], l, rbb, ALU.add))
                        link(dve.tensor_reduce(m1[:, :], lg[:, :, :], axis=AX.X, op=ALU.max))
                        dve.tensor_tensor(lg[:, :, :], lg[:, :, :], each(m1[:, :]),
                                          ALU.subtract).then_inc(lg_ready, 1)

                def gate(u):
                    dve.wait_ge(pr_ready, c.next(pr_ready))
                    descb = desc[:, :].unsqueeze(1).broadcast_to([P, BLK, R])

                    def best(p, m, sel):
                        link(dve.tensor_reduce(m[:, :], p[:, :, :], axis=AX.X, op=ALU.max))
                        link(dve.tensor_tensor(eq[:, :, :], p[:, :, :], each(m[:, :]), ALU.is_equal))
                        link(dve.tensor_tensor(eq[:, :, :], eq[:, :, :], descb, ALU.mult))
                        link(dve.tensor_reduce(den[:, :], eq[:, :, :], axis=AX.X, op=ALU.max))
                        link(dve.tensor_tensor(sel[:, :, :], descb, each(den[:, :]), ALU.is_equal))

                    best(pr, m1, sel1)
                    link(dve.scalar_tensor_tensor(ex[:, :, :], sel1[:, :, :], -2.0, pr[:, :, :], ALU.mult, ALU.add))
                    best(ex, m2, sel2)
                    link(dve.tensor_tensor(m1[:, :], m1[:, :], m2[:, :], ALU.add))
                    if not swiglu:
                        link(dve.tensor_reduce(m2[:, :], pr[:, :, :], axis=AX.X, op=ALU.add))
                        link(dve.scalar_tensor_tensor(m1[:, :], m2[:, :], 1e-8, m1[:, :], ALU.mult, ALU.add))
                    link(dve.reciprocal(m1[:, :], m1[:, :]))
                    link(dve.tensor_tensor(sel1[:, :, :], sel1[:, :, :], sel2[:, :, :], ALU.add))
                    link(dve.tensor_tensor(sel1[:, :, :], sel1[:, :, :], pr[:, :, :], ALU.mult))
                    link(dve.tensor_tensor(wts[:, u, :, :], sel1[:, :, :], each(m1[:, :]), ALU.mult))
                    dve.sem_inc(wts_ready, 1)

                def add_expert(n, u, e):
                    dve.wait_ge(o_ready, c.next(o_ready))
                    o = ps[:, OB + e % 2, :].rearrange("p (b c) -> p b c", b=BLK)
                    if e < FIRST:
                        link(dve.tensor_tensor(acc[:, u, :, :], o, X[:, n, :, :], ALU.add))
                        dve.sem_inc(o_free, 1)
                        return
                    for b in range(BLK):
                        last = dve.scalar_tensor_tensor(acc[:, u, b, :], o[:, b, :],
                                                        wts[:, u, b, e - FIRST:e - FIRST + 1],
                                                        acc[:, u, b, :], ALU.mult, ALU.add)
                    link(last)
                    dve.sem_inc(o_free, 1)

                def begin(n, u):
                    dve.wait_ge(b_ready, c.next(b_ready))
                    link(dve.tensor_tensor(acc[:, u, :, :], ps[:, TB, :].rearrange("p (b c) -> p b c", b=BLK),
                                           X[:, n, :, :], ALU.add))
                    dve.sem_inc(b_free, 1)

                def finish_stats(u):
                    block_stats(dve, c, done, acc[:, u, :, :], st, mv).then_inc(mv_ready, 1)

                def finish(n, u):
                    dve.wait_ge(rstd_ready, c.next(rstd_ready))
                    for b in range(BLK):
                        last = dve.tensor_scalar(X[:, n, b, :], acc[:, u, b, :], mv[:, b, 0:1],
                                                 rstd[:, b:b + 1], ALU.subtract, ALU.mult)
                    link(last)
                    dve.sem_inc(y_ready, 1)

                def tile(n, u, first, more):
                    for e in range(EXP):
                        if swiglu:
                            dve.wait_ge(s_ready, c.next(s_ready))
                            dve.tensor_tensor(hid[:, e % 2, :], sg[:, e % 2, :], ps[:, FB + 2 * (e % 2) + 1, :],
                                              ALU.mult).then_inc(hid_ready, 1)
                        if e > 0:
                            add_expert(n, u, e - 1)
                        elif not first:
                            add_expert(n - 1, 1 - u, EXP - 1)
                        if e == 0 and not swiglu:
                            begin(n, u)
                        if e == 0 and not first:
                            finish_stats(1 - u)
                        if e == 1 and not first:
                            finish(n - 1, 1 - u)
                        if more:
                            if e == 2 and swiglu:
                                mean_square(n + 1, 1 - u)
                            if e == 3 and swiglu:
                                over_rms(n + 1, 1 - u)
                            if e == 4:
                                low_x(1 - u)
                            if e == 5:
                                logits()
                            if e == 6:
                                gate(1 - u)

                if swiglu:
                    mean_square(0, 0)
                    over_rms(0, 0)
                low_x(0)
                logits()
                gate(0)
                walk(dve, c, tile)
                add_expert(NB - 1, (NB - 1) % 2, EXP - 1)
                finish_stats((NB - 1) % 2)
                finish(NB - 1, (NB - 1) % 2)

            @block.gpsimd
            def _(pool):
                c = Counts(pool)

                def source(n):
                    pool.wait_ge(xs_free, c.next(xs_free))
                    pool.tensor_copy(xs[:, :, :], X[:, n, :, :]).then_inc(xs_ready, 1)

                def root():
                    pool.wait_ge(ms_ready, c.next(ms_ready))
                    pool.tensor_tensor(rms[:, :], ms[:, :], phalf[:, :], ALU.pow).then_inc(rms_ready, 1)

                def power():
                    pool.wait_ge(lg_ready, c.next(lg_ready))
                    if swiglu:
                        chain(pool, c, pdone, pool.tensor_tensor(pr[:, :, :], euler[:, :, :], lg[:, :, :], ALU.pow))
                        chain(pool, c, pdone, pool.tensor_scalar(pr[:, :, :], pr[:, :, :], 1.0, 1.0, ALU.add, ALU.mult))
                        pool.tensor_tensor(pr[:, :, :], pr[:, :, :], minus1[:, :, :], ALU.pow).then_inc(pr_ready, 1)
                    else:
                        pool.tensor_tensor(pr[:, :, :], euler[:, :, :], lg[:, :, :], ALU.pow).then_inc(pr_ready, 1)

                def tile(n, u, first, more):
                    if not first:
                        pool.wait_ge(mv_ready, c.next(mv_ready))
                        pool_rstd(pool, c, pdone, mv, var, mhalf, rstd).then_inc(rstd_ready, 1)
                    if more:
                        if swiglu:
                            root()
                        else:
                            source(n + 1)
                        power()

                if swiglu:
                    root()
                else:
                    source(0)
                power()
                walk(pool, c, tile)
                pool.wait_ge(mv_ready, c.next(mv_ready))
                pool_rstd(pool, c, pdone, mv, var, mhalf, rstd).then_inc(rstd_ready, 1)

            @block.scalar
            def _(act):
                c = Counts(act)
                act.preload_act_table(ACT.Silu if swiglu else ACT.Gelu_apprx_tanh)

                def high_x(u):
                    act.wait_ge(t_ready, c.next(t_ready))
                    act.activation(xth[:, u, :], ps[:, TB, :], ACT.Copy).then_inc(th_ready, 1)

                def turned_weights():
                    act.wait_ge(wtt_ready, c.next(wtt_ready))
                    act.activation(wt[:, :], ps[0:EXP, LB, :], ACT.Copy).then_inc(wt_ready, 1)

                def tile(n, u, first, more):
                    for e in range(EXP):
                        if more and e == 4:
                            high_x(1 - u)
                        if more and e == 7 and not swiglu:
                            turned_weights()
                        for m in range(HB):
                            r = e * HB + m
                            act.wait_ge(f_ready, c.next(f_ready))
                            if swiglu:
                                act.activation(sg[:, r % 2, :], ps[:, FB + 2 * (r % 2), :],
                                               ACT.Silu).then_inc(s_ready, 1)
                            else:
                                act.activation(hid[:, r % 2, :], ps[:, FB + r % 4, :], ACT.Gelu_apprx_tanh,
                                               bias=b1[:, e, m:m + 1]).then_inc(hid_ready, 1)

                high_x(0)
                if not swiglu:
                    turned_weights()
                walk(act, c, tile)

            @block.tensor
            def _(pe):
                c = Counts(pe)
                pe.wait_ge(weights_ready, 1)

                def three(o, hi, lo, u):
                    pe.matmul(o, hi, xth[:, u, :], start=True, stop=False)
                    pe.matmul(o, lo, xth[:, u, :], start=False, stop=False)
                    return pe.matmul(o, hi, xtl[:, u, :], start=False, stop=True)

                def transpose_x():
                    pe.wait_ge(xs_ready, c.next(xs_ready))
                    if not swiglu:
                        pe.wait_ge(b_free, c.next(b_free))
                    for b in range(BLK):
                        last = pe.transpose(ps[:, TB, b * P:(b + 1) * P], xs[:, b, :], ident[:, :])
                    last.then_inc(t_ready, 1)

                def logits(u):
                    pe.wait_ge(x_ready, c.next(x_ready))
                    for b in range(BLK):
                        o, tok = ps[:, LB, 8 * b:8 * b + 8], slice(b * P, (b + 1) * P)
                        pe.matmul(o, xth[:, u, tok], wrh[:, :], start=True, stop=False)
                        pe.matmul(o, xth[:, u, tok], wrl[:, :], start=False, stop=False)
                        last = pe.matmul(o, xtl[:, u, tok], wrh[:, :], start=False, stop=True)
                    last.then_inc(l_ready, 1)

                def turn_weights(u):
                    pe.wait_ge(wts_ready, c.next(wts_ready))
                    for b in range(BLK):
                        last = pe.transpose(ps[0:EXP, LB, b * P:(b + 1) * P], wts[:, u, b, :], ident[:, :])
                    last.then_inc(wtt_ready, 1)

                def second_bias():
                    pe.wait_ge(wt_ready, c.next(wt_ready))
                    for b in range(BLK):
                        last = pe.matmul(ps[:, TB, b * P:(b + 1) * P], wt[:, b * P:(b + 1) * P], b2[:, :],
                                         start=True, stop=True)
                    last.then_inc(b_ready, 1)

                def first_products(u, r):
                    e, m = divmod(r, HB)
                    if swiglu:
                        bank = FB + 2 * (r % 2)
                        three(ps[:, bank, :], wh[:, e, 0, :], wl[:, e, 0, :], u)
                        three(ps[:, bank + 1, :], wh[:, e, 1, :], wl[:, e, 1, :], u).then_inc(f_ready, 1)
                    else:
                        three(ps[:, FB + r % 4, :], wh[:, e, m, :], wl[:, e, m, :], u).then_inc(f_ready, 1)

                def second_products(r):
                    e, m = divmod(r, HB)
                    pe.wait_ge(hid_ready, c.next(hid_ready))
                    if m == 0:
                        pe.wait_ge(o_free, c.next(o_free))
                    for b in range(BLK):
                        last = pe.matmul(ps[:, OB + e % 2, b * P:(b + 1) * P], hid[:, r % 2, b * P:(b + 1) * P],
                                         wd[:, e, m, :], start=(m == 0 and b == 0), stop=(m == HB - 1),
                                         skip_group_check=True)
                    if m == HB - 1:
                        last.then_inc(o_ready, 1)

                def tile(n, u, first, more):
                    for r in range(UNITS):
                        e, m = divmod(r, HB)
                        first_products(u, r)
                        if r > 0:
                            second_products(r - 1)
                        elif not first:
                            second_products(UNITS - 1)
                        if m == 0 and more:
                            if e == 4:
                                transpose_x()
                            if e == 5:
                                logits(1 - u)
                            if e == 7 and not swiglu:
                                turn_weights(1 - u)
                        if m == HB - 1 and e == 7 and more and not swiglu:
                            second_bias()

                transpose_x()
                logits(0)
                if not swiglu:
                    turn_weights(0)
                    second_bias()
                walk(pe, c, tile)
                second_products(UNITS - 1)


def constants():
    m = (np.arange(P) < NS).astype(np.float32)
    half = np.stack([m, -m, 1 - m, m * np.float32(math.pi / 2), m - 1], 1)
    hh = HD // 2
    freq = 1.0 / 10000.0 ** (np.arange(0, hh, 2, dtype=np.float32) / hh)
    angle = np.arange(L, dtype=np.float32)[None, :] * freq[:, None].astype(np.float32)
    d = np.arange(P) // NG % HD
    cos = np.where(d[:, None] < hh, 1.0, np.cos(angle)[d % 2])
    sin = np.where(d[:, None] < hh, 0.0, np.sin(angle)[d % 2])
    r = np.arange(P) // LAT
    return {
        "c_t": np.tile(np.arange(L, dtype=np.float32), (P, 1)),
        "c_half": half.astype(np.float32),
        "c_rows": np.stack([-1.0 * (r == 2), -1.0 * (r == 1)], 1).astype(np.float32),
        "c_ident": np.eye(P, dtype=np.float32),
        "c_flip": np.eye(P, dtype=np.float32)[::-1].copy(),
        "c_mask": np.where(np.arange(P)[:, None] >= np.arange(P)[None, :], 0.0, NEG).astype(np.float32),
        "c_cos": cos.astype(np.float32),
        "c_sin": sin.astype(np.float32),
    }


def of_layer(a, name):
    return {k[len(name):]: v for k, v in a.items() if k.startswith(name)} | {
        k: v for k, v in a.items() if k.startswith("c_")}


def program(nc, a, out, upto=4):
    Names.used = set()
    kd = nc.dram_tensor("conv_kernel", (NC, KROW), F32, kind="Internal").ap()
    yd = nc.dram_tensor("conv_out", (NC, NB, L), F32, kind="Internal").ap()
    xm_d = nc.dram_tensor("mid_sum", (NB, L, C), F32, kind="Internal").ap()
    with ExitStack() as ctx:
        ps = ctx.enter_context(nc.psum_tensor("banks", [P, 8, 512], F32))
        X = ctx.enter_context(nc.sbuf_tensor("X", [P, NB, BLK, C], F32))
        ident = ctx.enter_context(nc.sbuf_tensor("ident", [P, P], F32))
        mhalf = ctx.enter_context(nc.sbuf_tensor("mhalf", [P, BLK], F32))
        io = of_layer(a, "L0_attn_")
        kernel_stage(nc, io, ps, kd)
        with ExitStack() as first:
            stats = first.enter_context(nc.sbuf_tensor("stats", [P, NB, BLK, 2], F32))
            with ExitStack() as conv:
                flip = conv.enter_context(nc.sbuf_tensor("flip", [P, P], F32))
                U = conv.enter_context(nc.sbuf_tensor("U", [P, NC, BLK, NB], F32))
                input_stage(nc, io, ps, X, stats, ident, flip, mhalf, U)
                convolution_stage(nc, io, ps, U, kd, yd)
            gate_stage(nc, io, ps, X, stats, ident, mhalf, yd)
        with ExitStack() as attn:
            if upto >= 1:
                Qb = attn.enter_context(nc.sbuf_tensor("Qb", [P, 2, HG, NG, L], F32R))
                Kb = attn.enter_context(nc.sbuf_tensor("Kb", [P, 2, NG, L], F32R))
                attention_stage(nc, of_layer(a, "L0_ffn_"), ps, X, ident, mhalf, Qb, Kb, KIND_LATENT, xm_d)
            if upto >= 2:
                experts_stage(nc, of_layer(a, "L0_ffn_"), ps, X, ident, mhalf, KIND_SWIGLU, xm_d)
                clear(nc)
            if upto >= 3:
                attention_stage(nc, of_layer(a, "L1_attn_"), ps, X, ident, mhalf, Qb, Kb, KIND_DIRECT)
        if upto >= 4:
            experts_stage(nc, of_layer(a, "L1_ffn_"), ps, X, ident, mhalf, KIND_GELU, out=out)
        else:
            store_stage(nc, X, out)


def store_stage(nc, X, out):
    with nc.semaphore("stored") as stored, nc.Block() as block:

        @block.sync
        def _(sp):
            for n in range(NB):
                sp.dma_start(out[n].rearrange("(k p) c -> p k c", p=P), X[:, n, :, :]).then_inc(stored, 16)
            sp.wait_ge(stored, NB * 16)


def kernel(**arrays):
    from concourse import bacc
    from concourse.bass_utils import run_bass_kernel_spmd

    arrays = {k: np.ascontiguousarray(v) for k, v in (arrays | constants()).items()}
    nc = bacc.Bacc("TRN2", target_bir_lowering=False, num_devices=1)
    a = {k: nc.dram_tensor(k, v.shape, mybir.dt.from_np(v.dtype), kind="ExternalInput").ap() for k, v in arrays.items()}
    out = nc.dram_tensor("out", (NB, L, C), F32, kind="ExternalOutput").ap()
    program(nc, a, out)
    nc.finalize()
    return run_bass_kernel_spmd(nc, [arrays], core_ids=[0]).results[0]["out"]
```

```python
from contextlib import ExitStack
import math

import numpy as np
import concourse.bass as bass
from concourse import mybir
from concourse.alu_op_type import AluOpType as ALU

F32 = mybir.dt.float32
F32R = mybir.dt.float32r
BF16 = mybir.dt.bfloat16
I32 = mybir.dt.int32
ACT = mybir.ActivationFunctionType
AX = mybir.AxisListType

P = 128
NB, L, C = 16, 512, 128
BLK = L // P
HID = 512
NS, NC = 64, 64
NH, HD = 16, 8
NG, HG = 4, 4
LAT = 32
E0, E1, H1 = 8, 8, 512
H1B = H1 // P
EPS = 1e-5
NEG = -1e30
KPAD = P - 1
KROW = KPAD + L + 1
MROW = 3 * 8 * HG


class Counts:

    def __init__(self, eng):
        self.eng, self.taken = eng, {}

    def next(self, sem, n=1):
        self.taken[sem] = self.taken.get(sem, 0) + n
        return self.taken[sem]

    def settle(self):
        for sem, n in self.taken.items():
            self.eng.sem_inc(sem, -n)
        self.taken = {}


class Names:

    used = set()

    def __init__(self, nc, ctx, stage):
        self.nc, self.ctx, self.stage = nc, ctx, stage

    def sems(self, text):
        made = [self.ctx.enter_context(self.nc.semaphore(f"{self.stage}_{n}")) for n in text.split()]
        Names.used.update(s.num for s in made)
        return made

    def sb(self, name, shape, dt=F32):
        return self.ctx.enter_context(self.nc.sbuf_tensor(f"{self.stage}_{name}", shape, dt))


def clear(nc):
    with nc.Block() as block:

        @block.sync
        def _(sp):
            while Names.used:
                lo = hi = min(Names.used)
                while hi in Names.used:
                    Names.used.discard(hi)
                    hi += 1
                sp.sem_clear(range(lo, hi))


def f32(ap):
    return ap.bitcast(F32)


def chain(eng, c, done, ins):
    ins.then_inc(done, 1)
    eng.wait_ge(done, c.next(done))


def rows(ap, n=P):
    return bass.AP(tensor=ap.tensor, offset=ap.offset, ap=[[0, n]] + [list(x) for x in ap.ap])


def column(ap):
    return ap.rearrange("(p a) -> p a", a=1)


def block_stats(dve, c, done, src, st, mv):
    for b in range(BLK):
        last = dve.bn_stats(st[:, b, :], src[:, b, :])
    chain(dve, c, done, last)
    for b in range(BLK):
        last = dve.bn_aggr(mv[:, b, :], st[:, b, :])
    return last


def pool_rstd(pool, c, done, mv, var, mhalf, out):
    chain(pool, c, done, pool.tensor_scalar(var[:, :], mv[:, :, 1], EPS, 1.0, ALU.add, ALU.mult))
    return pool.tensor_tensor(out[:, :], var[:, :], mhalf[:, :], ALU.pow)


def split(dve, c, done, x, hi, lo):
    chain(dve, c, done, dve.tensor_copy(hi, x))
    return dve.tensor_tensor(lo, x, f32(hi), ALU.subtract)



LOG2E = math.log2(math.e)
LN2_HI, LN2_LO = 0.693145751953125, math.log(2) - 0.693145751953125
MAGIC = 1.5 * 2.0 ** 23


def parts(x, bits, n):
    out = []
    for _ in range(n - 1):
        e = math.floor(math.log2(abs(x))) + 1 - bits
        p = math.trunc(x / 2.0 ** e) * 2.0 ** e
        out.append(p)
        x -= p
    return out + [x]


def exact_exp(dve, link, z, k, r, q, ki, out):
    link(dve.tensor_scalar(z, z, -87.0, 87.0, ALU.max, ALU.min))
    link(dve.tensor_scalar(k, z, LOG2E, MAGIC, ALU.mult, ALU.add))
    link(dve.tensor_scalar(k, k, -MAGIC, None, ALU.add))
    link(dve.scalar_tensor_tensor(r, k, -LN2_HI, z, ALU.mult, ALU.add))
    link(dve.scalar_tensor_tensor(r, k, -LN2_LO, r, ALU.mult, ALU.add))
    link(dve.tensor_scalar(q, r, 1.0 / math.factorial(8), None, ALU.mult))
    for d in range(7, 0, -1):
        link(dve.scalar_tensor_tensor(q, q, 1.0 / math.factorial(d), r, ALU.add, ALU.mult))
    link(dve.tensor_scalar(q, q, 1.0, None, ALU.add))
    link(dve.tensor_scalar(ki, k, 127.0, None, ALU.add))
    link(dve.tensor_scalar(ki, ki, 23, None, ALU.logical_shift_left))
    link(dve.tensor_tensor(out, q, ki.bitcast(F32), ALU.mult))


def kernel_stage(nc, io, ps, kd, Qb, Kb):
    with ExitStack() as ctx:
        N = Names(nc, ctx, "kern")
        z, k, r, q, ex = (N.sb(n, [P, 2]) for n in ("z", "k", "r", "q", "ex"))
        ki = N.sb("ki", [P, 2], I32)
        crt, cit, coef = (N.sb(n, [P, NC]) for n in ("crt", "cit", "coef"))
        t = N.sb("t", [P, L])
        half = N.sb("half", [P, 5])
        turn, ph, ph2, arg, decay = (N.sb(n, [P, L]) for n in ("turn", "ph", "ph2", "arg", "decay"))
        arg1, cs, w = N.sb("arg1", [P, 2]), N.sb("cs", [P, 2]), N.sb("w", [P, 16])
        kpad, dcol = N.sb("kpad", [NC, KROW]), N.sb("dcol", [NC, 1])
        loaded, done, args_ready, waves_ready, table_ready, k_ready, kpad_ready, stored = N.sems(
            "loaded done args_ready waves_ready table_ready k_ready kpad_ready stored")
        a_ready, decay_ready, ones_ready = N.sems("a_ready decay_ready ones_ready")
        with nc.Block() as block:

            @block.sync
            def _(sp):
                for lo in (0, NS):
                    sp.dma_start(z[lo:lo + NS, 0:1], column(io["LR"])).then_inc(loaded, 16)
                    sp.dma_start(z[lo:lo + NS, 1:2], column(io["LI"])).then_inc(loaded, 16)
                    sp.dma_start(crt[lo:lo + NS, :], io["CR"].rearrange("h n -> n h"),
                                 allow_slow_non_contiguous=True).then_inc(loaded, 16)
                    sp.dma_start(cit[lo:lo + NS, :], io["CI"].rearrange("h n -> n h"),
                                 allow_slow_non_contiguous=True).then_inc(loaded, 16)
                sp.dma_start(t[:, :], io["c_t"]).then_inc(loaded, 16)
                sp.dma_start(half[:, :], io["c_half"]).then_inc(loaded, 16)
                sp.dma_start(dcol[:, :], column(io["D"])).then_inc(loaded, 16)
                sp.wait_ge(kpad_ready, 1)
                sp.dma_start(kd, kpad[:, :]).then_inc(stored, 16)
                sp.wait_ge(stored, 16)

            @block.vector
            def _(dve):
                c = Counts(dve)
                link = lambda ins: chain(dve, c, done, ins)
                link(dve.memset(kpad[:, :], 0.0))
                dve.wait_ge(loaded, 11 * 16)
                exact_exp(dve, link, z[:, :], k[:, :], r[:, :], q[:, :], ki[:, :], ex[:, :])
                a, b = w[:, 0:1], ex[:, 1:2]
                dve.tensor_scalar(a, ex[:, 0:1], -1.0, None, ALU.mult).then_inc(a_ready, 1)
                link(dve.tensor_scalar(ph[:, :], t[:, :], b, None, ALU.mult))
                for unit, bits, n in ((2048 * 2 * math.pi, 8, 5), (2 * math.pi, 12, 3)):
                    link(dve.tensor_scalar(turn[:, :], ph[:, :], 1.0 / unit, MAGIC, ALU.mult, ALU.add))
                    link(dve.tensor_scalar(turn[:, :], turn[:, :], -MAGIC, None, ALU.add))
                    for p in parts(unit, bits, n):
                        link(dve.scalar_tensor_tensor(ph[:, :], turn[:, :], -p, ph[:, :], ALU.mult, ALU.add))
                link(dve.tensor_scalar(ph[:, :], ph[:, :], 3.1415925, -3.1415925, ALU.min, ALU.max))
                link(dve.tensor_scalar(ph2[:, :], ph[:, :], -1.0, None, ALU.mult))
                link(dve.tensor_tensor(ph2[:, :], ph2[:, :], ph[:, :], ALU.max))
                link(dve.tensor_scalar(arg1[:, 0:1], ph2[:, 1:2], -1.0, math.pi / 2, ALU.mult, ALU.add))
                link(dve.tensor_copy(arg1[:, 1:2], ph[:, 1:2]))
                link(dve.tensor_scalar(ph2[:, :], ph2[:, :], half[:, 1:2], half[:, 3:4], ALU.mult, ALU.add))
                dve.scalar_tensor_tensor(arg[:, :], ph[:, :], half[:, 2:3], ph2[:, :], ALU.mult,
                                         ALU.add).then_inc(args_ready, 1)
                dve.wait_ge(a_ready, 1)
                link(dve.tensor_copy(z[:, 0:1], a))
                exact_exp(dve, link, z[:, 0:1], k[:, 0:1], r[:, 0:1], q[:, 0:1], ki[:, 0:1], ex[:, 0:1])
                ea = ex[:, 0:1]
                er, ei, dd, u, wr, wi, p1, p2 = (w[:, n:n + 1] for n in range(1, 9))
                dve.wait_ge(waves_ready, 1)
                link(dve.tensor_tensor(er, ea, cs[:, 0:1], ALU.mult))
                link(dve.tensor_scalar(er, er, -1.0, None, ALU.add))
                link(dve.tensor_tensor(ei, ea, cs[:, 1:2], ALU.mult))
                link(dve.tensor_tensor(dd, a, a, ALU.mult))
                link(dve.scalar_tensor_tensor(dd, b, b, dd, ALU.mult, ALU.add))
                link(dve.reciprocal(dd, dd))
                link(dve.tensor_tensor(u, er, a, ALU.mult))
                link(dve.scalar_tensor_tensor(wr, ei, b, u, ALU.mult, ALU.add))
                link(dve.tensor_tensor(wr, wr, dd, ALU.mult))
                link(dve.tensor_tensor(u, er, b, ALU.mult))
                link(dve.scalar_tensor_tensor(wi, ei, a, u, ALU.mult, ALU.subtract))
                link(dve.tensor_tensor(wi, wi, dd, ALU.mult))
                link(dve.tensor_tensor(u, wi, half[:, 2:3], ALU.mult))
                link(dve.scalar_tensor_tensor(p1, wr, half[:, 0:1], u, ALU.mult, ALU.subtract))
                link(dve.tensor_tensor(u, wr, half[:, 2:3], ALU.mult))
                link(dve.scalar_tensor_tensor(p2, wi, half[:, 1:2], u, ALU.mult, ALU.subtract))
                link(dve.tensor_scalar(crt[:, :], crt[:, :], p1, None, ALU.mult))
                link(dve.scalar_tensor_tensor(coef[:, :], cit[:, :], p2, crt[:, :], ALU.mult, ALU.add))
                dve.wait_ge(decay_ready, 1)
                dve.tensor_tensor(arg[:, :], arg[:, :], decay[:, :], ALU.mult).then_inc(table_ready, 1)
                dve.wait_ge(k_ready, 1)
                link(dve.tensor_copy(kpad[:, KPAD:KPAD + L], ps[0:NC, 0, :]))
                dve.tensor_tensor(kpad[:, KPAD:KPAD + 1], kpad[:, KPAD:KPAD + 1], dcol[:, :],
                                  ALU.add).then_inc(kpad_ready, 1)

            @block.gpsimd
            def _(pool):
                pool.memset(f32(Kb[MROW:P, :, :, :].rearrange("p a g l -> p (a g l)")), 1.0).then_inc(ones_ready, 1)
                pool.wait_ge(ones_ready, 1)
                pool.memset(f32(Qb[:, :, :, :, :].rearrange("p a g h l -> p (a g h l)")), 0.0)

            @block.scalar
            def _(act):
                act.wait_ge(a_ready, 1)
                act.activation(decay[:, :], t[:, :], ACT.Exp, scale=w[:, 0:1]).then_inc(decay_ready, 1)
                act.wait_ge(args_ready, 1)
                act.activation(cs[:, :], arg1[:, :], ACT.Sin)
                act.activation(arg[:, :], arg[:, :], ACT.Sin).then_inc(waves_ready, 1)

            @block.tensor
            def _(pe):
                pe.wait_ge(table_ready, 1)
                pe.matmul(ps[0:NC, 0, :], coef[:, :], arg[:, :], start=True, stop=True).then_inc(k_ready, 1)


def walk_sequences(eng, c, body):
    body(0, 0, False, True, True)
    c.settle()
    with eng.Fori(0, (NB - 2) // 2, 1) as i:
        for v in range(2):
            body(i * 2 + (v + 1), (v + 1) % 2, True, True, True)
        c.settle()
    body(NB - 1, (NB - 1) % 2, True, True, False)
    body(NB, NB % 2, True, False, False)



def input_stage(nc, io, ps, X, stats, ident, flip, mhalf, U):
    with ExitStack() as ctx:
        N = Names(nc, ctx, "inp")
        w1, b1, wd, bcast = N.sb("w1", [P, 1]), N.sb("b1", [P, 1]), N.sb("wd", [P, NC]), N.sb("bcast", [P, P])
        wdh, wdl = N.sb("wdh", [P, NC], F32R), N.sb("wdl", [P, NC], F32R)
        bd, w2, b2 = N.sb("bd", [P, NC]), N.sb("w2", [P, NC]), N.sb("b2", [P, NC])
        st, mv = N.sb("st", [P, 2, BLK, 6]), N.sb("mv", [P, 2, BLK, 2])
        st2, mv2, rstd2 = N.sb("st2", [P, BLK, 6]), N.sb("mv2", [P, BLK, 2]), N.sb("rstd2", [P, BLK])
        var, var2 = N.sb("var", [P, BLK]), N.sb("var2", [P, BLK])
        xh = N.sb("xh", [P, 2, BLK, C])
        xth, xtl = N.sb("xth", [P, 2, L], F32R), N.sb("xtl", [P, 2, L], F32R)
        d = N.sb("d", [P, 2, BLK, NC])
        consts, done, pdone, w_ready, wb_ready, bd_ready, bd_free = N.sems(
            "consts done pdone w_ready wb_ready bd_ready bd_free")
        x_in = N.sems("x_in0 x_in1")
        x_next, mv_ready, rstd_ready, xh_ready, t_ready, th_ready, t_split, d_ready, d_free = N.sems(
            "x_next mv_ready rstd_ready xh_ready t_ready th_ready t_split d_ready d_free")
        mv2_ready, rstd2_ready, t_free = N.sems("mv2_ready rstd2_ready t_free")
        with nc.Block() as block:

            @block.sync
            def _(sp):
                sp.dma_start(ident[:, :], io["c_ident"]).then_inc(consts, 16)
                sp.dma_start(flip[:, :], io["c_flip"]).then_inc(consts, 16)
                sp.dma_start(w1[:, :], column(io["n1_w"])).then_inc(consts, 16)
                sp.dma_start(b1[:, :], column(io["n1_b"])).then_inc(consts, 16)
                sp.dma_start(wd[:, :], io["Wdin"]).then_inc(consts, 16)
                sp.dma_start(w2[:, :], rows(io["n2_w"])).then_inc(consts, 16)
                sp.dma_start(b2[:, :], rows(io["n2_b"])).then_inc(consts, 16)
                c = Counts(sp)
                with sp.Fori(0, NB // 2, 1) as i:
                    for u in range(2):
                        sp.wait_ge(x_next, c.next(x_next))
                        sp.dma_start(X[:, i * 2 + u, :, :],
                                     io["idx"][i * 2 + u].rearrange("(k p) c -> p k c", p=P)).then_inc(x_in[u], 16)
                    c.settle()

            @block.vector
            def _(dve):
                c = Counts(dve)
                dve.sem_inc(x_next, 2)
                dve.wait_ge(consts, 7 * 16)
                chain(dve, c, done, dve.memset(mhalf[:, :], -0.5))
                chain(dve, c, done, dve.tensor_copy(bcast[:, :], b1[:, :].broadcast_to([P, P])))
                dve.drain().then_inc(wb_ready, 1)
                dve.wait_ge(bd_ready, 1)
                chain(dve, c, done, dve.tensor_copy(bd[:, :], ps[:, 0, 0:NC]))
                chain(dve, c, done, dve.tensor_scalar(wd[:, :], wd[:, :], w1[:, :], None, ALU.mult))
                chain(dve, c, done, split(dve, c, done, wd[:, :], wdh[:, :], wdl[:, :]))
                dve.sem_inc(bd_free, 1)
                c.settle()

                def means(n, u):
                    dve.wait_ge(x_in[u], c.next(x_in[u], 16))
                    dve.sem_inc(x_next, 1)
                    block_stats(dve, c, done, X[:, n, :, :], st[:, u, :, :], mv[:, u, :, :]).then_inc(mv_ready, 1)

                def normalise(n, u):
                    dve.wait_ge(rstd_ready, c.next(rstd_ready))
                    chain(dve, c, done, dve.tensor_copy(stats[:, n, :, 0], mv[:, u, :, 0]))
                    for b in range(BLK):
                        last = dve.tensor_scalar(xh[:, u, b, :], X[:, n, b, :], stats[:, n, b, 0:1],
                                                 stats[:, n, b, 1:2], ALU.subtract, ALU.mult)
                    last.then_inc(xh_ready, 1)

                def low_x(u):
                    dve.wait_ge(th_ready, c.next(th_ready))
                    dve.tensor_tensor(xtl[:, u, :], ps[:, 1 + u, :], f32(xth[:, u, :]),
                                      ALU.subtract).then_inc(t_split, 1)

                def second_means(u):
                    dve.wait_ge(d_ready, c.next(d_ready))
                    chain(dve, c, done, dve.tensor_tensor(
                        d[:, u, :, :], ps[:, 3 + u, 0:BLK * NC].rearrange("p (b h) -> p b h", b=BLK),
                        bd[:, :].unsqueeze(1).broadcast_to([P, BLK, NC]), ALU.add))
                    dve.sem_inc(d_free, 1)
                    block_stats(dve, c, done, d[:, u, :, :], st2, mv2).then_inc(mv2_ready, 1)

                def second_norm(n, u):
                    dve.wait_ge(rstd2_ready, c.next(rstd2_ready))
                    for b in range(BLK):
                        last = dve.tensor_scalar(d[:, u, b, :], d[:, u, b, :], mv2[:, b, 0:1],
                                                 rstd2[:, b:b + 1], ALU.subtract, ALU.mult)
                    chain(dve, c, done, last)
                    chain(dve, c, done, dve.tensor_tensor(
                        d[:, u, :, :], d[:, u, :, :], w2[:, :].unsqueeze(1).broadcast_to([P, BLK, NC]), ALU.mult))
                    chain(dve, c, done, dve.tensor_tensor(
                        U[:, :, :, n].rearrange("p h b -> p b h"), d[:, u, :, :],
                        b2[:, :].unsqueeze(1).broadcast_to([P, BLK, NC]), ALU.add))

                def turn(n, u, before, now, after):
                    if now:
                        normalise(n, u)
                    if after:
                        means(n + 1, 1 - u)
                    if before:
                        second_means(1 - u)
                    if now:
                        low_x(u)
                    if before:
                        second_norm(n - 1, 1 - u)

                means(0, 0)
                walk_sequences(dve, c, turn)

            @block.gpsimd
            def _(pool):
                c = Counts(pool)

                def first_rstd(n, u):
                    pool.wait_ge(mv_ready, c.next(mv_ready))
                    pool_rstd(pool, c, pdone, mv[:, u, :, :], var, mhalf, stats[:, n, :, 1]).then_inc(rstd_ready, 1)

                def turn(n, u, before, now, after):
                    if after:
                        first_rstd(n + 1, 1 - u)
                    if before:
                        pool.wait_ge(mv2_ready, c.next(mv2_ready))
                        pool_rstd(pool, c, pdone, mv2, var2, mhalf, rstd2).then_inc(rstd2_ready, 1)

                first_rstd(0, 0)
                walk_sequences(pool, c, turn)

            @block.scalar
            def _(act):
                c = Counts(act)
                act.preload_act_table(ACT.Exp)
                with act.Fori(0, NB // 2, 1) as i:
                    for u in range(2):
                        act.wait_ge(t_ready, c.next(t_ready))
                        act.activation(xth[:, u, :], ps[:, 1 + u, :], ACT.Copy).then_inc(th_ready, 1)
                    c.settle()

            @block.tensor
            def _(pe):
                c = Counts(pe)
                pe.wait_ge(wb_ready, 1)
                pe.matmul(ps[:, 0, 0:NC], bcast[:, :], wd[:, :], start=True, stop=True).then_inc(bd_ready, 1)
                pe.wait_ge(bd_free, 1)
                pe.sem_inc(d_free, 2)
                with pe.Fori(0, NB // 2, 1) as i:
                    for u in range(2):
                        pe.wait_ge(xh_ready, c.next(xh_ready))
                        for b in range(BLK):
                            last = pe.transpose(ps[:, 1 + u, b * P:(b + 1) * P], xh[:, u, b, :], flip[:, :])
                        last.then_inc(t_ready, 1)
                        pe.wait_ge(t_split, c.next(t_split))
                        pe.wait_ge(d_free, c.next(d_free))
                        for b in range(BLK):
                            o = ps[:, 3 + u, b * NC:(b + 1) * NC]
                            tok = slice(b * P, (b + 1) * P)
                            pe.matmul(o, xth[:, u, tok], wdh[:, :], start=True, stop=False)
                            pe.matmul(o, xth[:, u, tok], wdl[:, :], start=False, stop=False)
                            last = pe.matmul(o, xtl[:, u, tok], wdh[:, :], start=False, stop=True)
                        last.then_inc(d_ready, 1)
                    c.settle()


def convolution_stage(nc, io, ps, U, kd, yd):
    with ExitStack() as ctx:
        N = Names(nc, ctx, "conv")
        CH = 4
        tz = N.sb("tz", [P, 2, CH, L])
        uw = N.sb("uw", [P, 2, CH, BLK, 32])
        y = N.sb("y", [P, 2, L])
        t_in, y_out = N.sems("t_in0 t_in1"), N.sems("y_out0 y_out1")
        t_next, u_ready, c_ready, c_free, y_ready, zeroed, u_next = N.sems(
            "t_next u_ready c_ready c_free y_ready zeroed u_next")
        with nc.Block() as block:

            @block.sync
            def _(sp):
                c = Counts(sp)
                with sp.Fori(0, NC // CH // 2, 1) as i:
                    for u in range(2):
                        sp.wait_ge(t_next, c.next(t_next))
                        g = i * 2 + u
                        src = kd.rearrange("(g a) x -> g a x", a=CH)[g]
                        src = bass.AP(tensor=kd.tensor, offset=src.offset,
                                      ap=[[1, P], [KROW, CH], [1, L]])
                        sp.dma_start(tz[:, u, :, :], src).then_inc(t_in[u], 16)
                    c.settle()

            @block.gpsimd
            def _(pool):
                c = Counts(pool)
                pool.memset(uw[:, :, :, :, :].rearrange("p a b c d -> p (a b c d)"), 0.0).then_inc(zeroed, 1)
                pool.wait_ge(zeroed, 1)
                with pool.Fori(0, NC // CH // 2, 1) as i:
                    for u in range(2):
                        pool.wait_ge(u_next, c.next(u_next))
                        pool.tensor_copy(uw[:, u, :, :, 0:NB],
                                         U[:, :, :, :].rearrange("p (g a) b n -> p g a b n", a=CH)[:, i * 2 + u]
                                         ).then_inc(u_ready, 1)
                    c.settle()

            @block.tensor
            def _(pe):
                c = Counts(pe)
                pe.sem_inc(t_next, 2)
                pe.sem_inc(u_next, 2)
                with pe.Fori(0, NC // CH // 2, 1) as i:
                    for u in range(2):
                        pe.wait_ge(t_in[u], c.next(t_in[u], 16))
                        pe.wait_ge(u_ready, c.next(u_ready))
                        pe.wait_ge(c_free, c.next(c_free))
                        for b in range(BLK):
                            for a in range(CH):
                                last = pe.matmul(ps[32 * a:32 * a + 32, u, b * P:L], uw[:, u, a, b, :],
                                                 tz[:, u, a, 0:L - b * P], start=(b == 0), stop=(b == BLK - 1),
                                                 skip_group_check=True)
                        last.then_inc(c_ready, 1)
                    c.settle()

            @block.vector
            def _(dve):
                c = Counts(dve)
                dve.sem_inc(c_free, 2)
                with dve.Fori(0, NC // CH // 2, 1) as i:
                    for u in range(2):
                        dve.wait_ge(c_ready, c.next(c_ready))
                        dve.sem_inc(t_next, 1)
                        dve.sem_inc(u_next, 1)
                        dve.wait_ge(y_out[u], c.next(y_out[u], 64))
                        dve.tensor_copy(y[:, u, :], ps[:, u, :]).then_inc(y_ready, 1)
                        dve.drain().then_inc(c_free, 1)
                    c.settle()
                dve.wait_ge(y_out[0], 64)
                dve.wait_ge(y_out[1], 64)

            @block.scalar
            def _(act):
                c = Counts(act)
                act.sem_inc(y_out[0], 64)
                act.sem_inc(y_out[1], 64)
                with act.Fori(0, NC // CH // 2, 1) as i:
                    for u in range(2):
                        act.wait_ge(y_ready, c.next(y_ready))
                        for a in range(CH):
                            dst = yd.rearrange("(g a) n l -> g a n l", a=CH)[i * 2 + u]
                            act.dma_start(dst[a], y[32 * a:32 * a + NB, u, :]).then_inc(y_out[u], 16)
                    c.settle()


def gate_stage(nc, io, ps, X, stats, ident, mhalf, yd):
    with ExitStack() as ctx:
        N = Names(nc, ctx, "gate")
        HB = HID // P
        w1, b1 = N.sb("w1", [P, 1]), N.sb("b1", [P, 1])
        wx = N.sb("wx", [P, HID])
        wxh, wxl = N.sb("wxh", [P, HID], F32R), N.sb("wxl", [P, HID], F32R)
        bx = N.sb("bx", [P, HB])
        wg = N.sb("wg", [P, HID])
        wgh, wgl = N.sb("wgh", [P, HID], F32R), N.sb("wgl", [P, HID], F32R)
        wo = N.sb("wo", [P, HB, C])
        bo = N.sb("bo", [P, C])
        sel = N.sb("sel", [P, 5])
        yt, ya, ys = N.sb("yt", [P, 2, L]), N.sb("ya", [P, L], F32R), N.sb("ys", [P, 2, L], F32R)
        xh = N.sb("xh", [P, 2, BLK, C])
        xth, xtl = N.sb("xth", [P, 2, L], F32R), N.sb("xtl", [P, 2, L], F32R)
        xg = N.sb("xg", [P, 2, L])
        gx = N.sb("gx", [P, 2, HB, L])
        r = N.sb("r", [P, 2, BLK, C])
        st, mv, var, rstd = (N.sb(n, [P, BLK, m]) for n, m in (("st", 6), ("mv", 2), ("var", 1), ("rstd", 1)))
        var, rstd = var[:, :, 0], rstd[:, :, 0]
        consts, done, pdone, bx_ready, w_done = N.sems("consts done pdone bx_ready w_done")
        y_in = N.sems("y_in0 y_in1")
        (y_next, ya_ready, ya_free, ys_ready, xh_ready, t_ready, th_ready, t_split, xg_ready, xgs_ready,
         g_ready, gx_ready, xg_free, o_ready, o_free, mv_ready, rstd_ready) = N.sems(
            "y_next ya_ready ya_free ys_ready xh_ready t_ready th_ready t_split xg_ready xgs_ready "
            "g_ready gx_ready xg_free o_ready o_free mv_ready rstd_ready")
        TB, XB, GB, OB = 0, 1, 3, 5
        with nc.Block() as block:

            @block.sync
            def _(sp):
                sp.dma_start(w1[:, :], column(io["n1_w"])).then_inc(consts, 16)
                sp.dma_start(b1[:, :], column(io["n1_b"])).then_inc(consts, 16)
                sp.dma_start(wx[:, :], io["Wxg"]).then_inc(consts, 16)
                for lo in (0, NC):
                    sp.dma_start(wg[lo:lo + NC, :], io["Wgate"]).then_inc(consts, 16)
                sp.dma_start(wo[:, :, :], io["Wout"].rearrange("(m p) c -> p m c", p=P)).then_inc(consts, 16)
                sp.dma_start(bo[:, :], rows(io["bout"])).then_inc(consts, 16)
                sp.dma_start(sel[:, :], io["c_half"]).then_inc(consts, 16)
                c = Counts(sp)
                with sp.Fori(0, NB // 2, 1) as i:
                    for u in range(2):
                        sp.wait_ge(y_next, c.next(y_next))
                        for lo in (0, NC):
                            sp.dma_start(yt[lo:lo + NC, u, :], yd[:, i * 2 + u, :]).then_inc(y_in[u], 16)
                    c.settle()

            @block.vector
            def _(dve):
                c = Counts(dve)
                dve.sem_inc(y_next, 2)
                dve.wait_ge(consts, 8 * 16)
                dve.wait_ge(bx_ready, 1)
                chain(dve, c, done, dve.tensor_copy(bx[:, :], ps[:, 0, 0:HB]))
                chain(dve, c, done, dve.tensor_scalar(wx[:, :], wx[:, :], w1[:, :], None, ALU.mult))
                chain(dve, c, done, split(dve, c, done, wx[:, :], wxh[:, :], wxl[:, :]))
                chain(dve, c, done, split(dve, c, done, wg[:, :], wgh[:, :], wgl[:, :]))
                chain(dve, c, done, dve.tensor_scalar(wgl[:, :], f32(wgl[:, :]), sel[:, 0:1], None, ALU.mult))
                dve.sem_inc(w_done, 1)
                c.settle()

                def inputs(n, u):
                    for b in range(BLK):
                        last = dve.tensor_scalar(xh[:, u, b, :], X[:, n, b, :], stats[:, n, b, 0:1],
                                                 stats[:, n, b, 1:2], ALU.subtract, ALU.mult)
                    last.then_inc(xh_ready, 1)
                    dve.wait_ge(ya_ready, c.next(ya_ready))
                    chain(dve, c, done, dve.scalar_tensor_tensor(ys[:, u, :], f32(ya[:, :]), sel[:, 4:5],
                                                                 yt[:, u, :], ALU.mult, ALU.add))
                    dve.sem_inc(ys_ready, 1)
                    dve.sem_inc(ya_free, 1)
                    dve.sem_inc(y_next, 1)

                def low_x(u):
                    dve.wait_ge(th_ready, c.next(th_ready))
                    dve.tensor_tensor(xtl[:, u, :], ps[:, TB, :], f32(xth[:, u, :]),
                                      ALU.subtract).then_inc(t_split, 1)

                def product(u, m):
                    dve.wait_ge(g_ready, c.next(g_ready))
                    dve.wait_ge(xgs_ready, c.next(xgs_ready))
                    dve.tensor_tensor(gx[:, u, m, :], ps[:, GB + m % 2, :], xg[:, m % 2, :],
                                      ALU.mult).then_inc(gx_ready, 1)

                def residual(n, u):
                    dve.wait_ge(o_ready, c.next(o_ready))
                    chain(dve, c, done, dve.scalar_tensor_tensor(
                        r[:, u, :, :].rearrange("p b c -> p (b c)"),
                        X[:, n, :, :].rearrange("p b c -> p (b c)"), 2.0, ps[:, OB + u, :], ALU.mult, ALU.add))
                    dve.sem_inc(o_free, 1)
                    chain(dve, c, done, dve.tensor_tensor(
                        r[:, u, :, :], r[:, u, :, :], bo[:, :].unsqueeze(1).broadcast_to([P, BLK, C]), ALU.add))
                    block_stats(dve, c, done, r[:, u, :, :], st, mv).then_inc(mv_ready, 1)

                def finish(n, u):
                    dve.wait_ge(rstd_ready, c.next(rstd_ready))
                    for b in range(BLK):
                        last = dve.tensor_scalar(X[:, n, b, :], r[:, u, b, :], mv[:, b, 0:1],
                                                 rstd[:, b:b + 1], ALU.subtract, ALU.mult)
                    chain(dve, c, done, last)

                def turn(n, u, before, now, after):
                    if now:
                        product(u, 0)
                    if after:
                        inputs(n + 1, 1 - u)
                    if now:
                        product(u, 1)
                    if before:
                        residual(n - 1, 1 - u)
                    if after:
                        low_x(1 - u)
                    if now:
                        product(u, 2)
                    if before:
                        finish(n - 1, 1 - u)
                    if now:
                        product(u, 3)

                inputs(0, 0)
                low_x(0)
                walk_sequences(dve, c, turn)

            @block.gpsimd
            def _(pool):
                c = Counts(pool)
                with pool.Fori(0, NB, 1):
                    pool.wait_ge(mv_ready, c.next(mv_ready))
                    pool_rstd(pool, c, pdone, mv, var, mhalf, rstd).then_inc(rstd_ready, 1)
                    c.settle()

            @block.scalar
            def _(act):
                c = Counts(act)
                act.preload_act_table(ACT.Exp)
                act.wait_ge(w_done, 1)
                act.sem_inc(ya_free, 1)

                def high_y(u):
                    act.wait_ge(y_in[u], c.next(y_in[u], 32))
                    act.wait_ge(ya_free, c.next(ya_free))
                    act.activation(ya[:, :], yt[:, u, :], ACT.Copy).then_inc(ya_ready, 1)

                def high_x(u):
                    act.wait_ge(t_ready, c.next(t_ready))
                    act.activation(xth[:, u, :], ps[:, TB, :], ACT.Copy).then_inc(th_ready, 1)

                def biased(m):
                    act.wait_ge(xg_ready, c.next(xg_ready))
                    act.activation(xg[:, m % 2, :], ps[:, XB + m % 2, :], ACT.Identity,
                                   bias=bx[:, m:m + 1]).then_inc(xgs_ready, 1)

                def turn(n, u, before, now, after):
                    if now:
                        biased(0)
                    if after:
                        high_y(1 - u)
                    if now:
                        biased(1)
                    if after:
                        high_x(1 - u)
                    if now:
                        biased(2)
                        biased(3)

                high_y(0)
                high_x(0)
                walk_sequences(act, c, turn)

            @block.tensor
            def _(pe):
                c = Counts(pe)
                pe.wait_ge(consts, 8 * 16)
                for m in range(HB):
                    last = pe.matmul(ps[:, 0, m:m + 1], wx[:, m * P:(m + 1) * P], b1[:, :], start=True, stop=True)
                last.then_inc(bx_ready, 1)
                pe.wait_ge(w_done, 1)
                pe.sem_inc(o_free, 2)
                pe.sem_inc(gx_ready, 2)

                def transpose_x(u):
                    pe.wait_ge(xh_ready, c.next(xh_ready))
                    for b in range(BLK):
                        last = pe.transpose(ps[:, TB, b * P:(b + 1) * P], xh[:, u, b, :], ident[:, :])
                    last.then_inc(t_ready, 1)

                def hidden(u, m):
                    pe.wait_ge(gx_ready, c.next(gx_ready))
                    w = slice(m * P, (m + 1) * P)
                    o = ps[:, XB + m % 2, :]
                    pe.matmul(o, wxh[:, w], xth[:, u, :], start=True, stop=False)
                    pe.matmul(o, wxl[:, w], xth[:, u, :], start=False, stop=False)
                    pe.matmul(o, wxh[:, w], xtl[:, u, :], start=False, stop=True).then_inc(xg_ready, 1)
                    o = ps[:, GB + m % 2, :]
                    pe.matmul(o, wgh[:, w], ys[:, u, :], start=True, stop=False)
                    pe.matmul(o, wgl[:, w], ys[:, u, :], start=False, stop=True).then_inc(g_ready, 1)

                def output(u):
                    pe.wait_ge(o_free, c.next(o_free))
                    for b in range(BLK):
                        for m in range(HB):
                            last = pe.matmul(ps[:, OB + u, b * P:(b + 1) * P], gx[:, u, m, b * P:(b + 1) * P],
                                             wo[:, m, :], start=(m == 0), stop=(m == HB - 1))
                    last.then_inc(o_ready, 1)

                def turn(n, u, before, now, after):
                    if now:
                        pe.wait_ge(ys_ready, c.next(ys_ready))
                        pe.wait_ge(t_split, c.next(t_split))
                        hidden(u, 0)
                        hidden(u, 1)
                    else:
                        pe.wait_ge(gx_ready, c.next(gx_ready, 2))
                    if before:
                        output(1 - u)
                    if after:
                        transpose_x(1 - u)
                    if now:
                        hidden(u, 2)
                        hidden(u, 3)

                transpose_x(0)
                walk_sequences(pe, c, turn)



KIND_LATENT, KIND_DIRECT = range(2)
UNITS1 = [(0, 0, 2), (0, 2, 2)] + [(1, h, 2) for h in (0, 2)] + [(j, h, 1) for j in (2, 3) for h in range(HG)]
UNITS2 = [u for a in (0, 2) for u in ([(a, 0, 0, L)], [(a, 3, 0, P), (a, 1, P, L - P)],
                                      [(a + 1, 0, 0, L)], [(a + 1, 3, 0, P), (a + 1, 1, P, L - P)],
                                      [(a, 2, 0, 2 * P), (a + 1, 2, 2 * P, 2 * P)])]
WHERE = {(h, kb): (n, at, w) for n, unit in enumerate(UNITS2) for h, kb, at, w in unit}
DIAGONALS = [sorted(at for _, _, at, _ in unit) for unit in UNITS2]


def spread(ap):
    return ap.rearrange("p (g hh d) -> p hh d g", g=NG, hh=HG)


def compact(ap):
    return ap.rearrange("p (hh d g) -> p hh d g", hh=HG, d=HD)


def attention_stage(nc, io, ps, X, ident, mhalf, Qb, Kb, kind, xm_d=None):
    name = "mla" if kind == KIND_LATENT else "mha"
    latent = kind == KIND_LATENT
    with ExitStack() as ctx:
        N = Names(nc, ctx, name)
        mask, identb = N.sb("mask", [P, 2, P], BF16), N.sb("identb", [P, P], BF16)
        xs = N.sb("xs", [P, BLK, C])
        xth, xtl = N.sb("xth", [P, L], F32R), N.sb("xtl", [P, L], F32R)
        qh, ql, kh, kl = (N.sb(n, [P, L], F32R) for n in ("qh", "ql", "kh", "kl"))
        tmp = N.sb("tmp", [P, L])
        tmp2 = xs[:, :, :].rearrange("p b c -> p (b c)")
        V = N.sb("V", [P, 2, BLK, NH, HD + 1])
        prob = N.sb("prob", [P, 2, len(UNITS2), L])
        nm = N.sb("nm", [P, 2, HG, BLK])
        mh, ml = N.sb("mh", [HG * BLK, 2, P], F32R), N.sb("ml", [HG * BLK, 2, P], F32R)
        osb = N.sb("osb", [P, L])
        rec = N.sb("rec", [P, BLK, HG])
        ctxs = N.sb("ctxs", [P, 2, BLK, C])
        ctxt = tmp
        st, mv = N.sb("st", [P, BLK, 6]), N.sb("mv", [P, BLK, 2])
        var, rstd = N.sb("var", [P, BLK]), N.sb("rstd", [P, BLK])
        xm = N.sb("xm", [P, BLK, C])
        wo = N.sb("wo", [P, C])
        raw, raw2, maskf = prob[:, 0, 0, 0:3 * P], prob[:, 0, 1, 0:3 * P], prob[:, 0, 4, 0:P]
        if latent:
            w1 = N.sb("w1", [P, 1])
            sel = N.sb("sel", [P, 2])
            phalf = N.sb("phalf", [P, BLK])
            lath, latl = N.sb("lath", [P, 2, 96], F32R), N.sb("latl", [P, 2, 96], F32R)
            up = N.sb("up", [96, 4, P], F32R)
            upa = qh[0:96, :].rearrange("p (a m) -> p a m", a=4)
            upw = prob[0:96, 0, 2, :].rearrange("p (a m) -> p a m", a=4)
            kxw = prob[:, 0, 3, 0:2 * P].rearrange("p (a m) -> p a m", a=2)
            kxh, kxl = N.sb("kxh", [P, 2, P], F32R), N.sb("kxl", [P, 2, P], F32R)
            cosr, sinr = N.sb("cosr", [P, L]), N.sb("sinr", [P, L])
            lata = (qh[0:96, :], kh[0:96, :])
            lats = N.sb("lats", [96, 2, L], F32R)
        else:
            wph, wpl = N.sb("wph", [P, 3, P], F32R), N.sb("wpl", [P, 3, P], F32R)
            bcol = N.sb("bcol", [P, 2])
            vb, bd = N.sb("vb", [P, P]), N.sb("bd", [P, P])
        consts, done, pdone, adone, weights_ready = N.sems("consts done pdone adone weights_ready")
        (ma_free, mb_free, xs_ready, t_ready, th_ready, lat_ready, lata_ready, k_ready, k_full, k_high, k_split,
         q_ready, q_full, q_high, q_split, v_ready, k_rows, q_rows, kb_used) = N.sems(
            "ma_free mb_free xs_ready t_ready th_ready lat_ready lata_ready k_ready k_full k_high k_split "
            "q_ready q_full q_high q_split v_ready k_rows q_rows kb_used")
        (s1_ready, s1_free, nm_ready, mt_ready, mh_ready, ml_ready, s2_ready, e_ready, p_ready, o_ready,
         osb_ready, ot_ready, ct_ready, ctxt_ready, y_ready, mv_ready, rstd_ready, xm_ready) = N.sems(
            "s1_ready s1_free nm_ready mt_ready mh_ready ml_ready s2_ready e_ready p_ready o_ready "
            "osb_ready ot_ready ct_ready ctxt_ready y_ready mv_ready rstd_ready xm_ready")
        m_rows, (xm_out,) = N.sems("m_rows0 m_rows1"), N.sems("xm_out")
        S1, S2, OB, MA, MB = (0, 1, 7), 2, 4, 5, 6

        def has_probs(turn, g):
            return turn == "inner" or (turn == "first" and g >= 2) or (turn == "last" and g < 2)

        def has_values(turn, g):
            return turn == "inner" or (turn == "first" and g == 3) or (turn == "last" and g < 3)

        def has_maxima(turn, g):
            return turn == "inner" or (turn == "first" and g >= 1) or (turn == "last" and g == 0)

        def has_output(turn):
            return turn != "first"

        MAXIMA = dict(pe=1, act=2, dve=3)
        OUTPUT = dict(act=0, pe=2, dve=3)
        NEXT_X = dict(pe=4, act=5, dve=6)
        LATENTS = dict(pe=8, act=9, dve=10)
        KEYS_QUERIES = dict(pe=5, turn=6, act=7, dve=9)
        VALUES = dict(pe=10, act=11, dve=11)
        NEXT_XS = dict(stats=1, dve=5)
        DENSE = dict(pe=4, act=5, pe2=6, dve=7, stats=8, norm=10)

        def walk(eng, c, body):
            body(0, 0, "first", True, True)
            c.settle()
            with eng.Fori(0, (NB - 4) // 2, 1) as i:
                for v in range(2):
                    body(i * 2 + (v + 1), (v + 1) % 2, "inner", True, True)
                c.settle()
            for n in range(NB - 3, NB):
                body(n, n % 2, "inner", n + 2 < NB, n + 1 < NB)
            body(NB, NB % 2, "last", False, False)

        with nc.Block() as block:

            @block.sync
            def _(sp):
                sp.dma_start(maskf, io["c_mask"]).then_inc(consts, 16)
                if latent:
                    sp.dma_start(w1[:, :], column(io["w_ln1"])).then_inc(consts, 16)
                    sp.dma_start(sel[:, :], io["c_rows"]).then_inc(consts, 16)
                    sp.dma_start(raw[:, 0:LAT], io["W_kvd"]).then_inc(consts, 16)
                    sp.dma_start(raw[:, LAT:2 * LAT], io["W_qd"]).then_inc(consts, 16)
                    sp.dma_start(raw[:, 2 * LAT:2 * LAT + 64], io["W_ropek"]).then_inc(consts, 16)
                    for name, lo, w in (("W_qu", 0, 64), ("W_ropeq", 64, 64), ("W_ku", 128, 64), ("W_vu", 192, P)):
                        sp.dma_start(raw2[0:3 * LAT, lo:lo + w],
                                     bass.AP(tensor=io[name].tensor, offset=io[name].offset,
                                             ap=[[0, 3], [w, LAT], [1, w]])).then_inc(consts, 16)
                    sp.dma_start(cosr[:, :], io["c_cos"]).then_inc(consts, 16)
                    sp.dma_start(sinr[:, :], io["c_sin"]).then_inc(consts, 16)
                    sp.dma_start(wo[:, :], io["W_o"]).then_inc(consts, 16)
                else:
                    sp.dma_start(raw, io["w_qkv"]).then_inc(consts, 16)
                    for at, lo in ((0, 0), (1, 2 * P)):
                        for hh in range(HG):
                            src = bass.AP(tensor=io["b_qkv"].tensor, offset=io["b_qkv"].offset + lo + hh * HD,
                                          ap=[[1, HD], [HG * HD, NG], [1, 1]])
                            sp.dma_start(bcol[32 * hh:32 * hh + 32, at:at + 1], src,
                                         allow_slow_non_contiguous=True).then_inc(consts, 16)
                    sp.dma_start(vb[:, :], rows(io["b_qkv"][P:2 * P])).then_inc(consts, 16)
                    sp.dma_start(bd[:, :], rows(io["b_dense"])).then_inc(consts, 16)
                    sp.dma_start(wo[:, :], io["w_dense"]).then_inc(consts, 16)
                c = Counts(sp)

                def keys(u):
                    sp.wait_ge(k_split, c.next(k_split))
                    for at in (0, 2):
                        sp.dma_start(f32(Kb[32 * at:32 * at + 32, u, :, :]), f32(kh[:, :])).then_inc(k_rows, 16)
                    sp.dma_start(f32(Kb[32:64, u, :, :]), f32(kl[:, :])).then_inc(k_rows, 16)

                def queries(u):
                    sp.wait_ge(q_split, c.next(q_split))
                    for hh in range(HG):
                        for at in (0, 1):
                            lo = 32 * at + HD * hh
                            sp.dma_start(f32(Qb[lo:lo + HD, u, :, hh, :]), f32(qh[32 * hh:32 * hh + 32, :])).then_inc(q_rows, 16)
                    for hh in range(HG):
                        lo = 64 + HD * hh
                        sp.dma_start(f32(Qb[lo:lo + HD, u, :, hh, :]), f32(ql[32 * hh:32 * hh + 32, :])).then_inc(q_rows, 16)

                def slots(n, u, turn, prep, proj):
                    for g in range(NG):
                        if has_maxima(turn, g):
                            par, grp, to = (g + 1) % 2, (g + 3) % NG, u if g else 1 - u
                            sp.wait_ge(ml_ready, c.next(ml_ready))
                            for row, m in ((MROW, mh), (MROW + 1, ml)):
                                sp.dma_start(f32(Qb[row:row + 1, to, grp, :, :]),
                                             f32(m[:, par, :])).then_inc(m_rows[par], 16)
                        if turn != "last":
                            if g == 1 and proj:
                                sp.wait_ge(kb_used, c.next(kb_used))
                                keys(1 - u)
                            if g == 2 and proj:
                                queries(1 - u)
                        if g == 3 and turn != "first" and latent:
                            sp.wait_ge(xm_ready, c.next(xm_ready))
                            sp.dma_start(xm_d[n - 1].rearrange("(k p) c -> p k c", p=P),
                                         xm[:, :, :]).then_inc(xm_out, 16)

                keys(0)
                queries(0)
                walk(sp, c, slots)

            @block.vector
            def _(dve):
                c = Counts(dve)
                link = lambda ins: chain(dve, c, done, ins)
                link(dve.memset(V[:, :, :, :, HD:HD + 1], 1.0))
                link(dve.memset(ps[:, OB, :], 0.0))
                if latent:
                    link(dve.memset(mhalf[:, :], -0.5))
                    link(dve.memset(phalf[:, :], 0.5))
                    link(dve.memset(upw[:, :, :], 0.0))
                    link(dve.memset(kxw[:, :, :], 0.0))
                nconst = (6 + 4 + 3) if latent else (1 + 1 + 8 + 3)
                dve.wait_ge(consts, nconst * 16)
                link(dve.tensor_copy(mask[:, :, :], maskf.unsqueeze(1).broadcast_to([P, 2, P])))
                link(dve.tensor_copy(identb[:, :], ident[:, :]))
                if latent:
                    link(dve.tensor_scalar(raw[:, 0:P], raw[:, 0:P], w1[:, :], None, ALU.mult))
                    for s in range(3):
                        link(dve.tensor_copy(raw[:, P + LAT * s:P + LAT * (s + 1)], raw[:, LAT:2 * LAT]))
                        link(dve.tensor_copy(raw[:, P + 96 + LAT * s:P + 96 + LAT * (s + 1)], raw[:, 0:LAT]))
                    link(split(dve, c, done, raw[:, P:P + 192].rearrange("p (a m) -> p a m", a=2),
                               lath[:, :, :], latl[:, :, :]))
                    half = HD // 2

                    def turned(dst, src):
                        link(dve.tensor_scalar(dst[:, :, half:half + 2, :], src[:, :, 2:4, :], -1.0, None, ALU.mult))
                        link(dve.tensor_copy(dst[:, :, half + 2:HD, :], src[:, :, 0:2, :]))

                    link(dve.tensor_copy(compact(upw[:, 0, :])[:, :, 0:half, :], spread(raw2[0:96, 0:64])))
                    link(dve.tensor_copy(compact(upw[:, 0, :])[:, :, half:HD, :], spread(raw2[0:96, 64:128])))
                    link(dve.tensor_copy(compact(upw[:, 2, :])[:, :, 0:half, :], spread(raw2[0:96, 128:192])))
                    link(dve.tensor_copy(compact(kxw[:, 0, :])[:, :, half:HD, :],
                                         spread(raw[:, 2 * LAT:2 * LAT + 64])))
                    turned(compact(upw[:, 1, :]), spread(raw2[0:96, 64:128]))
                    turned(compact(kxw[:, 1, :]), spread(raw[:, 2 * LAT:2 * LAT + 64]))
                    link(dve.tensor_copy(upw[:, 3, :], raw2[0:96, 192:320]))
                    link(split(dve, c, done, kxw[:, :, :], kxh[:, :, :], kxl[:, :, :]))
                    link(dve.tensor_copy(upa[:, :, :], upw[:, :, :]))
                    link(dve.scalar_tensor_tensor(up[:, :, :].rearrange("p a m -> p (a m)"),
                                                  f32(upa[:, :, :]).rearrange("p a m -> p (a m)"), sel[0:96, 1:2],
                                                  upw[:, :, :].rearrange("p a m -> p (a m)"), ALU.mult, ALU.add))
                else:
                    for a, at in ((0, 0), (2, 2 * P)):
                        for hh in range(HG):
                            link(dve.tensor_copy(compact(raw2[:, a * P:(a + 1) * P])[:, hh],
                                                 spread(raw[:, at:at + P])[:, hh]))
                    link(dve.tensor_copy(raw2[:, P:2 * P], raw[:, P:2 * P]))
                    link(split(dve, c, done, raw2.rearrange("p (a m) -> p a m", a=3), wph[:, :, :], wpl[:, :, :]))
                dve.sem_inc(weights_ready, 1)
                dve.sem_inc(ma_free, 1)
                dve.sem_inc(mb_free, 1)
                dve.sem_inc(s1_free, 3)
                if latent:
                    dve.sem_inc(xm_out, 16)
                c.settle()

                def prepare_stats(n):
                    link(block_stats(dve, c, done, X[:, n, :, :], st, mv))
                    link(dve.tensor_tensor(var[:, :], mv[:, :, 0], mv[:, :, 0], ALU.mult))
                    dve.tensor_tensor(var[:, :], var[:, :], mv[:, :, 1], ALU.add).then_inc(mv_ready, 1)

                def prepare(n):
                    if not latent:
                        link(dve.tensor_copy(xs[:, :, :], X[:, n, :, :]))
                        dve.sem_inc(xs_ready, 1)
                        return
                    dve.wait_ge(rstd_ready, c.next(rstd_ready))
                    link(dve.tensor_scalar(var[:, :], rstd[:, :], EPS, None, ALU.add))
                    link(dve.reciprocal(var[:, :], var[:, :]))
                    for b in range(BLK):
                        last = dve.tensor_scalar(xs[:, b, :], X[:, n, b, :], var[:, b:b + 1], None, ALU.mult)
                    link(last)
                    dve.sem_inc(xs_ready, 1)

                def low_x():
                    dve.wait_ge(th_ready, c.next(th_ready))
                    dve.tensor_tensor(xtl[:, :], ps[:, MA, :], f32(xth[:, :]), ALU.subtract).then_inc(ma_free, 1)

                def low_latents():
                    for a, bank, free in ((1, MA, ma_free), (0, MB, mb_free)):
                        dve.wait_ge(lata_ready, c.next(lata_ready))
                        dve.scalar_tensor_tensor(lats[:, a, :], f32(lata[a]), sel[0:96, 0:1],
                                                 ps[0:96, bank, :], ALU.mult, ALU.add).then_inc(free, 1)

                def turn_rows(ready, full):
                    dve.wait_ge(ready, c.next(ready))
                    link(dve.tensor_tensor(tmp2, ps[:, MB, :], sinr[:, :], ALU.mult))
                    dve.sem_inc(mb_free, 1)
                    link(dve.tensor_tensor(tmp[:, :], ps[:, MA, :], cosr[:, :], ALU.mult))
                    dve.sem_inc(ma_free, 1)
                    dve.tensor_tensor(tmp[:, :], tmp[:, :], tmp2, ALU.add).then_inc(full, 1)

                def low_part(high, hi, lo, split_done):
                    dve.wait_ge(high, c.next(high))
                    link(dve.tensor_tensor(lo[:, :], tmp[:, :], f32(hi[:, :]), ALU.subtract))
                    dve.sem_inc(split_done, 1)
                    if not latent:
                        dve.sem_inc(ma_free, 1)

                def values(u):
                    if latent:
                        return
                    dve.wait_ge(v_ready, c.next(v_ready))
                    for b in range(BLK):
                        last = dve.tensor_tensor(
                            V[:, u, b, :, 0:HD], ps[:, MA, b * P:(b + 1) * P].rearrange("p (h d) -> p h d", h=NH),
                            vb[:, :].rearrange("p (h d) -> p h d", h=NH), ALU.add)
                    last.then_inc(ma_free, 1)

                def normalise(par, g):
                    dve.wait_ge(ot_ready, c.next(ot_ready))
                    o = ps[:, MB, :].rearrange("p (j h m) -> p j h m", j=BLK, h=HG)
                    link(dve.reciprocal(rec[:, :, :], o[:, :, :, HD]))
                    dve.tensor_tensor(
                        ctxs[:, par, :, g * 32:g * 32 + 32].rearrange("p j (h d) -> p j h d", h=HG),
                        o[:, :, :, 0:HD], rec[:, :, :].unsqueeze(3).broadcast_to([P, BLK, HG, HD]),
                        ALU.mult).then_inc(mb_free, 1)

                def finish(n):
                    x = X[:, n, :, :]
                    if latent:
                        dve.wait_ge(xm_out, c.next(xm_out, 16))
                    dve.wait_ge(y_ready, c.next(y_ready))
                    y = ps[:, MB, :].rearrange("p (b c) -> p b c", b=BLK)
                    link(dve.tensor_tensor(xm[:, :, :], x, y, ALU.add))
                    dve.sem_inc(mb_free, 1)
                    if latent:
                        dve.sem_inc(xm_ready, 1)
                        link(dve.tensor_tensor(x, x, xm[:, :, :], ALU.add))
                    else:
                        link(dve.tensor_tensor(xm[:, :, :], xm[:, :, :],
                                               bd[:, :].unsqueeze(1).broadcast_to([P, BLK, C]), ALU.add))

                def finish_stats():
                    block_stats(dve, c, done, xm[:, :, :], st, mv).then_inc(mv_ready, 1)

                def finish_norm(n):
                    dve.wait_ge(rstd_ready, c.next(rstd_ready))
                    for b in range(BLK):
                        last = dve.tensor_scalar(X[:, n, b, :], xm[:, b, :], mv[:, b, 0:1],
                                                 rstd[:, b:b + 1], ALU.subtract, ALU.mult)
                    link(last)

                def low_maxima(par):
                    dve.wait_ge(mh_ready, c.next(mh_ready))
                    link(dve.tensor_tensor(ml[:, par, :], ps[0:HG * BLK, MA, 0:P], f32(mh[:, par, :]), ALU.subtract))
                    dve.sem_inc(ml_ready, 1)
                    dve.sem_inc(ma_free, 1)

                def slots(n, u, turn, prep, proj):
                    for g in range(NG):
                        for k, (j, h, heads) in enumerate(UNITS1):
                            if turn != "last":
                                dve.wait_ge(s1_ready, c.next(s1_ready))
                                w = P * (j + 1)
                                dve.tensor_reduce(nm[:, g % 2, h:h + heads, j],
                                                  ps[:, S1[k % 3], 0:heads * w].rearrange("p (h k) -> p h k", h=heads),
                                                  axis=AX.X, op=ALU.max, negate=True).then_inc(s1_free, 1)
                            if k == MAXIMA["dve"] and has_maxima(turn, g):
                                low_maxima((g + 1) % 2)
                            if k == OUTPUT["dve"] and has_output(turn):
                                normalise(1 - u, g)
                            if proj and g == 0 and k == NEXT_X["dve"]:
                                low_x()
                            if proj and latent and g == 0 and k == LATENTS["dve"]:
                                low_latents()
                            if proj and g in (1, 2):
                                if latent and k == KEYS_QUERIES["turn"]:
                                    turn_rows(*((k_ready, k_full), (q_ready, q_full))[g - 1])
                                if k == KEYS_QUERIES["dve"]:
                                    low_part(*((k_high, kh, kl, k_split), (q_high, qh, ql, q_split))[g - 1])
                            if proj and g == 2 and k == VALUES["dve"]:
                                values(1 - u)
                            if g == 3 and turn != "first":
                                if k == DENSE["dve"]:
                                    finish(n - 1)
                                if k == DENSE["stats"] and not latent:
                                    finish_stats()
                                if k == DENSE["norm"] and not latent:
                                    finish_norm(n - 1)
                            if g == 3 and prep and k == NEXT_XS["dve"]:
                                prepare(n + 2)
                            if g == 3 and prep and latent and k == NEXT_XS["stats"]:
                                prepare_stats(n + 2)
                        if turn != "last":
                            dve.drain().then_inc(nm_ready, 1)

                def first_projections(n, u):
                    if latent:
                        prepare_stats(n)
                    prepare(n)
                    low_x()
                    if latent:
                        low_latents()
                        turn_rows(k_ready, k_full)
                    low_part(k_high, kh, kl, k_split)
                    if latent:
                        turn_rows(q_ready, q_full)
                    low_part(q_high, qh, ql, q_split)
                    values(u)

                first_projections(0, 0)
                if latent:
                    prepare_stats(1)
                prepare(1)
                walk(dve, c, slots)
                if latent:
                    dve.wait_ge(xm_out, c.next(xm_out, 16))

            @block.gpsimd
            def _(pool):
                c = Counts(pool)
                def rms_or_rstd():
                    pool.wait_ge(mv_ready, c.next(mv_ready))
                    if latent:
                        pool.tensor_tensor(rstd[:, :], var[:, :], phalf[:, :], ALU.pow).then_inc(rstd_ready, 1)
                    else:
                        pool_rstd(pool, c, pdone, mv, var, mhalf, rstd).then_inc(rstd_ready, 1)

                def slots(n, u, turn, prep, proj):
                    for g in range(NG):
                        if has_probs(turn, g):
                            for k, ats in enumerate(DIAGONALS):
                                pool.wait_ge(e_ready, c.next(e_ready))
                                if len(ats) == 1:
                                    part, pattern = prob[:, g % 2, k, 0:P], [[1, P]]
                                else:
                                    step = ats[1]
                                    part = prob[:, g % 2, k, 0:2 * step].rearrange("p (a w) -> p a w", a=2)[:, :, 0:P]
                                    pattern = [[0, 2], [1, P]]
                                pool.affine_select(out=part, in_=part, compare_op=ALU.is_ge, fill=0.0, base=0,
                                                   pattern=pattern, channel_multiplier=-1).then_inc(p_ready, 1)
                                if g == 3 and prep and latent and k == NEXT_XS["stats"]:
                                    rms_or_rstd()
                                if g == 3 and turn == "inner" and not latent and k == DENSE["stats"]:
                                    rms_or_rstd()
                        if g == 3 and turn == "last" and not latent:
                            rms_or_rstd()

                if latent:
                    rms_or_rstd()
                    rms_or_rstd()
                walk(pool, c, slots)

            @block.scalar
            def _(act):
                c = Counts(act)
                act.preload_act_table(ACT.Exp)

                def high_x():
                    act.wait_ge(t_ready, c.next(t_ready))
                    act.activation(xth[:, :], ps[:, MA, :], ACT.Copy).then_inc(th_ready, 1)

                def high_part(ready, full, high, hi, col):
                    if latent:
                        act.wait_ge(full, c.next(full))
                    else:
                        act.wait_ge(ready, c.next(ready))
                        chain(act, c, adone, act.activation(tmp[:, :], ps[:, MA, :], ACT.Identity,
                                                            bias=bcol[:, col:col + 1]))
                    act.activation(hi[:, :], tmp[:, :], ACT.Copy).then_inc(high, 1)

                def latents():
                    for a, bank in ((1, MA), (0, MB)):
                        act.wait_ge(lat_ready, c.next(lat_ready))
                        act.activation(lata[a], ps[0:96, bank, :], ACT.Copy).then_inc(lata_ready, 1)

                def values(u):
                    act.wait_ge(v_ready, c.next(v_ready))
                    act.activation(V[:, u, :, :, 0:HD],
                                   ps[:, MA, :].rearrange("p (b h d) -> p b h d", b=BLK, h=NH),
                                   ACT.Copy).then_inc(ma_free, 1)

                def slots(n, u, turn, prep, proj):
                    for g in range(NG):
                        for k in range(len(UNITS1)):
                            if has_probs(turn, g) and k < len(UNITS2):
                                act.wait_ge(s2_ready, c.next(s2_ready))
                                act.activation(prob[:, g % 2, k, :], ps[:, S2 + k % 2, :], ACT.Exp,
                                               scale=HD ** -0.5).then_inc(e_ready, 1)
                            if k == OUTPUT["act"] and has_output(turn):
                                act.wait_ge(o_ready, c.next(o_ready))
                                act.activation(osb[:, :], ps[:, OB, :], ACT.Copy).then_inc(osb_ready, 1)
                            if k == MAXIMA["act"] and has_maxima(turn, g):
                                act.wait_ge(mt_ready, c.next(mt_ready))
                                act.activation(mh[:, (g + 1) % 2, :], ps[0:HG * BLK, MA, 0:P], ACT.Copy).then_inc(mh_ready, 1)
                            if proj and g == 0 and k == NEXT_X["act"]:
                                high_x()
                            if proj and latent and g == 0 and k == LATENTS["act"]:
                                latents()
                            if proj and g in (1, 2) and k == KEYS_QUERIES["act"]:
                                high_part(*((k_ready, k_full, k_high, kh, 0), (q_ready, q_full, q_high, qh, 1))[g - 1])
                            if proj and latent and g == 2 and k == VALUES["act"]:
                                values(1 - u)
                            if g == 3 and turn != "first" and k == DENSE["act"]:
                                act.wait_ge(ct_ready, c.next(ct_ready))
                                act.activation(ctxt[:, :], ps[:, MA, :], ACT.Copy).then_inc(ctxt_ready, 1)

                high_x()
                if latent:
                    latents()
                high_part(k_ready, k_full, k_high, kh, 0)
                high_part(q_ready, q_full, q_high, qh, 1)
                if latent:
                    values(0)
                walk(act, c, slots)

            @block.tensor
            def _(pe):
                c = Counts(pe)
                pe.wait_ge(weights_ready, 1)
                pe.sem_inc(p_ready, 2)

                def three(o, hi, lo, a, first=True, last=True):
                    pe.matmul(o, hi, xth[:, :], start=first, stop=False)
                    pe.matmul(o, lo, xth[:, :], start=False, stop=False)
                    return pe.matmul(o, hi, xtl[:, :], start=False, stop=last)

                def transpose_x():
                    pe.wait_ge(xs_ready, c.next(xs_ready))
                    pe.wait_ge(ma_free, c.next(ma_free))
                    for b in range(BLK):
                        last = pe.transpose(ps[:, MA, b * P:(b + 1) * P], xs[:, b, :], ident[:, :])
                    last.then_inc(t_ready, 1)

                def project(g, u):
                    if g == 0 and latent:
                        for a, bank, free in ((1, MA, ma_free), (0, MB, mb_free)):
                            pe.wait_ge(free, c.next(free))
                            three(ps[0:96, bank, :], lath[:, a, :], latl[:, a, :], a).then_inc(lat_ready, 1)
                    if g == 1:
                        pe.wait_ge(ma_free, c.next(ma_free))
                        if latent:
                            pe.wait_ge(mb_free, c.next(mb_free))
                            pe.matmul(ps[:, MA, :], up[:, 2, :], lats[:, 1, :], start=True, stop=False)
                            three(ps[:, MA, :], kxh[:, 0, :], kxl[:, 0, :], 0, first=False)
                            three(ps[:, MB, :], kxh[:, 1, :], kxl[:, 1, :], 0).then_inc(k_ready, 1)
                        else:
                            three(ps[:, MA, :], wph[:, 0, :], wpl[:, 0, :], 0).then_inc(k_ready, 1)
                    if g == 2:
                        pe.wait_ge(ma_free, c.next(ma_free))
                        if latent:
                            pe.wait_ge(mb_free, c.next(mb_free))
                            pe.matmul(ps[:, MA, :], up[:, 0, :], lats[:, 0, :], start=True, stop=True)
                            pe.matmul(ps[:, MB, :], up[:, 1, :], lats[:, 0, :], start=True,
                                      stop=True).then_inc(q_ready, 1)
                        else:
                            three(ps[:, MA, :], wph[:, 2, :], wpl[:, 2, :], 0).then_inc(q_ready, 1)
                    if g == 3:
                        pe.wait_ge(ma_free, c.next(ma_free))
                        for b in range(BLK):
                            tok = slice(b * P, (b + 1) * P)
                            o = ps[:, MA, tok]
                            if latent:
                                last = pe.matmul(o, lats[:, 1, tok], up[:, 3, :], start=True, stop=True)
                            else:
                                pe.matmul(o, xth[:, tok], wph[:, 1, :], start=True, stop=False)
                                pe.matmul(o, xth[:, tok], wpl[:, 1, :], start=False, stop=False)
                                last = pe.matmul(o, xtl[:, tok], wph[:, 1, :], start=False, stop=True)
                        last.then_inc(v_ready, 1)

                def scores(g, u, k):
                    j, h, heads = UNITS1[k]
                    w = P * (j + 1)
                    bank = S1[k % 3]
                    pe.wait_ge(s1_free, c.next(s1_free))
                    for x in range(heads):
                        pe.matmul(ps[:, bank, x * w:(x + 1) * w], Qb[0:MROW, u, g, h + x, j * P:(j + 1) * P],
                                  Kb[0:MROW, u, g, 0:w], start=(x == 0), stop=False, skip_group_check=True)
                    pe.matmul(ps[:, bank, 0:heads * w].rearrange("p (x w) -> p x w", x=heads)[:, :, w - P:w],
                              identb[:, :], mask[:, 0:heads, :], start=False, stop=True,
                              skip_group_check=True).then_inc(s1_ready, 1)

                def scores_less_max(grp, u, k):
                    pe.wait_ge(p_ready, c.next(p_ready))
                    for h, kb, at, w in UNITS2[k]:
                        last = pe.matmul(ps[:, S2 + k % 2, at:at + w],
                                         Kb[0:MROW + 2, u, grp, kb * P:(kb + 1) * P],
                                         Qb[0:MROW + 2, u, grp, h, kb * P:L], start=True, stop=True)
                    last.then_inc(s2_ready, 1)

                def times_v(grp, u, par, kb):
                    for hh in range(HG):
                        unit, at, w = WHERE[hh, kb]
                        last = pe.matmul(ps[32 * hh:32 * hh + HD + 1, OB, kb * P:L], V[:, u, kb, grp * HG + hh, :],
                                         prob[:, par, unit, at:at + w], start=(kb == 0), stop=(kb == BLK - 1),
                                         skip_group_check=True)
                    return last

                def slots(n, u, turn, prep, proj):
                    for g in range(NG):
                        if g == 0 and turn != "last":
                            pe.wait_ge(k_rows, c.next(k_rows, 3 * 16))
                            pe.wait_ge(q_rows, c.next(q_rows, 12 * 16))
                        if has_probs(turn, g):
                            pe.wait_ge(m_rows[g % 2], c.next(m_rows[g % 2], 32))
                        elif has_values(turn, g):
                            pe.wait_ge(p_ready, c.next(p_ready, 2))
                        for k in range(len(UNITS1)):
                            if turn != "last":
                                scores(g, u, k)
                            if has_probs(turn, g) and k < len(UNITS2):
                                scores_less_max((g + 2) % NG, u if g >= 2 else 1 - u, k)
                            if has_values(turn, g) and k in (3, 5, 7, 9):
                                last = times_v((g + 1) % NG, u if g == 3 else 1 - u, (g + 1) % 2, (k - 3) // 2)
                                if k == 9:
                                    last.then_inc(o_ready, 1)
                            if k == MAXIMA["pe"] and has_maxima(turn, g):
                                pe.wait_ge(nm_ready, c.next(nm_ready))
                                pe.wait_ge(ma_free, c.next(ma_free))
                                pe.transpose(ps[0:HG * BLK, MA, 0:P], nm[:, (g + 1) % 2, :, :].rearrange(
                                    "p h j -> p (h j)"), ident[:, :]).then_inc(mt_ready, 1)
                            if k == OUTPUT["pe"] and has_output(turn):
                                pe.wait_ge(osb_ready, c.next(osb_ready))
                                pe.wait_ge(mb_free, c.next(mb_free))
                                for j in range(BLK):
                                    last = pe.transpose(ps[:, MB, j * P:(j + 1) * P],
                                                        osb[:, j * P:(j + 1) * P], ident[:, :])
                                last.then_inc(ot_ready, 1)
                            if proj and g == 0 and k == NEXT_X["pe"]:
                                transpose_x()
                            if proj and g == 0 and k == LATENTS["pe"]:
                                project(0, 1 - u)
                            if proj and g in (1, 2) and k == KEYS_QUERIES["pe"]:
                                project(g, 1 - u)
                            if proj and g == 2 and k == VALUES["pe"]:
                                project(3, 1 - u)
                            if g == 3 and turn != "first" and k == DENSE["pe"]:
                                pe.wait_ge(mb_free, c.next(mb_free))
                                pe.wait_ge(ma_free, c.next(ma_free))
                                for b in range(BLK):
                                    last = pe.transpose(ps[:, MA, b * P:(b + 1) * P], ctxs[:, 1 - u, b, :],
                                                        ident[:, :])
                                last.then_inc(ct_ready, 1)
                            if g == 3 and turn != "first" and k == DENSE["pe2"]:
                                pe.wait_ge(ctxt_ready, c.next(ctxt_ready))
                                pe.sem_inc(ma_free, 1)
                                for b in range(BLK):
                                    last = pe.matmul(ps[:, MB, b * P:(b + 1) * P], ctxt[:, b * P:(b + 1) * P],
                                                     wo[:, :], start=True, stop=True)
                                last.then_inc(y_ready, 1)
                        if g == 1 and turn != "last":
                            pe.drain().then_inc(kb_used, 1)

                transpose_x()
                for g in range(NG):
                    project(g, 0)
                walk(pe, c, slots)



KIND_SWIGLU, KIND_GELU = range(2)


def experts_stage(nc, io, ps, X, ident, mhalf, kind, xm_d=None, out=None):
    swiglu = kind == KIND_SWIGLU
    with ExitStack() as ctx:
        N = Names(nc, ctx, "glu" if swiglu else "moe")
        EXP = E0 if swiglu else E1
        R = E0 - 1 if swiglu else E1
        FIRST = EXP - R
        HB = 1 if swiglu else H1B
        UNITS = EXP * HB
        WB = 2 if swiglu else HB
        w_raw = N.sb("w_raw", [P, EXP, WB, P])
        wh, wl = N.sb("wh", [P, EXP, WB, P], F32R), N.sb("wl", [P, EXP, WB, P], F32R)
        wd = N.sb("wd", [P, EXP, HB, C])
        wr = N.sb("wr", [P, R])
        wrh, wrl = N.sb("wrh", [P, 8], F32R), N.sb("wrl", [P, 8], F32R)
        rb = N.sb("rb", [P, R])
        desc, euler = N.sb("desc", [P, R]), N.sb("euler", [P, BLK, R])
        xs = N.sb("xs", [P, BLK, C])
        xth, xtl = N.sb("xth", [P, 2, L], F32R), N.sb("xtl", [P, 2, L], F32R)
        hid = N.sb("hid", [P, 2, L])
        wts = N.sb("wts", [P, 2, BLK, R])
        acc = N.sb("acc", [P, 2, BLK, C])
        lg, pr, ex, eq, sel1, sel2 = (N.sb(n, [P, BLK, R]) for n in ("lg", "pr", "ex", "eq", "sel1", "sel2"))
        m1, m2, den = (N.sb(n, [P, BLK]) for n in ("m1", "m2", "den"))
        st, mv = N.sb("st", [P, BLK, 6]), N.sb("mv", [P, BLK, 2])
        var, rstd = N.sb("var", [P, BLK]), N.sb("rstd", [P, BLK])
        if swiglu:
            w2 = N.sb("w2", [P, 1])
            xi = N.sb("xi", [P, 2, BLK, C])
            sg = N.sb("sg", [P, 2, L])
            phalf, ms, rms = (N.sb(n, [P, BLK]) for n in ("phalf", "ms", "rms"))
            st2, mv2 = N.sb("st2", [P, BLK, 6]), N.sb("mv2", [P, BLK, 2])
        else:
            b1 = N.sb("b1", [P, EXP, HB])
            b2 = N.sb("b2", [EXP, C])
            wt = N.sb("wt", [EXP, L])
        consts, done, pdone, weights_ready, router_ready = N.sems("consts done pdone weights_ready router_ready")
        (xi_next, ms_ready, rms_ready, xs_ready, xs_free, t_ready, th_ready, x_ready, l_ready, lg_ready, pr_ready,
         wts_ready, wtt_ready, wt_ready, b_ready, b_free) = N.sems(
            "xi_next ms_ready rms_ready xs_ready xs_free t_ready th_ready x_ready l_ready lg_ready pr_ready "
            "wts_ready wtt_ready wt_ready b_ready b_free")
        f_ready, s_ready, hid_ready, o_ready, o_free, mv_ready, rstd_ready, y_ready, stored = N.sems(
            "f_ready s_ready hid_ready o_ready o_free mv_ready rstd_ready y_ready stored")
        xi_in = N.sems("xi_in0 xi_in1")
        w_in = N.sems("w_in0 w_in1" if swiglu else " ".join(f"w_in{e}" for e in range(E1)))
        TB, FB, OB, LB = 0, 1, 5, 7
        if swiglu:
            TURN, LOGITS, STATS, GATE, SCALE, TURN_WEIGHTS = 1, 2, 3, (5, 6, 7), 7, None
        else:
            TURN, LOGITS, GATE, TURN_WEIGHTS = 2, 3, (4, 5, 6), 7

        def walk(eng, c, tile):
            tile(0, 0, True, 2)
            c.settle()
            with eng.Fori(0, (NB - 4) // 2, 1) as i:
                for v in range(2):
                    tile(i * 2 + (v + 1), (v + 1) % 2, False, 2)
                c.settle()
            for n in range(NB - 3, NB):
                tile(n, n % 2, False, min(2, NB - 1 - n))

        with nc.Block() as block:

            @block.sync
            def _(sp):
                if swiglu:
                    sp.dma_start(w2[:, :], column(io["w_ln2"])).then_inc(consts, 16)
                    sp.dma_start(wr[:, :], io["W_router"]).then_inc(consts, 16)
                    sp.dma_start(rb[:, :], rows(io["routing_bias"])).then_inc(consts, 16)
                    sp.dma_start(w_raw[:, 0, 0, :], io["Wg_s"]).then_inc(w_in[0], 16)
                    sp.dma_start(w_raw[:, 0, 1, :], io["Wu_s"]).then_inc(w_in[0], 16)
                    sp.dma_start(wd[:, 0, 0, :], io["Wd_s"]).then_inc(w_in[0], 16)
                    sp.dma_start(w_raw[:, 1:E0, 0, :], io["Wg_r"].rearrange("e c i -> c e i")).then_inc(w_in[1], 16)
                    sp.dma_start(w_raw[:, 1:E0, 1, :], io["Wu_r"].rearrange("e c i -> c e i")).then_inc(w_in[1], 16)
                    sp.dma_start(wd[:, 1:E0, 0, :], io["Wd_r"].rearrange("e i c -> i e c")).then_inc(w_in[1], 16)
                else:
                    sp.dma_start(wr[:, :], io["Wg"]).then_inc(consts, 16)
                    sp.dma_start(rb[:, :], rows(io["bg"])).then_inc(consts, 16)
                    for e in range(E1):
                        sp.dma_start(w_raw[:, e, :, :].rearrange("c m i -> c (m i)"), io["W1"][e]).then_inc(w_in[e], 16)
                        sp.dma_start(wd[:, e, :, :],
                                     io["W2"][e].rearrange("(m p) c -> p m c", p=P)).then_inc(w_in[e], 16)
                        if e == 0:
                            sp.dma_start(b2[:, :], io["b2"]).then_inc(w_in[0], 16)
                            sp.dma_start(b1[:, :, :], io["b1"].rearrange("e (m p) -> p e m", p=P),
                                         allow_slow_non_contiguous=True).then_inc(w_in[0], 16)
                c = Counts(sp)

                def load(n, u):
                    sp.wait_ge(xi_next, c.next(xi_next))
                    sp.dma_start(xi[:, u, :, :], xm_d[n].rearrange("(k p) c -> p k c", p=P)).then_inc(xi_in[u], 16)

                def store(n):
                    sp.wait_ge(y_ready, c.next(y_ready))
                    sp.dma_start(out[n].rearrange("(k p) c -> p k c", p=P), X[:, n, :, :]).then_inc(stored, 16)

                if swiglu:
                    with sp.Fori(0, NB // 2, 1) as i:
                        for u in range(2):
                            load(i * 2 + u, u)
                        c.settle()
                else:
                    with sp.Fori(0, NB, 1) as i:
                        store(i)
                        c.settle()
                    sp.wait_ge(stored, NB * 16)

            @block.vector
            def _(dve):
                c = Counts(dve)
                link = lambda ins: chain(dve, c, done, ins)
                link(dve.memset(euler[:, :, :], math.e))
                for e in range(R):
                    last = dve.memset(desc[:, e:e + 1], float(R - e))
                link(last)
                if swiglu:
                    link(dve.memset(phalf[:, :], 0.5))
                    link(dve.memset(f32(wrh[:, R:8]), 0.0))
                    link(dve.memset(f32(wrl[:, R:8]), 0.0))
                dve.wait_ge(consts, (3 if swiglu else 2) * 16)
                if swiglu:
                    link(dve.tensor_scalar(wr[:, :], wr[:, :], w2[:, :], None, ALU.mult))
                link(split(dve, c, done, wr[:, :], wrh[:, 0:R], wrl[:, 0:R]))
                dve.sem_inc(router_ready, 1)

                def weights(e):
                    w = w_raw[:, e, :, :]
                    if swiglu:
                        dve.wait_ge(w_in[min(e, 1)], 3 * 16)
                        link(dve.tensor_scalar(w, w, w2[:, :], None, ALU.mult))
                    else:
                        dve.wait_ge(w_in[e], (2 if e else 4) * 16)
                    split(dve, c, done, w, wh[:, e, :, :], wl[:, e, :, :]).then_inc(weights_ready, 1)

                if swiglu:
                    dve.sem_inc(xi_next, 2)
                dve.sem_inc(o_free, 2)
                dve.sem_inc(b_free, 1)
                dve.sem_inc(xs_free, 1)
                c.settle()

                def mean_square(n, u):
                    dve.wait_ge(xi_in[u], c.next(xi_in[u], 16))
                    link(block_stats(dve, c, done, xi[:, u, :, :], st2, mv2))
                    link(dve.tensor_tensor(ms[:, :], mv2[:, :, 0], mv2[:, :, 0], ALU.mult))
                    dve.tensor_tensor(ms[:, :], ms[:, :], mv2[:, :, 1], ALU.add).then_inc(ms_ready, 1)

                def over_rms(n, u):
                    dve.wait_ge(rms_ready, c.next(rms_ready))
                    link(dve.tensor_scalar(ms[:, :], rms[:, :], EPS, None, ALU.add))
                    link(dve.reciprocal(ms[:, :], ms[:, :]))
                    for b in range(BLK):
                        last = dve.tensor_scalar(xs[:, b, :], xi[:, u, b, :], ms[:, b:b + 1], None, ALU.mult)
                    link(last)
                    dve.sem_inc(xs_ready, 1)
                    dve.sem_inc(xi_next, 1)

                def low_x(u):
                    dve.wait_ge(th_ready, c.next(th_ready))
                    link(dve.tensor_tensor(xtl[:, u, :], ps[:, TB, :], f32(xth[:, u, :]), ALU.subtract))
                    dve.sem_inc(x_ready, 1)
                    dve.sem_inc(xs_free, 1)

                def each(ap):
                    return ap.unsqueeze(2).broadcast_to([P, BLK, R])

                def logits():
                    dve.wait_ge(l_ready, c.next(l_ready))
                    l = ps[:, LB, 0:8 * BLK].rearrange("p (b e) -> p b e", b=BLK)[:, :, 0:R]
                    rbb = rb[:, :].unsqueeze(1).broadcast_to([P, BLK, R])
                    if swiglu:
                        link(dve.tensor_tensor(lg[:, :, :], l, rbb, ALU.add))
                        dve.tensor_scalar(lg[:, :, :], lg[:, :, :], -1.0, None, ALU.mult).then_inc(lg_ready, 1)
                    else:
                        link(dve.tensor_tensor(lg[:, :, :], l, rbb, ALU.add))
                        link(dve.tensor_reduce(m1[:, :], lg[:, :, :], axis=AX.X, op=ALU.max))
                        dve.tensor_tensor(lg[:, :, :], lg[:, :, :], each(m1[:, :]),
                                          ALU.subtract).then_inc(lg_ready, 1)

                def gate(u, step):
                    descb = desc[:, :].unsqueeze(1).broadcast_to([P, BLK, R])

                    def best(p, m, sel):
                        link(dve.tensor_reduce(m[:, :], p[:, :, :], axis=AX.X, op=ALU.max))
                        link(dve.tensor_tensor(eq[:, :, :], p[:, :, :], each(m[:, :]), ALU.is_equal))
                        link(dve.tensor_tensor(eq[:, :, :], eq[:, :, :], descb, ALU.mult))
                        link(dve.tensor_reduce(den[:, :], eq[:, :, :], axis=AX.X, op=ALU.max))
                        link(dve.tensor_tensor(sel[:, :, :], descb, each(den[:, :]), ALU.is_equal))

                    if step == 0:
                        dve.wait_ge(pr_ready, c.next(pr_ready))
                        if swiglu:
                            link(dve.tensor_scalar(pr[:, :, :], pr[:, :, :], 1.0, None, ALU.add))
                            link(dve.reciprocal(pr[:, :, :], pr[:, :, :]))
                        best(pr, m1, sel1)
                    if step == 1:
                        link(dve.scalar_tensor_tensor(ex[:, :, :], sel1[:, :, :], -2.0, pr[:, :, :],
                                                      ALU.mult, ALU.add))
                        best(ex, m2, sel2)
                    if step == 2:
                        link(dve.tensor_tensor(m1[:, :], m1[:, :], m2[:, :], ALU.add))
                        if not swiglu:
                            link(dve.tensor_reduce(m2[:, :], pr[:, :, :], axis=AX.X, op=ALU.add))
                            link(dve.scalar_tensor_tensor(m1[:, :], m2[:, :], 1e-8, m1[:, :], ALU.mult, ALU.add))
                        link(dve.reciprocal(m1[:, :], m1[:, :]))
                        link(dve.tensor_tensor(sel1[:, :, :], sel1[:, :, :], sel2[:, :, :], ALU.add))
                        link(dve.tensor_tensor(sel1[:, :, :], sel1[:, :, :], pr[:, :, :], ALU.mult))
                        link(dve.tensor_tensor(wts[:, u, :, :], sel1[:, :, :], each(m1[:, :]), ALU.mult))
                        dve.sem_inc(wts_ready, 1)

                def add_expert(n, u, e):
                    dve.wait_ge(o_ready, c.next(o_ready))
                    o = ps[:, OB + e % 2, :].rearrange("p (b c) -> p b c", b=BLK)
                    if e < FIRST:
                        link(dve.tensor_tensor(acc[:, u, :, :], o, X[:, n, :, :], ALU.add))
                        dve.sem_inc(o_free, 1)
                        return
                    for b in range(BLK):
                        last = dve.scalar_tensor_tensor(acc[:, u, b, :], o[:, b, :],
                                                        wts[:, u, b, e - FIRST:e - FIRST + 1],
                                                        acc[:, u, b, :], ALU.mult, ALU.add)
                    link(last)
                    dve.sem_inc(o_free, 1)

                def begin(n, u):
                    dve.wait_ge(b_ready, c.next(b_ready))
                    link(dve.tensor_tensor(acc[:, u, :, :], ps[:, TB, :].rearrange("p (b c) -> p b c", b=BLK),
                                           X[:, n, :, :], ALU.add))
                    dve.sem_inc(b_free, 1)

                def finish_stats(u):
                    block_stats(dve, c, done, acc[:, u, :, :], st, mv).then_inc(mv_ready, 1)

                def finish(n, u):
                    dve.wait_ge(rstd_ready, c.next(rstd_ready))
                    for b in range(BLK):
                        last = dve.tensor_scalar(X[:, n, b, :], acc[:, u, b, :], mv[:, b, 0:1],
                                                 rstd[:, b:b + 1], ALU.subtract, ALU.mult)
                    link(last)
                    dve.sem_inc(y_ready, 1)

                def tile(n, u, first, more):
                    for e in range(EXP):
                        if swiglu:
                            dve.wait_ge(s_ready, c.next(s_ready))
                            dve.tensor_tensor(hid[:, e % 2, :], sg[:, e % 2, :], ps[:, FB + 2 * (e % 2) + 1, :],
                                              ALU.mult).then_inc(hid_ready, 1)
                        if e > 0:
                            add_expert(n, u, e - 1)
                        elif not first:
                            add_expert(n - 1, 1 - u, EXP - 1)
                        if e == 0 and not swiglu:
                            begin(n, u)
                        if e == 0 and not first:
                            finish_stats(1 - u)
                        if e == 1 and not first:
                            finish(n - 1, 1 - u)
                        if more:
                            if e == TURN:
                                low_x(1 - u)
                            if e == LOGITS:
                                logits()
                            if e in GATE:
                                gate(1 - u, GATE.index(e))
                        if more == 2 and swiglu:
                            if e == STATS:
                                mean_square(n + 2, u)
                            if e == SCALE:
                                over_rms(n + 2, u)

                if swiglu:
                    mean_square(0, 0)
                    over_rms(0, 0)
                low_x(0)
                logits()
                weights(0)
                for step in range(3):
                    gate(0, step)
                for e in range(1, EXP):
                    weights(e)
                if swiglu:
                    mean_square(1, 1)
                    over_rms(1, 1)
                walk(dve, c, tile)
                add_expert(NB - 1, (NB - 1) % 2, EXP - 1)
                finish_stats((NB - 1) % 2)
                finish(NB - 1, (NB - 1) % 2)

            @block.gpsimd
            def _(pool):
                c = Counts(pool)

                def source(n):
                    pool.wait_ge(xs_free, c.next(xs_free))
                    pool.tensor_copy(xs[:, :, :], X[:, n, :, :]).then_inc(xs_ready, 1)

                def root():
                    pool.wait_ge(ms_ready, c.next(ms_ready))
                    pool.tensor_tensor(rms[:, :], ms[:, :], phalf[:, :], ALU.pow).then_inc(rms_ready, 1)

                def power():
                    pool.wait_ge(lg_ready, c.next(lg_ready))
                    pool.tensor_tensor(pr[:, :, :], euler[:, :, :], lg[:, :, :], ALU.pow).then_inc(pr_ready, 1)

                def tile(n, u, first, more):
                    if not first:
                        pool.wait_ge(mv_ready, c.next(mv_ready))
                        pool_rstd(pool, c, pdone, mv, var, mhalf, rstd).then_inc(rstd_ready, 1)
                    if more:
                        if not swiglu:
                            source(n + 1)
                        power()
                    if more == 2 and swiglu:
                        root()

                if swiglu:
                    root()
                else:
                    source(0)
                power()
                if swiglu:
                    root()
                walk(pool, c, tile)
                pool.wait_ge(mv_ready, c.next(mv_ready))
                pool_rstd(pool, c, pdone, mv, var, mhalf, rstd).then_inc(rstd_ready, 1)

            @block.scalar
            def _(act):
                c = Counts(act)
                act.preload_act_table(ACT.Silu if swiglu else ACT.Gelu_apprx_tanh)

                def high_x(u):
                    act.wait_ge(t_ready, c.next(t_ready))
                    act.activation(xth[:, u, :], ps[:, TB, :], ACT.Copy).then_inc(th_ready, 1)

                def turned_weights():
                    act.wait_ge(wtt_ready, c.next(wtt_ready))
                    act.activation(wt[:, :], ps[0:EXP, LB, :], ACT.Copy).then_inc(wt_ready, 1)

                def tile(n, u, first, more):
                    for e in range(EXP):
                        if more and e == TURN:
                            high_x(1 - u)
                        if more and e == TURN_WEIGHTS and not swiglu:
                            turned_weights()
                        for m in range(HB):
                            r = e * HB + m
                            act.wait_ge(f_ready, c.next(f_ready))
                            if swiglu:
                                act.activation(sg[:, r % 2, :], ps[:, FB + 2 * (r % 2), :],
                                               ACT.Silu).then_inc(s_ready, 1)
                            else:
                                act.activation(hid[:, r % 2, :], ps[:, FB + r % 4, :], ACT.Gelu_apprx_tanh,
                                               bias=b1[:, e, m:m + 1]).then_inc(hid_ready, 1)

                high_x(0)
                if not swiglu:
                    turned_weights()
                walk(act, c, tile)

            @block.tensor
            def _(pe):
                c = Counts(pe)
                pe.wait_ge(router_ready, 1)

                def three(o, hi, lo, u):
                    pe.matmul(o, hi, xth[:, u, :], start=True, stop=False)
                    pe.matmul(o, lo, xth[:, u, :], start=False, stop=False)
                    return pe.matmul(o, hi, xtl[:, u, :], start=False, stop=True)

                def transpose_x():
                    pe.wait_ge(xs_ready, c.next(xs_ready))
                    if not swiglu:
                        pe.wait_ge(b_free, c.next(b_free))
                    for b in range(BLK):
                        last = pe.transpose(ps[:, TB, b * P:(b + 1) * P], xs[:, b, :], ident[:, :])
                    last.then_inc(t_ready, 1)

                def logits(u):
                    pe.wait_ge(x_ready, c.next(x_ready))
                    for b in range(BLK):
                        o, tok = ps[:, LB, 8 * b:8 * b + 8], slice(b * P, (b + 1) * P)
                        pe.matmul(o, xth[:, u, tok], wrh[:, :], start=True, stop=False)
                        pe.matmul(o, xth[:, u, tok], wrl[:, :], start=False, stop=False)
                        last = pe.matmul(o, xtl[:, u, tok], wrh[:, :], start=False, stop=True)
                    last.then_inc(l_ready, 1)

                def turn_weights(u):
                    pe.wait_ge(wts_ready, c.next(wts_ready))
                    for b in range(BLK):
                        last = pe.transpose(ps[0:EXP, LB, b * P:(b + 1) * P], wts[:, u, b, :], ident[:, :])
                    last.then_inc(wtt_ready, 1)

                def second_bias():
                    pe.wait_ge(wt_ready, c.next(wt_ready))
                    for b in range(BLK):
                        last = pe.matmul(ps[:, TB, b * P:(b + 1) * P], wt[:, b * P:(b + 1) * P], b2[:, :],
                                         start=True, stop=True)
                    last.then_inc(b_ready, 1)

                def first_products(u, r):
                    e, m = divmod(r, HB)
                    if swiglu:
                        bank = FB + 2 * (r % 2)
                        three(ps[:, bank, :], wh[:, e, 0, :], wl[:, e, 0, :], u)
                        three(ps[:, bank + 1, :], wh[:, e, 1, :], wl[:, e, 1, :], u).then_inc(f_ready, 1)
                    else:
                        three(ps[:, FB + r % 4, :], wh[:, e, m, :], wl[:, e, m, :], u).then_inc(f_ready, 1)

                def second_products(r):
                    e, m = divmod(r, HB)
                    pe.wait_ge(hid_ready, c.next(hid_ready))
                    if m == 0:
                        pe.wait_ge(o_free, c.next(o_free))
                    for b in range(BLK):
                        last = pe.matmul(ps[:, OB + e % 2, b * P:(b + 1) * P], hid[:, r % 2, b * P:(b + 1) * P],
                                         wd[:, e, m, :], start=(m == 0 and b == 0), stop=(m == HB - 1),
                                         skip_group_check=True)
                    if m == HB - 1:
                        last.then_inc(o_ready, 1)

                def tile(n, u, first, more):
                    for r in range(UNITS):
                        e, m = divmod(r, HB)
                        if first and m == 0:
                            pe.wait_ge(weights_ready, e + 1)
                        first_products(u, r)
                        if first and r == 0 and not swiglu:
                            turn_weights(0)
                            second_bias()
                        if r > 0:
                            second_products(r - 1)
                        elif not first:
                            second_products(UNITS - 1)
                        if m == 0 and more:
                            if e == TURN:
                                transpose_x()
                            if e == LOGITS:
                                logits(1 - u)
                            if e == TURN_WEIGHTS and not swiglu:
                                turn_weights(1 - u)
                        if m == HB - 1 and e == TURN_WEIGHTS and more and not swiglu:
                            second_bias()

                transpose_x()
                logits(0)
                walk(pe, c, tile)
                second_products(UNITS - 1)


def constants():
    m = (np.arange(P) < NS).astype(np.float32)
    half = np.stack([m, -m, 1 - m, m * np.float32(math.pi / 2), m - 1], 1)
    hh = HD // 2
    freq = 1.0 / 10000.0 ** (np.arange(0, hh, 2, dtype=np.float32) / hh)
    angle = np.arange(L, dtype=np.float32)[None, :] * freq[:, None].astype(np.float32)
    d = np.arange(P) // NG % HD
    cos = np.where(d[:, None] < hh, 1.0, np.cos(angle)[d % 2])
    sin = np.where(d[:, None] < hh, 0.0, np.sin(angle)[d % 2])
    r = np.arange(P) // LAT
    return {
        "c_t": np.tile(np.arange(L, dtype=np.float32), (P, 1)),
        "c_half": half.astype(np.float32),
        "c_rows": np.stack([-1.0 * (r == 2), -1.0 * (r == 1)], 1).astype(np.float32),
        "c_ident": np.eye(P, dtype=np.float32),
        "c_flip": np.eye(P, dtype=np.float32)[::-1].copy(),
        "c_mask": np.where(np.arange(P)[:, None] >= np.arange(P)[None, :], 0.0, NEG).astype(np.float32),
        "c_cos": cos.astype(np.float32),
        "c_sin": sin.astype(np.float32),
    }


def of_layer(a, name):
    return {k[len(name):]: v for k, v in a.items() if k.startswith(name)} | {
        k: v for k, v in a.items() if k.startswith("c_")}


def program(nc, a, out, upto=4):
    Names.used = set()
    kd = nc.dram_tensor("conv_kernel", (NC, KROW), F32, kind="Internal").ap()
    yd = nc.dram_tensor("conv_out", (NC, NB, L), F32, kind="Internal").ap()
    xm_d = nc.dram_tensor("mid_sum", (NB, L, C), F32, kind="Internal").ap()
    with ExitStack() as ctx:
        ps = ctx.enter_context(nc.psum_tensor("banks", [P, 8, 512], F32))
        X = ctx.enter_context(nc.sbuf_tensor("X", [P, NB, BLK, C], F32))
        ident = ctx.enter_context(nc.sbuf_tensor("ident", [P, P], F32))
        mhalf = ctx.enter_context(nc.sbuf_tensor("mhalf", [P, BLK], F32))
        attn = ctx.enter_context(ExitStack())
        Qb = attn.enter_context(nc.sbuf_tensor("Qb", [P, 2, NG, HG, L], F32R))
        Kb = attn.enter_context(nc.sbuf_tensor("Kb", [P, 2, NG, L], F32R))
        io = of_layer(a, "L0_attn_")
        kernel_stage(nc, io, ps, kd, Qb, Kb)
        with ExitStack() as first:
            stats = first.enter_context(nc.sbuf_tensor("stats", [P, NB, BLK, 2], F32))
            with ExitStack() as conv:
                flip = conv.enter_context(nc.sbuf_tensor("flip", [P, P], F32))
                U = conv.enter_context(nc.sbuf_tensor("U", [P, NC, BLK, NB], F32))
                input_stage(nc, io, ps, X, stats, ident, flip, mhalf, U)
                convolution_stage(nc, io, ps, U, kd, yd)
            gate_stage(nc, io, ps, X, stats, ident, mhalf, yd)
        with attn:
            if upto >= 1:
                attention_stage(nc, of_layer(a, "L0_ffn_"), ps, X, ident, mhalf, Qb, Kb, KIND_LATENT, xm_d)
            if upto >= 2:
                experts_stage(nc, of_layer(a, "L0_ffn_"), ps, X, ident, mhalf, KIND_SWIGLU, xm_d)
                clear(nc)
            if upto >= 3:
                attention_stage(nc, of_layer(a, "L1_attn_"), ps, X, ident, mhalf, Qb, Kb, KIND_DIRECT)
        if upto >= 4:
            experts_stage(nc, of_layer(a, "L1_ffn_"), ps, X, ident, mhalf, KIND_GELU, out=out)
        else:
            store_stage(nc, X, out)


def store_stage(nc, X, out):
    with nc.semaphore("stored") as stored, nc.Block() as block:

        @block.sync
        def _(sp):
            for n in range(NB):
                sp.dma_start(out[n].rearrange("(k p) c -> p k c", p=P), X[:, n, :, :]).then_inc(stored, 16)
            sp.wait_ge(stored, NB * 16)


def kernel(**arrays):
    from concourse import bacc
    from concourse.bass_utils import run_bass_kernel_spmd

    arrays = {k: np.ascontiguousarray(v) for k, v in (arrays | constants()).items()}
    nc = bacc.Bacc("TRN2", target_bir_lowering=False, num_devices=1)
    a = {k: nc.dram_tensor(k, v.shape, mybir.dt.from_np(v.dtype), kind="ExternalInput").ap() for k, v in arrays.items()}
    out = nc.dram_tensor("out", (NB, L, C), F32, kind="ExternalOutput").ap()
    program(nc, a, out)
    nc.finalize()
    return run_bass_kernel_spmd(nc, [arrays], core_ids=[0]).results[0]["out"]
```
